# Optimizing a Trainium2 kernel written in Bass

```python
import numpy as np
import jax
import jax.numpy as jnp

def _softmax(x, axis=-1):
    return jax.nn.softmax(x, axis=axis)

def _gelu(x):
    return jax.nn.gelu(x, approximate=True)

def _silu(x):
    return jax.nn.silu(x)

def _sigmoid(x):
    return jax.nn.sigmoid(x)

def _layernorm(x, axis=-1, eps=1e-05):
    m = jnp.mean(x, axis=axis, keepdims=True)
    v = jnp.var(x, axis=axis, keepdims=True)
    return (x - m) / jnp.sqrt(v + eps)

def _scatter_add(tgt, idx, src, axis=0):
    return tgt.at[idx].add(src)

def _segment_sum(src, seg, n):
    return jax.ops.segment_sum(src, seg, n)
kernel_name = 'mk_macaron_d2_jaxref_r8_84f7f8'

def setup_inputs(seed: int=0):
    np.random.seed(seed)
    _w = jnp.asarray

    def _L0_attn_setup():
        import jax, jax.numpy as jnp
        import numpy as np
        D_MODEL = 128
        N_HEADS = 16
        D_HEAD = D_MODEL // N_HEADS
        SCALE = 1.0 / np.sqrt(D_HEAD).astype(np.float32)

        def _feature_map(x):
            return jax.nn.elu(x) + 1.0
        key = jax.random.key(seed)
        ks = jax.random.split(key, 7)
        b, s = (4, 256)
        w = 1.0 / np.sqrt(D_MODEL).astype(np.float32)
        return {'x': jax.random.normal(ks[0], (b, s, D_MODEL), dtype=jnp.float32), 'Wq': jax.random.normal(ks[1], (D_MODEL, D_MODEL), dtype=jnp.float32) * w, 'Wk': jax.random.normal(ks[2], (D_MODEL, D_MODEL), dtype=jnp.float32) * w, 'Wv': jax.random.normal(ks[3], (D_MODEL, D_MODEL), dtype=jnp.float32) * w, 'Wo': jax.random.normal(ks[4], (D_MODEL, D_MODEL), dtype=jnp.float32) * w, 'Wg': jax.random.normal(ks[5], (N_HEADS, D_MODEL), dtype=jnp.float32) * w, 'bg': jax.random.normal(ks[6], (N_HEADS,), dtype=jnp.float32) * 0.02}
    _L0_attn_in = _L0_attn_setup()

    def _L0_ffn_setup():
        import jax, jax.numpy as jnp
        import numpy as np
        key = jax.random.key(seed)
        ks = jax.random.split(key, 5)
        B, T, D, E = (4, 256, 128, 8)
        inputs = jax.random.normal(ks[0], (B, T, D), dtype=jnp.float32)
        Wr = jax.random.normal(ks[1], (D, E), dtype=jnp.float32) * 0.02
        br = jnp.zeros((E,), dtype=jnp.float32)
        W1 = jax.random.normal(ks[2], (E, D, D), dtype=jnp.float32) * 0.02
        b1 = jnp.zeros((E, D), dtype=jnp.float32)
        W2 = jax.random.normal(ks[3], (E, D, D), dtype=jnp.float32) * 0.02
        b2 = jnp.zeros((E, D), dtype=jnp.float32)
        return {'inputs': inputs, 'Wr': Wr, 'br': br, 'W1': W1, 'b1': b1, 'W2': W2, 'b2': b2}
    _L0_ffn_in = _L0_ffn_setup()

    def _L1_attn_setup():
        import jax, jax.numpy as jnp
        import numpy as np
        B, S, D, H = (2, 256, 128, 16)
        HD = D // H
        LN_EPS = 1e-05
        key = jax.random.key(seed)
        ks = jax.random.split(key, 8)
        inv = 1.0 / np.sqrt(D)
        return {'embedded': jax.random.normal(ks[0], (B, S, D), dtype=jnp.float32), 'Wq': jax.random.normal(ks[1], (D, D), dtype=jnp.float32) * inv, 'bq': jax.random.normal(ks[2], (D,), dtype=jnp.float32) * 0.01, 'Wk': jax.random.normal(ks[3], (D, D), dtype=jnp.float32) * inv, 'bk': jax.random.normal(ks[4], (D,), dtype=jnp.float32) * 0.01, 'Wv': jax.random.normal(ks[5], (D, D), dtype=jnp.float32) * inv, 'bv': jax.random.normal(ks[6], (D,), dtype=jnp.float32) * 0.01, 'gamma': jnp.ones((D,), dtype=jnp.float32), 'beta': jnp.zeros((D,), dtype=jnp.float32)}
    _L1_attn_in = _L1_attn_setup()

    def _L1_ffn_setup():
        import jax, jax.numpy as jnp
        import numpy as np
        B, S, D, E, F = (2, 256, 128, 8, 512)
        key = jax.random.key(seed)
        ks = jax.random.split(key, 4)
        return {'hidden_states': jax.random.normal(ks[0], (B, S, D), dtype=jnp.float32), 'Wr': jax.random.normal(ks[1], (D, E), dtype=jnp.float32) * (1.0 / np.sqrt(D)), 'W1': jax.random.normal(ks[2], (E, D, F), dtype=jnp.float32) * (1.0 / np.sqrt(D)), 'b1': jnp.zeros((E, F), dtype=jnp.float32), 'W2': jax.random.normal(ks[3], (E, F, D), dtype=jnp.float32) * (1.0 / np.sqrt(F)), 'b2': jnp.zeros((E, D), dtype=jnp.float32)}
    _L1_ffn_in = _L1_ffn_setup()
    _d = {'L0_attn_x': _L0_attn_in['x'], 'L0_attn_Wq': _L0_attn_in['Wq'], 'L0_attn_Wk': _L0_attn_in['Wk'], 'L0_attn_Wv': _L0_attn_in['Wv'], 'L0_attn_Wo': _L0_attn_in['Wo'], 'L0_attn_Wg': _L0_attn_in['Wg'], 'L0_attn_bg': _L0_attn_in['bg'], 'L0_ffn_Wr': _L0_ffn_in['Wr'], 'L0_ffn_br': _L0_ffn_in['br'], 'L0_ffn_W1': _L0_ffn_in['W1'], 'L0_ffn_b1': _L0_ffn_in['b1'], 'L0_ffn_W2': _L0_ffn_in['W2'], 'L0_ffn_b2': _L0_ffn_in['b2'], 'L1_attn_Wq': _L1_attn_in['Wq'], 'L1_attn_bq': _L1_attn_in['bq'], 'L1_attn_Wk': _L1_attn_in['Wk'], 'L1_attn_bk': _L1_attn_in['bk'], 'L1_attn_Wv': _L1_attn_in['Wv'], 'L1_attn_bv': _L1_attn_in['bv'], 'L1_attn_gamma': _L1_attn_in['gamma'], 'L1_attn_beta': _L1_attn_in['beta'], 'L1_ffn_Wr': _L1_ffn_in['Wr'], 'L1_ffn_W1': _L1_ffn_in['W1'], 'L1_ffn_b1': _L1_ffn_in['b1'], 'L1_ffn_W2': _L1_ffn_in['W2'], 'L1_ffn_b2': _L1_ffn_in['b2']}
    _x0 = _d['L0_attn_x']
    _d['L0_attn_x'] = jax.random.normal(jax.random.fold_in(jax.random.key(seed), 1), (2, 1024, 128), dtype=_x0.dtype)
    del _x0
    return _d

def reference(L0_attn_x, L0_attn_Wq, L0_attn_Wk, L0_attn_Wv, L0_attn_Wo, L0_attn_Wg, L0_attn_bg, L0_ffn_Wr, L0_ffn_br, L0_ffn_W1, L0_ffn_b1, L0_ffn_W2, L0_ffn_b2, L1_attn_Wq, L1_attn_bq, L1_attn_Wk, L1_attn_bk, L1_attn_Wv, L1_attn_bv, L1_attn_gamma, L1_attn_beta, L1_ffn_Wr, L1_ffn_W1, L1_ffn_b1, L1_ffn_W2, L1_ffn_b2):

    def _L0_attn_ref(x, Wq, Wk, Wv, Wo, Wg, bg):
        import jax, jax.numpy as jnp
        import numpy as np
        D_MODEL = 128
        N_HEADS = 16
        D_HEAD = D_MODEL // N_HEADS
        SCALE = 1.0 / np.sqrt(D_HEAD).astype(np.float32)

        def _feature_map(x):
            return jax.nn.elu(x) + 1.0
        b, s, _ = x.shape
        q = (x @ Wq.T).reshape(b, s, N_HEADS, D_HEAD)
        k = (x @ Wk.T).reshape(b, s, N_HEADS, D_HEAD)
        v = (x @ Wv.T).reshape(b, s, N_HEADS, D_HEAD)
        q = _feature_map(q * SCALE)
        k = _feature_map(k)
        gate = jax.nn.sigmoid(x @ Wg.T + bg)
        qt = jnp.moveaxis(q, 1, 0)
        kt = jnp.moveaxis(k, 1, 0)
        vt = jnp.moveaxis(v, 1, 0)
        gt = jnp.moveaxis(gate, 1, 0)
        S0 = jnp.zeros((b, N_HEADS, D_HEAD, D_HEAD), dtype=x.dtype)

        def step(S, inp):
            q_t, k_t, v_t, g_t = inp
            S = g_t[:, :, None, None] * S + k_t[..., :, None] * v_t[..., None, :]
            y_t = jnp.einsum('bhi,bhij->bhj', q_t, S)
            return (S, y_t)
        _, ys = jax.lax.scan(step, S0, (qt, kt, vt, gt))
        y = jnp.moveaxis(ys, 0, 1).reshape(b, s, D_MODEL)
        return y @ Wo.T

    def _L0_ffn_ref(inputs, Wr, br, W1, b1, W2, b2):
        import jax, jax.numpy as jnp
        import numpy as np
        B, T, D = inputs.shape
        E = Wr.shape[1]
        x = inputs.reshape(B * T, D)
        N = x.shape[0]
        C = N // E
        logits = x @ Wr + br
        probs = jax.nn.softmax(logits, axis=-1)
        gate = jnp.max(probs, axis=-1, keepdims=True)
        idx = jnp.argmax(probs, axis=-1)
        mask = jax.nn.one_hot(idx, E, dtype=jnp.float32)
        pos = (jnp.cumsum(mask, axis=0) * mask).astype(jnp.int32)
        mask = mask * (pos < C).astype(jnp.float32)
        mask_flat = jnp.sum(mask, axis=-1, keepdims=True)
        gate = gate * mask_flat
        combine = (gate * mask_flat * jax.nn.one_hot(idx, E, dtype=jnp.float32))[..., None] * jax.nn.one_hot(pos, C, dtype=jnp.float32)
        dispatch = combine
        expert_in = jnp.einsum('nd,nec->ecd', x, dispatch)
        h = jax.nn.relu(jnp.einsum('ecd,edf->ecf', expert_in, W1) + b1[:, None, :])
        eo = jnp.einsum('ecf,efd->ecd', h, W2) + b2[:, None, :]
        out = jnp.einsum('ecd,nec->nd', eo, combine)
        return out.reshape(B, T, D)

    def _L1_attn_ref(embedded, Wq, bq, Wk, bk, Wv, bv, gamma, beta):
        import jax, jax.numpy as jnp
        import numpy as np
        B, S, D, H = (2, 256, 128, 16)
        HD = D // H
        LN_EPS = 1e-05
        b, s, d = embedded.shape
        q = embedded @ Wq.T + bq
        k = embedded @ Wk.T + bk
        v = embedded @ Wv.T + bv
        q = q.reshape(b, s, H, HD).transpose(0, 2, 1, 3)
        k = k.reshape(b, s, H, HD).transpose(0, 2, 1, 3)
        v = v.reshape(b, s, H, HD).transpose(0, 2, 1, 3)
        qk = jnp.einsum('bhqd,bhkd->bhqk', q, k)
        qk = jnp.where(jnp.isnan(qk), -jnp.inf, qk)
        qk = qk / jnp.float32(np.sqrt(s))
        p = jax.nn.softmax(qk, axis=-1)
        p = jnp.where(jnp.isnan(p), 0.0, p)
        v = jnp.where(jnp.isnan(v), 0.0, v)
        mask = jnp.triu(jnp.ones((s, s), dtype=p.dtype), k=0)
        p = p * mask
        z = jnp.einsum('bhqk,bhkd->bhqd', p, v)
        z = z.reshape(b, s, d)
        x = embedded + z
        mu = jnp.mean(x, axis=-1, keepdims=True)
        var = jnp.mean(jnp.square(x - mu), axis=-1, keepdims=True)
        out = (x - mu) * jax.lax.rsqrt(var + LN_EPS) * gamma + beta
        return out

    def _L1_ffn_ref(hidden_states, Wr, W1, b1, W2, b2):
        import jax, jax.numpy as jnp
        import numpy as np
        B, S, D, E, F = (2, 256, 128, 8, 512)
        b, s, d = hidden_states.shape
        e = Wr.shape[1]
        x = hidden_states.reshape(b * s, d)
        router_logits = x @ Wr
        router_probs = jax.nn.softmax(router_logits, axis=-1)
        expert_idx = jnp.argmax(router_probs, axis=-1)
        p_max = jnp.max(router_probs, axis=-1, keepdims=True)

        def expert_mlp(w1, bb1, w2, bb2):
            h = jax.nn.gelu(x @ w1 + bb1, approximate=False)
            return h @ w2 + bb2
        outs = jax.vmap(expert_mlp)(W1, b1, W2, b2)
        onehot = jax.nn.one_hot(expert_idx, e, dtype=x.dtype)
        next_states = jnp.einsum('te,etd->td', onehot, outs)
        out = p_max * next_states
        return out.reshape(b, s, d)
    x = L0_attn_x
    x = x + 0.5 * _L0_ffn_ref(_layernorm(x, axis=-1), L0_ffn_Wr, L0_ffn_br, L0_ffn_W1, L0_ffn_b1, L0_ffn_W2, L0_ffn_b2)
    x = x + _L0_attn_ref(_layernorm(x, axis=-1), L0_attn_Wq, L0_attn_Wk, L0_attn_Wv, L0_attn_Wo, L0_attn_Wg, L0_attn_bg)
    x = x + 0.5 * _L0_ffn_ref(_layernorm(x, axis=-1), L0_ffn_Wr, L0_ffn_br, L0_ffn_W1, L0_ffn_b1, L0_ffn_W2, L0_ffn_b2)
    x = x + 0.5 * _L1_ffn_ref(_layernorm(x, axis=-1), L1_ffn_Wr, L1_ffn_W1, L1_ffn_b1, L1_ffn_W2, L1_ffn_b2)
    x = x + _L1_attn_ref(_layernorm(x, axis=-1), L1_attn_Wq, L1_attn_bq, L1_attn_Wk, L1_attn_bk, L1_attn_Wv, L1_attn_bv, L1_attn_gamma, L1_attn_beta)
    x = x + 0.5 * _L1_ffn_ref(_layernorm(x, axis=-1), L1_ffn_Wr, L1_ffn_W1, L1_ffn_b1, L1_ffn_W2, L1_ffn_b2)
    return x

_drawn_inputs = setup_inputs


def setup_inputs(seed=0):
    import zlib

    import numpy as np

    out = dict(_drawn_inputs(seed))
    spreads = {'L0_ffn_br': (0.0, 0.8),
     'L0_ffn_b1': (0.0, 0.8),
     'L0_ffn_b2': (0.0, 0.8),
     'L1_attn_gamma': (1.0, 0.6),
     'L1_attn_beta': (0.0, 0.8),
     'L1_ffn_b1': (0.0, 0.8),
     'L1_ffn_b2': (0.0, 0.8)}
    factors = {'L0_attn_bg': 8.0,
     'L0_ffn_Wr': 8.0,
     'L0_ffn_W1': 8.0,
     'L0_ffn_W2': 8.0,
     'L1_attn_Wq': 8.0,
     'L1_attn_bq': 64.0,
     'L1_attn_Wk': 8.0,
     'L1_attn_bk': 64.0,
     'L1_attn_Wv': 8.0,
     'L1_attn_bv': 64.0,
     'L1_ffn_Wr': 2.836,
     'L1_ffn_W1': 3.111,
     'L1_ffn_W2': 2.793}
    for name, (base, spread) in spreads.items():
        noise = np.random.default_rng([zlib.crc32(name.encode()), seed]).standard_normal(out[name].shape)
        drawn = base * np.exp(spread * noise) if base else spread * noise
        out[name] = jnp.asarray(drawn.astype(out[name].dtype))
    for name, factor in factors.items():
        out[name] = (out[name] * factor).astype(out[name].dtype)
    return out
```

```python
from contextlib import ExitStack

import concourse.bass as bass
from concourse import mybir

ALU = mybir.AluOpType
ACT = mybir.ActivationFunctionType
AX = mybir.AxisListType
F32 = mybir.dt.float32
BF16 = mybir.dt.bfloat16
U32 = mybir.dt.uint32
I32 = mybir.dt.int32

P = 128
B, S = 2, 1024
N = B * S
T = N // P
TB = S // P
E = 8
CAP = N // E
F1 = 512
FB = F1 // P
NT = T + E - 1
H, DH = 16, 8
EPS = 1e-5
QSCALE = DH ** -0.5
BIG = 65536.0
WB = F1 + FB * P + FB

NG = H // 4
GR = B * NG
PAIRS = 9
KQ = PAIRS * DH
MR = 96
Q3R = 3
DR = 12
NPT = 8

COLS = {}


def _columns():
    at = 0
    for name, width in (
        ("ident", P), ("tri", P), ("r8", P), ("r16", P), ("e256", P), ("jt", P), ("ti", NT * E),
        ("f0_wr", E), ("f0_br", E), ("f0_b1", E), ("f1_wr", E), ("a0_bg", 1), ("a1_bq", 1), ("a1_bk", 1),
        ("f0_w1", E * P), ("f0_w2", E * P), ("f0_b2", E * P),
        ("a0_wq", P), ("a0_wk", P), ("a0_wg", P), ("a0_wv", DH * P), ("a0_wo", DH * P),
        ("a1_wq", P), ("a1_wk", P), ("a1_wv", P), ("a1_bv", P), ("a1_gamma", P), ("a1_beta", P),
    ):
        COLS[name] = (at, width)
        at += width
    return at


NCOL = _columns()
EARLY = COLS["f0_w1"][0]
FFN0 = COLS["a0_wq"][0]


def head_of(group, g):
    u, ab = (group % NG) // 2, group % 2
    return 8 * u + 2 * g + ab


def attention_turns():
    turns = []
    for hh in range(4 * GR):
        for i in range(TB):
            turns.append(("A", hh, i))
            if i == 2 and hh >= 1:
                turns.append(("M", hh - 1, 0))
    turns.append(("M", 4 * GR - 1, 0))
    return turns


def attention_plan():
    turns = attention_turns()
    plan, at = [], 0
    ahead = turns.index(("M", 3, 0)) + 1
    rest = len(turns) - ahead
    while at < ahead:
        plan.append(turns[at])
        at += 1
    steps = GR * TB
    for m in range(steps):
        G, j = divmod(m, TB)
        for g in range(4):
            want = ahead + -(-rest * (4 * m + g + 1) // (4 * (steps - TB)))
            while at < min(want, len(turns)):
                plan.append(turns[at])
                at += 1
            if j == 0 and g == 0:
                while at <= turns.index(("M", 4 * G + 3, 0)):
                    plan.append(turns[at])
                    at += 1
            plan.append(("B", m, g))
        if m >= 1:
            plan.append(("V", m - 1, 0))
            if m % (2 * TB) == 0:
                plan += [("T", m // (2 * TB) - 1, 0), ("T", m // (2 * TB) - 1, 1)]
    plan.append(("V", steps - 1, 0))
    plan += [("T", GR // 2 - 1, 0), ("T", GR // 2 - 1, 1)]
    return plan


def macaron_kernel(nc, x_in, params, f1_pack, f1_b2, out):
    with ExitStack() as ctx:
        def sb(name, shape, dt=F32):
            return ctx.enter_context(nc.sbuf_tensor(name, shape, dt))

        def sem(name):
            return ctx.enter_context(nc.semaphore(name))

        X = sb("X", [P, T, P])
        XN = sb("XN", [P, T, P])
        XNT = sb("XNT", [P, N])
        C = sb("C", [P, NCOL])
        TRI = sb("TRI", [P, P], BF16)
        ONES = sb("ONES", [P, P], BF16)
        ONE1 = sb("ONE1", [1, P])
        IDB = sb("IDB", [P, P], BF16)
        STATS = sb("STATS", [P, T, 6])
        MV = sb("MV", [P, T, 2])
        RSTD = sb("RSTD", [P, T])
        ZERO = sb("ZERO", [P, P])
        LG = sb("LG", [P, T, E])
        LMAX = sb("LMAX", [P, T])
        EX = sb("EX", [P, T, E])
        SUM = sb("SUM", [P, T])
        GATE = sb("GATE", [P, T])
        HIT = sb("HIT", [P, T * E])
        NTH = sb("NTH", [P, T * E])
        MASK = sb("MASK", [P, E, T])
        MASKB = sb("MASKB", [P, E * T], BF16)
        INCL = sb("INCL", [P, E * T])
        POS = sb("POS", [P, E * T])
        PRD = sb("PRD", [P, E, T])
        SLOT = sb("SLOT", [P, T])
        PLACE = sb("PLACE", [P, T])
        KEPT = sb("KEPT", [P, T])
        SCAT = sb("SCAT", [P, T])
        GATH = sb("GATH", [P, T])
        EFF = sb("EFF", [P, T])
        CMP = sb("CMP", [P, E, T])
        TILES = sb("TILES", [P, E])
        ENDS = sb("ENDS", [P, E])
        BASE = sb("BASE", [P, E])
        CMP2 = sb("CMP2", [P, NT, E])
        OWNER = sb("OWNER", [P, NT])
        OWNERI = sb("OWNERI", [P, NT], I32)
        SCATI = sb("SCATI", [P, T], U32)
        GATHI = sb("GATHI", [P, T], U32)

        ARENA = sb("ARENA", [P, 32768])

        class Carve:
            def __init__(self):
                self.at = 0

            def __call__(self, *shape):
                size = 1
                for s in shape:
                    size *= s
                a = ARENA[:, self.at:self.at + size]
                self.at += size
                assert self.at <= 32768
                return a

            def bf(self, size):
                a = ARENA[:, self.at:self.at + size // 2].bitcast(BF16)
                self.at += size // 2
                assert self.at <= 32768
                return a

        m = Carve()
        XG = m(T * P).rearrange("p (t d) -> p t d", t=T)
        YG = m(T * P).rearrange("p (t d) -> p t d", t=T)
        XS = m(NT * P).rearrange("p (t d) -> p t d", t=NT)
        XST = m(NT * P)
        EO = m(NT * P).rearrange("p (t d) -> p t d", t=NT)
        HB = m(2 * F1).rearrange("p (r f) -> p r f", r=2)
        HG = m(2 * F1).rearrange("p (r f) -> p r f", r=2)
        WR = 3
        WT = m(WR * WB).rearrange("p (r w) -> p r w", r=WR)
        B2R = m(WR * P).rearrange("p (r w) -> p r w", r=WR)

        m = Carve()
        KT = m(N)
        QT = m(N)
        GT = m(N)
        RL = m(2 * 512).rearrange("p (r n) -> p r n", r=2)
        MN = m(2 * 512).rearrange("p (r n) -> p r n", r=2)
        EXQ = m(2 * 512).rearrange("p (r n) -> p r n", r=2)
        KV = m(2 * S).rearrange("p (r n) -> p r n", r=2)
        ST = m(2 * S).rearrange("p (r n) -> p r n", r=2)
        QS = m(2 * S).rearrange("p (r n) -> p r n", r=2)

        m = Carve()
        Q3 = m.bf(Q3R * 4 * S).rearrange("p (r g n) -> p r g n", r=Q3R, g=4)
        K3 = m.bf(Q3R * 4 * S).rearrange("p (r g n) -> p r g n", r=Q3R, g=4)
        PT = m(NPT * S).rearrange("p (r n) -> p r n", r=NPT)
        V9 = m(T * H * 9).rearrange("p (t h j) -> p t h j", t=T, h=H)
        ZT = m(2 * S).rearrange("p (r n) -> p r n", r=2)
        D32 = m(DR * TB * 32).rearrange("p (h i c) -> p h i c", h=DR, i=TB)
        NM = m(4 * TB).rearrange("p (r i) -> p r i", r=4)
        NMR = m(4 * TB).rearrange("p (r i) -> p r i", r=4)
        M3 = m.bf(4 * 3 * TB).rearrange("p (r c) -> p r c", r=4)
        MT = m.bf(4 * P).rearrange("p (r c) -> p r c", r=4)
        RD = m(32).rearrange("p (c g) -> p c g", g=4)
        free = m.at
        m.at = free
        assert m.at <= 32768, m.at
        Z = YGZ = XG_Z = None
        PS0 = 2 * (Q3R * 4 * S // 2)
        sp0 = ARENA[:, PS0:PS0 + NPT * S]
        QF = sp0[:, 0:N]
        RF = sp0[:, N:2 * N]
        PART = sp0[:, 2 * N:2 * N + 3 * N // 2].bitcast(BF16).rearrange("p (a n) -> p a n", a=3)
        Z = XNT[:, :].rearrange("p (t d) -> p t d", t=T)

        PS = ctx.enter_context(nc.psum_tensor("PS", [P, 8, 512], F32))

        sx = nc.dram_tensor("slots_x", [NT * P, P], F32, kind="Internal").ap()
        sy = nc.dram_tensor("slots_y", [NT * P, P], F32, kind="Internal").ap()
        qd = nc.dram_tensor("q_parts", [3, P, N], BF16, kind="Internal").ap()
        kd = nc.dram_tensor("k_parts", [3, P, N], BF16, kind="Internal").ap()

        def col(name, k=None, n=None):
            at, width = COLS[name]
            if k is None:
                return C[:, at:at + width]
            return C[:, at + k:at + k + n]

        x_loaded = sem("x_loaded")
        early_loaded = sem("early_loaded")
        ffn0_loaded = sem("ffn0_loaded")
        rest_loaded = sem("rest_loaded")
        consts_made = sem("consts_made")
        one_made = sem("one_made")
        zero_made = sem("zero_made")
        zeroed = sem("zeroed")
        dve_step = sem("dve_step")
        pool_step = sem("pool_step")
        act_step = sem("act_step")
        var_ready = sem("var_ready")
        std_ready = sem("std_ready")
        xn_ready = sem("xn_ready")
        xt_turned = sem("xt_turned")
        xt_copied = sem("xt_copied")
        logits_done = sem("logits_done")
        lg_ready = sem("lg_ready")
        ex_ready = sem("ex_ready")
        mask_ready = sem("mask_ready")
        counts_done = sem("counts_done")
        index_ready = sem("index_ready")
        owner_ready = sem("owner_ready")
        xg_ready = sem("xg_ready")
        scattered = sem("scattered")
        xs_loaded = [sem(f"xs_loaded{k}") for k in range(6)]
        xs_turned = sem("xs_turned")
        xs_copied = sem("xs_copied")
        hid_done = sem("hid_done")
        hid_biased = sem("hid_biased")
        hid_active = sem("hid_active")
        eo_done = sem("eo_done")
        eo_copied = sem("eo_copied")
        eo_stored = sem("eo_stored")
        w_loaded = [sem(f"w_loaded{k}") for k in range(3)]
        gathered = [sem(f"gathered{k}") for k in range(T)]
        x_updated = sem("x_updated")
        g_done = sem("g_done")
        g_ready = sem("g_ready")
        qk_done = sem("qk_done")
        relu_done = sem("relu_done")
        min_done = sem("min_done")
        exq_done = sem("exq_done")
        qk_ready = sem("qk_ready")
        v_done = sem("v_done")
        kv_done = sem("kv_done")
        state_done = sem("state_done")
        qs_done = sem("qs_done")
        lin_used = sem("lin_used")
        lin_done = sem("lin_done")
        proj_done = sem("proj_done")
        qf_done = sem("qf_done")
        rest1_done = sem("rest1_done")
        part1_done = sem("part1_done")
        parts_done = sem("parts_done")
        parts_stored = sem("parts_stored")
        vproj_done = sem("vproj_done")
        v9_ones = sem("v9_ones")
        v9_ready = sem("v9_ready")
        ring_zeroed = sem("ring_zeroed")
        ring_loaded = [sem(f"ring_loaded{k}") for k in range(Q3R)]
        a_scores = sem("a_scores")
        a_max = sem("a_max")
        a_exp = sem("a_exp")
        m_split = sem("m_split")
        m_turned = sem("m_turned")
        m_copied = sem("m_copied")
        m_rows = [sem(f"m_rows{k}") for k in range(4)]
        b_scores = sem("b_scores")
        b_exp = sem("b_exp")
        b_masked = sem("b_masked")
        pv_done = sem("pv_done")
        z_copied = sem("z_copied")
        z_turned = sem("z_turned")
        z_scaled = sem("z_scaled")
        out_stored = sem("out_stored")

        x_rows = x_in.rearrange("(t p) d -> p t d", p=P)
        out_rows = out.rearrange("(t p) d -> p t d", p=P)
        sx_rows = sx.rearrange("(t p) d -> p t d", p=P)
        sy_rows = sy.rearrange("(t p) d -> p t d", p=P)

        STAGES = (("ffn0", 0, 0), ("lin", 1, None), ("ffn0", 2, 1), ("ffn1", 3, 2), ("soft", 4, None), ("ffn1", 5, 3))

        def tiles_of(kind):
            return T if kind == "ffn0" else NT

        def chunks_of(kind):
            n = tiles_of(kind)
            return [(a, min(a + 4, n)) for a in range(0, n, 4)]

        def before(k, per0, per1):
            return min(k, 2) * per0 + max(k - 2, 0) * per1

        plan = attention_plan()
        turns = [x for x in plan if x[0] in "AMT"]
        turn_number = {x: n for n, x in enumerate(turns)}

        def chunk_list(j):
            w = P * (j + 1)
            return [(0, min(w, 512))] + ([(512, w)] if w > 512 else [])

        chunk_number = {}
        n = 0
        for x in plan:
            if x[0] == "B":
                G, j = divmod(x[1], TB)
                for k in range(len(chunk_list(j))):
                    chunk_number[(x[1], x[2], k)] = n
                    n += 1

        def last_chunk(mm, g):
            return chunk_number[(mm, g, len(chunk_list(mm % TB)) - 1)]

        def head_number(hh):
            G, g = divmod(hh, 4)
            return G // NG, head_of(G, g)

        block = ctx.enter_context(nc.Block())

        @block.sync
        def _(sp):
            for a in range(0, T, 4):
                sp.dma_start(X[:, a:a + 4, :], x_rows[:, a:a + 4, :]).then_inc(x_loaded, 16)
            sp.dma_start(C[:, 0:EARLY], params[:, 0:EARLY]).then_inc(early_loaded, 16)
            sp.dma_start(C[:, EARLY:FFN0], params[:, EARLY:FFN0]).then_inc(ffn0_loaded, 16)
            sp.dma_start(C[:, FFN0:NCOL], params[:, FFN0:NCOL]).then_inc(rest_loaded, 16)
            sp.wait_ge(zero_made, 1)
            for t in range(NT):
                sp.dma_start(sx_rows[:, t, :], ZERO[:, :]).then_inc(zeroed, 16)

            def moe(kind, k):
                sp.wait_ge(scattered, 16 * T * (k + 1))
                for c, (a, b) in enumerate(chunks_of(kind)):
                    sp.dma_start(XS[:, a:b, :], sx_rows[:, a:b, :]).then_inc(xs_loaded[c], 16)
                if kind == "ffn1":
                    sp.wait_ge(owner_ready, k - 1)
                    for i in range(NT):
                        n = (k - 2) * NT + i
                        if n >= WR:
                            sp.wait_ge(eo_done, before(k, E, NT) + i - WR + 1 if i >= WR else before(k, E, NT))
                        e = sp.value_load(OWNERI[0:1, i:i + 1], min_val=0, max_val=E - 1)
                        sp.dma_start(WT[:, n % WR, :], f1_pack[bass.ds(e, 1), :, :].rearrange("a p w -> p (a w)")
                                     ).then_inc(w_loaded[n % WR], 16)
                        sp.dma_start(B2R[0:1, n % WR, :], f1_b2[bass.ds(e, 1), :]).then_inc(w_loaded[n % WR], 16)
                        if i >= 2:
                            store(kind, k, i - 2)
                    store(kind, k, NT - 2)
                    store(kind, k, NT - 1)
                else:
                    for e in range(E):
                        store(kind, k, e)

            def store(kind, k, i):
                sp.wait_ge(eo_copied, before(k, E, NT) + i + 1)
                a, b = (2 * i, 2 * i + 2) if kind == "ffn0" else (i, i + 1)
                sp.dma_start(sy_rows[:, a:b, :], EO[:, a:b, :]).then_inc(eo_stored, 16)

            def soft():
                for w, dst in enumerate((qd, kd)):
                    sp.wait_ge(parts_done, w + 1)
                    for a in range(3):
                        sp.dma_start(dst[a], PART[:, a, :]).then_inc(parts_stored, 16)
                sp.wait_ge(parts_stored, 96)
                sp.wait_ge(ring_zeroed, 3)

                def load_group(G):
                    b, ring = G // NG, G % Q3R
                    u, ab = (G % NG) // 2, G % 2
                    for a in range(3):
                        for c in range(3):
                            row = (3 * a + c) * DH
                            for dst, src, part in ((Q3, qd, a), (K3, kd, c)):
                                v = src[part].rearrange("(u g s d) n -> u s d g n", u=2, g=4, s=2)
                                sp.dma_start(dst[row:row + DH, ring, :, :], v[u, ab, :, :, b * S:(b + 1) * S]
                                             ).then_inc(ring_loaded[ring], 16)

                for G in range(Q3R):
                    load_group(G)
                for x in plan:
                    if x[0] == "M":
                        hh = x[1]
                        G, g = divmod(hh, 4)
                        sp.wait_ge(m_copied, hh + 1)
                        for r in range(3):
                            sp.dma_start(Q3[MR + r:MR + r + 1, G % Q3R, g, :].rearrange("o (i n) -> o i n", i=TB),
                                         MT[r * TB:(r + 1) * TB, hh % 4, :]).then_inc(m_rows[hh % 4], 16)
                    if x[0] == "V" and x[1] % TB == TB - 1:
                        G = x[1] // TB
                        if G + Q3R < GR:
                            sp.wait_ge(pv_done, TB * (G + 1))
                            load_group(G + Q3R)

            for kind, ln, k in STAGES:
                if kind in ("ffn0", "ffn1"):
                    moe(kind, k)
                elif kind == "soft":
                    soft()
            for t in range(T):
                sp.wait_ge(x_updated, T * 3 + t + 1)
                sp.dma_start(out_rows[:, t, :], X[:, t, :]).then_inc(out_stored, 16)
            sp.wait_ge(out_stored, 16 * T)

        @block.tensor
        def _(pe):
            ident = col("ident")

            def norm_turned(ln):
                for c in range(T // 4):
                    pe.wait_ge(xn_ready, T * ln + 4 * c + 4)
                    if 4 * ln + c >= 2:
                        pe.wait_ge(xt_copied, 4 * ln + c - 1)
                    for t in range(4 * c, 4 * c + 4):
                        i = nc.tensor.transpose(PS[:, c % 2, (t % 4) * P:(t % 4 + 1) * P], XN[:, t, :], ident)
                    i.then_inc(xt_turned, 1)

            def moe(kind, ln, k):
                wr = col("f0_wr" if kind == "ffn0" else "f1_wr")
                pe.wait_ge(xt_copied, 4 * ln + 4)
                for t in range(T):
                    i = nc.tensor.matmul(PS[:, 2, t * E:(t + 1) * E], XNT[:, t * P:(t + 1) * P], wr,
                                         start=True, stop=True)
                i.then_inc(logits_done, 1)
                pe.wait_ge(mask_ready, k + 1)
                nc.tensor.matmul(PS[:, 3, 0:P], TRI[:, :], MASKB[:, :], start=True, stop=True)
                nc.tensor.matmul(PS[:, 3, P:2 * P], ONES[:, :], MASKB[:, :], start=True,
                                 stop=True).then_inc(counts_done, 1)

                chunks = chunks_of(kind)
                nb = before(k, len(chunks_of("ffn0")), len(chunks_of("ffn1")))

                def turn(c):
                    a, b = chunks[c]
                    pe.wait_ge(xs_loaded[c], 16 * (k + 1 if c < 4 else k - 1))
                    if c >= 2:
                        pe.wait_ge(xs_copied, nb + c - 1)
                    for t in range(a, b):
                        i = nc.tensor.transpose(PS[:, c % 2, (t - a) * P:(t - a + 1) * P], XS[:, t, :], ident)
                    i.then_inc(xs_turned, 1)

                base = before(k, E, NT)
                if kind == "ffn0":
                    w1, w2 = col("f0_w1"), col("f0_w2")

                    def up(e):
                        pe.wait_ge(xs_copied, nb + e // 2 + 1)
                        if e >= 2:
                            pe.wait_ge(hid_active, base + e - 1)
                        nc.tensor.matmul(PS[:, 4 + e % 2, 0:CAP], w1[:, e * P:(e + 1) * P],
                                         XST[:, e * CAP:(e + 1) * CAP], start=True, stop=True).then_inc(hid_done, 1)

                    def down(e):
                        pe.wait_ge(hid_active, base + e + 1)
                        if e >= 2:
                            pe.wait_ge(eo_copied, base + e - 1)
                        for s in range(2):
                            i = nc.tensor.matmul(PS[:, 6 + e % 2, s * P:(s + 1) * P],
                                                 HG[:, e % 2, s * P:(s + 1) * P],
                                                 w2[:, e * P:(e + 1) * P], start=True, stop=True)
                        i.then_inc(eo_done, 1)

                    turn(0)
                    turn(1)
                    for e in range(E):
                        if e % 2 == 0 and e // 2 + 2 < len(chunks):
                            turn(e // 2 + 2)
                        up(e)
                        if e >= 1:
                            down(e - 1)
                    down(E - 1)
                    return

                def up1(i):
                    n = (k - 2) * NT + i
                    pe.wait_ge(xs_copied, nb + i // 4 + 1)
                    pe.wait_ge(w_loaded[n % WR], 32 * (n // WR + 1))
                    if i >= 2:
                        pe.wait_ge(hid_biased, n - 1)
                    for f in range(FB):
                        ins = nc.tensor.matmul(PS[:, 4 + i % 2, f * P:(f + 1) * P],
                                               WT[:, n % WR, f * P:(f + 1) * P],
                                               XST[:, i * P:(i + 1) * P], start=True, stop=True)
                    ins.then_inc(hid_done, 1)

                def down1(i):
                    n = (k - 2) * NT + i
                    pe.wait_ge(hid_active, base + i + 1)
                    if i >= 2:
                        pe.wait_ge(eo_copied, base + i - 1)
                    o = PS[:, 6 + i % 2, 0:P]
                    for f in range(FB):
                        nc.tensor.matmul(o, HG[:, i % 2, f * P:(f + 1) * P],
                                         WT[:, n % WR, F1 + f * P:F1 + (f + 1) * P], start=(f == 0), stop=False)
                    nc.tensor.matmul(o, ONE1[:, :], B2R[0:1, n % WR, :], start=False, stop=True).then_inc(eo_done, 1)

                turn(0)
                turn(1)
                for i in range(NT):
                    if i % 4 == 0 and i // 4 + 2 < len(chunks):
                        turn(i // 4 + 2)
                    up1(i)
                    if i >= 1:
                        down1(i - 1)
                down1(NT - 1)

            def linear(ln):
                pe.wait_ge(xt_copied, 4 * ln + 4)
                pe.wait_ge(rest_loaded, 16)
                for c in range(4):
                    i = nc.tensor.matmul(PS[:, c, :], col("a0_wg"), XNT[:, c * 512:(c + 1) * 512],
                                         start=True, stop=True)
                    i.then_inc(g_done, 1)
                for n in range(8):
                    w, c = n % 2, n // 2
                    if n >= 4:
                        pe.wait_ge(qk_ready, n - 3)
                    nc.tensor.matmul(PS[:, 4 + n % 4, :], col(("a0_wk", "a0_wq")[w]),
                                     XNT[:, c * 512:(c + 1) * 512], start=True, stop=True).then_inc(qk_done, 1)
                pe.wait_ge(g_ready, 4)
                pe.wait_ge(qk_ready, 8)

                def values(n):
                    b, j = divmod(n, DH)
                    if n >= 2:
                        pe.wait_ge(kv_done, n - 1)
                    for c in range(2):
                        i = nc.tensor.matmul(PS[:, 2 * (n % 2) + c, :], col("a0_wv", j * P, P),
                                             XNT[:, b * S + c * 512:b * S + (c + 1) * 512], start=True, stop=True)
                    i.then_inc(v_done, 1)

                def project(n):
                    b, j = divmod(n, DH)
                    pe.wait_ge(qs_done, n + 1)
                    for t in range(TB):
                        i = nc.tensor.matmul(PS[:, 4 + 2 * b + t // 4, (t % 4) * P:(t % 4 + 1) * P],
                                             QS[:, n % 2, t * P:(t + 1) * P], col("a0_wo", j * P, P),
                                             start=(j == 0 and t % 4 == 0), stop=(j == DH - 1),
                                             skip_group_check=True)
                    i.then_inc(lin_used, 1)

                values(0)
                values(1)
                for n in range(B * DH):
                    project(n)
                    if n + 2 < B * DH:
                        values(n + 2)

            def soft(ln):
                pe.wait_ge(xt_copied, 4 * ln + 4)
                for n in range(8):
                    w, c = n // 4, n % 4
                    if n >= 4:
                        pe.wait_ge(qf_done, n - 3)
                    nc.tensor.matmul(PS[:, n % 4, :], col(("a1_wq", "a1_wk")[w]),
                                     XNT[:, c * 512:(c + 1) * 512], start=True, stop=True).then_inc(proj_done, 1)
                for c in range(4):
                    for t in range(4 * c, 4 * c + 4):
                        i = nc.tensor.matmul(PS[:, 4 + c, (t % 4) * P:(t % 4 + 1) * P],
                                             XNT[:, t * P:(t + 1) * P], col("a1_wv"), start=True, stop=True)
                    i.then_inc(vproj_done, 1)
                pe.wait_ge(qf_done, 8)
                pe.wait_ge(v9_ready, 4)

                def wait_slot(n):
                    if n < 2:
                        return
                    kind, k, i = turns[n - 2]
                    if kind == "A":
                        pe.wait_ge(a_exp, k * TB + i + 1)
                    elif kind == "M":
                        pe.wait_ge(m_copied, k + 1)
                    else:
                        pe.wait_ge(z_scaled, 2 * k + i + 1)

                for x in plan:
                    kind, k, i = x
                    if kind in "AMT":
                        n = turn_number[x]
                        slot = 2 * (n % 2)
                        wait_slot(n)
                    if kind == "A":
                        G, g = divmod(k, 4)
                        if i == 0 and g == 0:
                            pe.wait_ge(ring_loaded[G % Q3R], 16 * 18 * (G // Q3R + 1))
                        for c in range(2):
                            ins = nc.tensor.matmul(PS[:, slot + c, :], Q3[0:KQ, G % Q3R, g, i * P:(i + 1) * P],
                                                   K3[0:KQ, G % Q3R, g, c * 512:(c + 1) * 512],
                                                   start=True, stop=True)
                        ins.then_inc(a_scores, 1)
                    elif kind == "M":
                        pe.wait_ge(m_split, k + 1)
                        o = PS[0:3 * TB, slot, 0:P // 2].bitcast(BF16)
                        nc.tensor.transpose(o, M3[:, k % 4, :], IDB[:, :]).then_inc(m_turned, 1)
                    elif kind == "T":
                        pe.wait_ge(z_copied, 4 * (k + 1))
                        for c in range(8 * i, 8 * i + 8):
                            src = ZT[:, :, :].rearrange("p a (r c) -> p c a r", c=16)[:, c]
                            ins = nc.tensor.transpose(PS[:, slot + (c % 8) // 4, (c % 4) * P:(c % 4 + 1) * P],
                                                      src, ident)
                        ins.then_inc(z_turned, 1)
                    elif kind == "B":
                        G, j = divmod(k, TB)
                        if j == 0:
                            pe.wait_ge(m_rows[i], 48 * (G + 1))
                        for c, (lo, hi) in enumerate(chunk_list(j)):
                            n = chunk_number[(k, i, c)]
                            if n >= 2:
                                pe.wait_ge(b_exp, n - 1)
                            nc.tensor.matmul(PS[:, 4 + n % 2, 0:hi - lo], K3[0:MR + 3, G % Q3R, i, j * P:(j + 1) * P],
                                             Q3[0:MR + 3, G % Q3R, i, lo:hi], start=True, stop=True
                                             ).then_inc(b_scores, 1)
                    else:
                        G, j = divmod(k, TB)
                        if j == 0:
                            if G >= 1:
                                pe.wait_ge(z_copied, 2 * G)
                            pe.wait_ge(a_exp, TB * 4 * (G + 1))
                            for q in range(TB):
                                for g in range(4):
                                    nc.tensor.matmul(PS[32 * g:32 * g + 32, 6 + q // 4, (q % 4) * P:(q % 4 + 1) * P],
                                                     D32[:, (4 * G + g) % DR, q, :], ident, start=(q % 4 == 0),
                                                     stop=False, skip_group_check=True)
                        pe.wait_ge(b_masked, 4 * (k + 1))
                        pe.wait_ge(b_exp, last_chunk(k, 3) + 1)
                        parts = [(lo, min(hi, P * j), 9) for lo, hi in chunk_list(j) if lo < P * j]
                        parts.append((P * j, P * (j + 1), 8))
                        for lo, hi, width in parts:
                            for g in range(4):
                                b, h = head_number(4 * G + g)
                                ins = nc.tensor.matmul(PS[32 * g:32 * g + width, 6 + lo // 512, lo % 512:lo % 512 + hi - lo],
                                                       V9[:, b * TB + j, h, 0:width],
                                                       PT[:, (4 * k + g) % NPT, lo:hi],
                                                       start=False, stop=(j == TB - 1), skip_group_check=True)
                        ins.then_inc(pv_done, 1)

            pe.wait_ge(early_loaded, 16)
            pe.wait_ge(consts_made, 3)
            pe.wait_ge(one_made, 1)
            for kind, ln, k in STAGES:
                norm_turned(ln)
                if kind == "ffn0":
                    pe.wait_ge(ffn0_loaded, 16)
                if kind in ("ffn0", "ffn1"):
                    moe(kind, ln, k)
                elif kind == "lin":
                    linear(ln)
                else:
                    soft(ln)

        @block.scalar
        def _(act):
            def std(n):
                act.wait_ge(var_ready, n + 1)
                nc.scalar.activation(RSTD[:, :], RSTD[:, :], ACT.Sqrt).then_inc(std_ready, 1)

            def norm_turned(ln):
                for c in range(T // 4):
                    act.wait_ge(xt_turned, 4 * ln + c + 1)
                    nc.scalar.copy(XNT[:, c * 512:(c + 1) * 512], PS[:, c % 2, :]).then_inc(xt_copied, 1)

            def moe(kind, k):
                act.wait_ge(lg_ready, k + 1)
                nc.scalar.activation(EX[:, :, :], LG[:, :, :], ACT.Exp).then_inc(ex_ready, 1)
                chunks = chunks_of(kind)
                nb = before(k, len(chunks_of("ffn0")), len(chunks_of("ffn1")))

                def copy_turned(c):
                    a, b = chunks[c]
                    act.wait_ge(xs_turned, nb + c + 1)
                    nc.scalar.copy(XST[:, a * P:b * P], PS[:, c % 2, 0:(b - a) * P]).then_inc(xs_copied, 1)

                copy_turned(0)
                copy_turned(1)
                base = before(k, E, NT)
                if kind == "ffn0":
                    for e in range(E):
                        if e % 2 == 0 and e // 2 + 2 < len(chunks):
                            copy_turned(e // 2 + 2)
                        act.wait_ge(hid_done, base + e + 1)
                        if e >= 2:
                            act.wait_ge(eo_done, base + e - 1)
                        nc.scalar.activation(HG[:, e % 2, 0:CAP], PS[:, 4 + e % 2, 0:CAP], ACT.Relu,
                                             bias=col("f0_b1", e, 1)).then_inc(hid_active, 1)
                    return
                for i in range(NT):
                    if i % 4 == 0 and i // 4 + 2 < len(chunks):
                        copy_turned(i // 4 + 2)
                    act.wait_ge(hid_biased, (k - 2) * NT + i + 1)
                    if i >= 2:
                        act.wait_ge(eo_done, base + i - 1)
                    nc.scalar.activation(HG[:, i % 2, :], HB[:, i % 2, :], ACT.Gelu).then_inc(hid_active, 1)

            def linear():
                for c in range(4):
                    act.wait_ge(g_done, c + 1)
                    nc.scalar.activation(GT[:, c * 512:(c + 1) * 512], PS[:, c, :], ACT.Sigmoid,
                                         bias=col("a0_bg")).then_inc(g_ready, 1)
                for n in range(8):
                    w = n % 2
                    scale = (1.0, QSCALE)[w]
                    act.wait_ge(qk_done, n + 1)
                    if n >= 2:
                        act.wait_ge(qk_ready, n - 1)
                    nc.scalar.activation(RL[:, n % 2, :], PS[:, 4 + n % 4, :], ACT.Relu,
                                         scale=scale).then_inc(relu_done, 1)
                    act.wait_ge(min_done, n + 1)
                    nc.scalar.activation(EXQ[:, n % 2, :], MN[:, n % 2, :], ACT.Exp,
                                         scale=scale).then_inc(exq_done, 1)

            def soft():
                for n in range(8):
                    w, c = n // 4, n % 4
                    act.wait_ge(proj_done, n + 1)
                    if w == 1:
                        act.wait_ge(parts_stored, 48)
                    qf = QF[:, c * 512:(c + 1) * 512]
                    first = nc.scalar.activation(qf, PS[:, n % 4, :], ACT.Identity,
                                                 bias=col(("a1_bq", "a1_bk")[w]))
                    if w == 1:
                        first.then_inc(qf_done, 1)
                        continue
                    first.then_inc(act_step, 1)
                    act.wait_ge(act_step, n + 1)
                    nc.scalar.activation(qf, qf, ACT.Copy, scale=S ** -0.5).then_inc(qf_done, 1)

                def a_probs(x):
                    _, hh, i = x
                    slot = 2 * (turn_number[x] % 2)
                    act.wait_ge(a_max, hh * TB + i + 1)
                    if hh >= DR and i == 0:
                        act.wait_ge(pv_done, TB * ((hh - DR) // 4) + 1)
                    w = P * (i + 1)
                    scores = PS[:, slot:slot + 2, :].rearrange("p b n -> p (b n)")[:, 0:w]
                    nc.scalar.activation(
                        scores, scores, ACT.Exp, bias=NM[:, hh % 4, i:i + 1], accum_out=D32[:, hh % DR, i, 8:9]).then_inc(a_exp, 1)

                late = None
                act.wait_ge(ring_zeroed, 3)
                for x in plan:
                    kind, k, i = x
                    if kind in "AMT":
                        if late is not None:
                            a_probs(late)
                            late = None
                        if kind == "A":
                            late = x
                    if kind == "M":
                        act.wait_ge(m_turned, k + 1)
                        if k >= 4:
                            act.wait_ge(m_rows[k % 4], 48 * (k // 4))
                        slot = 2 * (turn_number[x] % 2)
                        nc.scalar.copy(MT[0:3 * TB, k % 4, :], PS[0:3 * TB, slot, 0:P // 2].bitcast(BF16)
                                       ).then_inc(m_copied, 1)
                    elif kind == "B":
                        G, j = divmod(k, TB)
                        for c, (lo, hi) in enumerate(chunk_list(j)):
                            n = chunk_number[(k, i, c)]
                            act.wait_ge(b_scores, n + 1)
                            if c == 0 and k >= 2:
                                act.wait_ge(pv_done, k - 1)
                            nc.scalar.activation(PT[:, (4 * k + i) % NPT, lo:hi], PS[:, 4 + n % 2, 0:hi - lo],
                                                 ACT.Exp).then_inc(b_exp, 1)
                    elif kind == "V" and k % TB == TB - 1:
                        G = k // TB
                        act.wait_ge(pv_done, k + 1)
                        if G >= 2:
                            act.wait_ge(z_turned, 2 * (G // 2))
                        for c in range(2):
                            nc.scalar.copy(ZT[:, G % 2, c * 512:(c + 1) * 512], PS[:, 6 + c, :]).then_inc(z_copied, 1)

            for kind, ln, k in STAGES:
                std(ln if ln < 5 else 6)
                norm_turned(ln)
                if kind in ("ffn0", "ffn1"):
                    moe(kind, k)
                elif kind == "lin":
                    linear()
                else:
                    soft()
                    std(5)

        @block.vector
        def _(dve):
            steps = [0]

            def link(ins):
                steps[0] += 1
                ins.then_inc(dve_step, 1)
                dve.wait_ge(dve_step, steps[0])

            def norm(src, n):
                for t in range(T):
                    last = nc.vector.bn_stats(STATS[:, t, :], src[:, t, :])
                link(last)
                for t in range(T):
                    last = nc.vector.bn_aggr(MV[:, t, :], STATS[:, t, :])
                link(last)
                nc.vector.tensor_scalar(RSTD[:, :], MV[:, :, 1], EPS, None, ALU.add).then_inc(var_ready, 1)
                dve.wait_ge(std_ready, n + 1)
                link(nc.vector.reciprocal(RSTD[:, :], RSTD[:, :]))

            def normed(ln, n):
                norm(X, n)
                for t in range(T):
                    nc.vector.tensor_scalar(XN[:, t, :], X[:, t, :], MV[:, t, 0:1], RSTD[:, t:t + 1],
                                            ALU.subtract, ALU.mult).then_inc(xn_ready, 1)

            def over_e(a):
                return a.rearrange("p (t e) -> p e t", e=E)

            def moe(kind, k):
                dve.wait_ge(logits_done, k + 1)
                logits = PS[:, 2, 0:T * E].rearrange("p (t e) -> p t e", e=E)
                if kind == "ffn0":
                    br = col("f0_br").unsqueeze(1).to_broadcast([P, T, E])
                    link(nc.vector.tensor_tensor(LG[:, :, :], logits, br, ALU.add))
                else:
                    link(nc.vector.tensor_copy(LG[:, :, :], logits))
                link(nc.vector.tensor_reduce(LMAX[:, :], LG[:, :, :], AX.X, ALU.max))
                nc.vector.tensor_tensor(LG[:, :, :], LG[:, :, :], LMAX[:, :].unsqueeze(2).to_broadcast([P, T, E]),
                                        ALU.subtract).then_inc(lg_ready, 1)
                dve.wait_ge(lg_ready, k + 1)
                link(nc.vector.tensor_scalar(HIT[:, :], LG[:, :, :].rearrange("p t e -> p (t e)"), -(2.0 ** -25), None,
                                             ALU.is_ge))
                link(nc.vector.tensor_tensor_scan(NTH[:, :], col("r8"), HIT[:, :], 0.0, ALU.mult, ALU.add))
                link(nc.vector.scalar_tensor_tensor(out=MASK[:, :, :], in0=over_e(NTH[:, :]), scalar=1.0,
                                                    in1=over_e(HIT[:, :]), op0=ALU.is_equal, op1=ALU.mult))
                nc.vector.tensor_copy(MASKB[:, :], MASK[:, :, :].rearrange("p e t -> p (e t)")
                                      ).then_inc(mask_ready, 1)
                dve.wait_ge(ex_ready, k + 1)
                link(nc.vector.tensor_reduce(SUM[:, :], EX[:, :, :], AX.X, ALU.add))
                link(nc.vector.reciprocal(GATE[:, :], SUM[:, :]))
                if kind == "ffn0":
                    for t in range(T):
                        nc.vector.tensor_scalar(XG[:, t, :], XN[:, t, :], GATE[:, t:t + 1], None,
                                                ALU.mult).then_inc(xg_ready, 1)
                dve.wait_ge(counts_done, k + 1)
                within, total = PS[:, 3, 0:P], PS[:, 3, P:2 * P]
                link(nc.vector.tensor_tensor_scan(INCL[:, :], col("r16"), total, 0.0, ALU.mult, ALU.add))
                link(nc.vector.tensor_tensor(POS[:, :], INCL[:, :], total, ALU.subtract))
                link(nc.vector.tensor_tensor(POS[:, :], POS[:, :], within, ALU.add))
                pos = POS[:, :].rearrange("p (e t) -> p e t", e=E)
                by_t = PRD[:, :, :].rearrange("p e t -> p t e")
                if kind == "ffn0":
                    link(nc.vector.tensor_tensor(PRD[:, :, :], pos, MASK[:, :, :], ALU.mult))
                    link(nc.vector.tensor_reduce(PLACE[:, :], by_t, AX.X, ALU.add))
                    link(nc.vector.tensor_scalar(KEPT[:, :], PLACE[:, :], float(CAP), None, ALU.is_lt))
                    link(nc.vector.tensor_tensor(PRD[:, :, :], col("e256").rearrange("p (e t) -> p e t", e=E),
                                                 MASK[:, :, :], ALU.mult))
                    link(nc.vector.tensor_reduce(SLOT[:, :], by_t, AX.X, ALU.add))
                    link(nc.vector.tensor_tensor(SLOT[:, :], SLOT[:, :], PLACE[:, :], ALU.add))
                    link(nc.vector.tensor_scalar(SCAT[:, :], KEPT[:, :], -BIG, BIG, ALU.mult, ALU.add))
                    link(nc.vector.tensor_tensor(SCAT[:, :], SCAT[:, :], SLOT[:, :], ALU.add))
                    link(nc.vector.tensor_tensor(GATH[:, :], SLOT[:, :], KEPT[:, :], ALU.mult))
                    link(nc.vector.tensor_copy(GATHI[:, :], GATH[:, :]))
                    nc.vector.tensor_copy(SCATI[:, :], SCAT[:, :]).then_inc(index_ready, 1)
                    link(nc.vector.scalar_tensor_tensor(out=EFF[:, :], in0=GATE[:, :], scalar=0.5, in1=KEPT[:, :],
                                                        op0=ALU.mult, op1=ALU.mult))
                else:
                    ends = INCL[:, :].rearrange("p (e t) -> p e t", e=E)[:, :, T - 1:T].to_broadcast([P, E, T])
                    link(nc.vector.tensor_tensor(CMP[:, :, :], ends, col("jt").rearrange("p (e t) -> p e t", e=E),
                                                 ALU.is_gt))
                    link(nc.vector.tensor_reduce(TILES[:, :], CMP[:, :, :], AX.X, ALU.add))
                    link(nc.vector.tensor_tensor_scan(ENDS[:, :], col("ident", P - 1, 1).to_broadcast([P, E])
                                                      if False else col("r16", 1, E), TILES[:, :], 0.0,
                                                      ALU.mult, ALU.add))
                    link(nc.vector.tensor_tensor(BASE[:, :], ENDS[:, :], TILES[:, :], ALU.subtract))
                    link(nc.vector.tensor_scalar(BASE[:, :], BASE[:, :], float(P), -1.0, ALU.mult, ALU.add))
                    link(nc.vector.tensor_tensor(PRD[:, :, :], pos, BASE[:, :].unsqueeze(2).to_broadcast([P, E, T]),
                                                 ALU.add))
                    link(nc.vector.tensor_tensor(PRD[:, :, :], PRD[:, :, :], MASK[:, :, :], ALU.mult))
                    link(nc.vector.tensor_reduce(SLOT[:, :], by_t, AX.X, ALU.add))
                    link(nc.vector.tensor_copy(GATHI[:, :], SLOT[:, :]))
                    nc.vector.tensor_copy(SCATI[:, :], SLOT[:, :]).then_inc(index_ready, 1)
                    link(nc.vector.tensor_tensor(CMP2[:, :, :], col("ti").rearrange("p (i e) -> p i e", e=E),
                                                 ENDS[:, :].unsqueeze(1).to_broadcast([P, NT, E]), ALU.is_ge))
                    link(nc.vector.tensor_reduce(OWNER[:, :], CMP2[:, :, :], AX.X, ALU.add))
                    nc.vector.tensor_scalar(OWNERI[:, :], OWNER[:, :], float(E - 1), None, ALU.min
                                            ).then_inc(owner_ready, 1)
                    link(nc.vector.tensor_scalar(EFF[:, :], GATE[:, :], 0.5, None, ALU.mult))

                base = before(k, E, NT)
                if kind == "ffn0":
                    for e in range(E):
                        dve.wait_ge(eo_done, base + e + 1)
                        nc.vector.tensor_tensor(
                            EO[:, 2 * e:2 * e + 2, :],
                            PS[:, 6 + e % 2, 0:2 * P].rearrange("p (s d) -> p s d", s=2),
                            col("f0_b2", e * P, P).unsqueeze(1).to_broadcast([P, 2, P]), ALU.add
                        ).then_inc(eo_copied, 1)
                else:
                    def biased(i):
                        n = (k - 2) * NT + i
                        dve.wait_ge(hid_done, base + i + 1)
                        if i >= 2:
                            dve.wait_ge(hid_active, base + i - 1)
                        b1 = WT[:, n % WR, F1 + FB * P:WB].unsqueeze(2).to_broadcast([P, FB, P])
                        nc.vector.tensor_tensor(HB[:, i % 2, :].rearrange("p (f n) -> p f n", f=FB),
                                                PS[:, 4 + i % 2, :].rearrange("p (f n) -> p f n", f=FB), b1,
                                                ALU.add).then_inc(hid_biased, 1)

                    biased(0)
                    for i in range(NT):
                        if i + 1 < NT:
                            biased(i + 1)
                        dve.wait_ge(eo_done, base + i + 1)
                        nc.vector.tensor_copy(EO[:, i, :], PS[:, 6 + i % 2, 0:P]).then_inc(eo_copied, 1)
                for t in range(T):
                    dve.wait_ge(gathered[t], 16 * (k + 1))
                    last = nc.vector.scalar_tensor_tensor(out=X[:, t, :], in0=YG[:, t, :], scalar=EFF[:, t:t + 1],
                                                          in1=X[:, t, :], op0=ALU.mult, op1=ALU.add)
                    last.then_inc(x_updated, 1)
                dve.wait_ge(x_updated, T * (k + 1))

            def linear():
                for n in range(8):
                    w, c = n % 2, n // 2
                    dve.wait_ge(qk_done, n + 1)
                    if n >= 2:
                        dve.wait_ge(exq_done, n - 1)
                    dve.wait_ge(relu_done, n + 1)
                    nc.vector.tensor_scalar(MN[:, n % 2, :], PS[:, 4 + n % 4, :], 0.0, None,
                                            ALU.min).then_inc(min_done, 1)
                    dve.wait_ge(exq_done, n + 1)
                    nc.vector.tensor_tensor((KT, QT)[w][:, c * 512:(c + 1) * 512], RL[:, n % 2, :], EXQ[:, n % 2, :],
                                            ALU.add).then_inc(qk_ready, 1)
                dve.wait_ge(qk_ready, 8)
                dve.wait_ge(g_ready, 4)
                for n in range(B * DH):
                    b, j = divmod(n, DH)
                    dve.wait_ge(v_done, n + 1)
                    if n >= 2:
                        dve.wait_ge(state_done, n - 1)
                    ps = PS[:, 2 * (n % 2):2 * (n % 2) + 2, :].rearrange("p c n -> p (c n)")
                    nc.vector.tensor_tensor(KV[:, n % 2, :], KT[:, b * S:(b + 1) * S], ps, ALU.mult
                                            ).then_inc(kv_done, 1)
                    dve.wait_ge(kv_done, n + 1)
                    if n >= 2:
                        dve.wait_ge(qs_done, n - 1)
                    nc.vector.tensor_tensor_scan(ST[:, n % 2, :], GT[:, b * S:(b + 1) * S], KV[:, n % 2, :], 0.0,
                                                 ALU.mult, ALU.add).then_inc(state_done, 1)
                for b in range(B):
                    dve.wait_ge(lin_used, DH * (b + 1))
                    for c in range(2):
                        t = TB * b + 4 * c
                        xt = X[:, t:t + 4, :]
                        last = nc.vector.tensor_tensor(xt, xt, PS[:, 4 + 2 * b + c, :].rearrange("p (t d) -> p t d", t=4),
                                                       ALU.add)
                link(last)

            def soft():
                for w in range(2):
                    dve.wait_ge(qf_done, 4 * w + 4)
                    if w == 1:
                        dve.wait_ge(parts_stored, 48)
                    link(nc.vector.tensor_copy(PART[:, 0, :], QF[:, :]))
                    link(nc.vector.tensor_tensor(RF[:, :], QF[:, :], PART[:, 0, :], ALU.subtract))
                    link(nc.vector.tensor_copy(PART[:, 1, :], RF[:, :]))
                    nc.vector.tensor_tensor(PART[:, 2, :], RF[:, :], PART[:, 1, :], ALU.subtract
                                            ).then_inc(parts_done, 1)
                    dve.wait_ge(parts_done, w + 1)
                dve.wait_ge(v9_ones, 1)
                for c in range(4):
                    dve.wait_ge(vproj_done, c + 1)
                    nc.vector.tensor_tensor(
                        V9[:, 4 * c:4 * c + 4, :, 0:DH],
                        PS[:, 4 + c, :].rearrange("p (t h j) -> p t h j", t=4, h=H),
                        col("a1_bv").rearrange("p (h j) -> p h j", h=H).unsqueeze(1).to_broadcast([P, 4, H, DH]),
                        ALU.add).then_inc(v9_ready, 1)
                z_steps = 0
                for x in plan:
                    kind, k, i = x
                    if kind == "A":
                        slot = 2 * (turn_number[x] % 2)
                        dve.wait_ge(a_scores, k * TB + i + 1)
                        if k >= 4 and i == 0:
                            dve.wait_ge(m_split, k - 3)
                            dve.wait_ge(a_exp, (k - 3) * TB)
                        nc.vector.tensor_reduce(NM[:, k % 4, i:i + 1],
                                                PS[:, slot:slot + 2, :].rearrange("p b n -> p (b n)"),
                                                AX.X, ALU.max, negate=True).then_inc(a_max, 1)
                    elif kind == "T":
                        slot = 2 * (turn_number[x] % 2)
                        dve.wait_ge(z_turned, 2 * k + i + 1)
                        tile0 = 4 * k
                        zz = Z[:, tile0:tile0 + 4, 64 * i:64 * i + 64].rearrange("p g (c j) -> p c g j", j=DH)
                        ps = PS[:, slot:slot + 2, :].rearrange("p b (c g w) -> p (b c) g w", g=4, w=32)
                        if 2 * k + i >= 1:
                            dve.wait_ge(z_scaled, 2 * k + i)
                        link(nc.vector.reciprocal(RD[:, :, :], ps[:, :, :, 8]))
                        nc.vector.tensor_tensor(zz, ps[:, :, :, 0:DH],
                                                RD[:, :, :].unsqueeze(3).to_broadcast([P, 8, 4, DH]),
                                                ALU.mult).then_inc(z_scaled, 1)
                dve.wait_ge(z_scaled, GR)
                link(nc.vector.tensor_tensor(Z[:, :, :], Z[:, :, :], XN[:, :, :], ALU.add))
                norm(Z, 5)
                for t in range(T):
                    last = nc.vector.tensor_scalar(Z[:, t, :], Z[:, t, :], MV[:, t, 0:1], RSTD[:, t:t + 1],
                                                   ALU.subtract, ALU.mult)
                link(last)
                link(nc.vector.tensor_tensor(Z[:, :, :], Z[:, :, :],
                                             col("a1_gamma").unsqueeze(1).to_broadcast([P, T, P]), ALU.mult))
                link(nc.vector.tensor_tensor(Z[:, :, :], Z[:, :, :],
                                             col("a1_beta").unsqueeze(1).to_broadcast([P, T, P]), ALU.add))
                link(nc.vector.tensor_tensor(X[:, :, :], X[:, :, :], Z[:, :, :], ALU.add))

            dve.wait_ge(x_loaded, 64)
            first = True
            for kind, ln, k in STAGES:
                normed(ln, ln if ln < 5 else 6)
                if first:
                    dve.wait_ge(early_loaded, 16)
                    nc.vector.tensor_copy(TRI[:, :], col("tri")).then_inc(consts_made, 1)
                    nc.vector.tensor_copy(IDB[:, :], col("ident")).then_inc(consts_made, 1)
                    nc.vector.memset(ONES[:, :], 1.0).then_inc(consts_made, 1)
                    dve.wait_ge(ffn0_loaded, 16)
                    first = False
                if kind in ("ffn0", "ffn1"):
                    moe(kind, k)
                elif kind == "lin":
                    linear()
                else:
                    soft()

        @block.gpsimd
        def _(pool):
            def moe(kind, k):
                pool.wait_ge(index_ready, k + 1)
                src = XG if kind == "ffn0" else XN
                slots = tiles_of(kind) * P
                for t in range(T):
                    if kind == "ffn0":
                        pool.wait_ge(xg_ready, T * k + t + 1)
                    pool.indirect_dma_start(sx[0:slots, :], bass.IndirectOffsetOnAxis(ap=SCATI[:, t:t + 1], axis=0),
                                            src[:, t, :], None, bounds_check=slots - 1, oob_is_err=False
                                            ).then_inc(scattered, 16)
                pool.wait_ge(eo_stored, 16 * before(k + 1, E, NT))
                for t in range(T):
                    pool.indirect_dma_start(YG[:, t, :], None, sy[0:slots, :],
                                            bass.IndirectOffsetOnAxis(ap=GATHI[:, t:t + 1], axis=0),
                                            bounds_check=slots - 1, oob_is_err=False).then_inc(gathered[t], 16)

            def linear():
                pool.wait_ge(qk_ready, 8)
                for n in range(B * DH):
                    b = n // DH
                    pool.wait_ge(state_done, n + 1)
                    if n >= 2:
                        pool.wait_ge(lin_used, n - 1)
                    nc.gpsimd.tensor_tensor(QS[:, n % 2, :], QT[:, b * S:(b + 1) * S], ST[:, n % 2, :], ALU.mult
                                            ).then_inc(qs_done, 1)

            def soft():
                pool.wait_ge(xn_ready, T * 5)
                nc.gpsimd.memset(V9[:, :, :, :], 1.0).then_inc(v9_ones, 1)
                nc.gpsimd.memset(D32[:, :, :, :], 0.0).then_inc(ring_zeroed, 1)
                nc.gpsimd.memset(Q3[:, :, :, :], 0.0).then_inc(ring_zeroed, 1)
                nc.gpsimd.memset(K3[:, :, :, :], 0.0).then_inc(pool_step, 1)
                pool.wait_ge(pool_step, 1)
                nc.gpsimd.memset(K3[MR:P, :, :, :], 1.0).then_inc(ring_zeroed, 1)
                pool.wait_ge(ring_zeroed, 3)
                step = 1
                for x in plan:
                    kind, k, i = x
                    if kind == "M":
                        pool.wait_ge(a_max, (k + 1) * TB)
                        if k >= 4:
                            pool.wait_ge(m_turned, k - 3)
                        nm, rest = NM[:, k % 4, :], NMR[:, k % 4, :]
                        m3 = M3[:, k % 4, :]
                        for ins in range(4):
                            if ins == 0:
                                a = nc.gpsimd.tensor_copy(m3[:, 0:TB], nm)
                            elif ins == 1:
                                a = nc.gpsimd.tensor_tensor(rest, nm, m3[:, 0:TB], ALU.subtract)
                            elif ins == 2:
                                a = nc.gpsimd.tensor_copy(m3[:, TB:2 * TB], rest)
                            else:
                                nc.gpsimd.tensor_tensor(m3[:, 2 * TB:3 * TB], rest, m3[:, TB:2 * TB],
                                                        ALU.subtract).then_inc(m_split, 1)
                                continue
                            step += 1
                            a.then_inc(pool_step, 1)
                            pool.wait_ge(pool_step, step)
                    elif kind == "B":
                        j = k % TB
                        pool.wait_ge(b_exp, last_chunk(k, i) + 1)
                        d = PT[:, (4 * k + i) % NPT, j * P:(j + 1) * P]
                        nc.gpsimd.affine_select(out=d, in_=d, compare_op=ALU.is_ge, fill=0.0, base=0,
                                                pattern=[[-1, P]], channel_multiplier=1).then_inc(b_masked, 1)

            nc.gpsimd.memset(ZERO[:, :], 0.0).then_inc(zero_made, 1)
            nc.gpsimd.memset(ONE1[:, :], 1.0).then_inc(one_made, 1)
            pool.wait_ge(zeroed, 16 * NT)
            for kind, ln, k in STAGES:
                if kind in ("ffn0", "ffn1"):
                    moe(kind, k)
                elif kind == "lin":
                    linear()
                else:
                    soft()


def kernel(**inputs):
    import numpy as np
    import concourse.bacc as _bacc
    from concourse.bass_utils import run_bass_kernel_spmd as _run

    g = {k: np.asarray(v) for k, v in inputs.items()}
    x = np.ascontiguousarray(g["L0_attn_x"].reshape(N, P))
    f = np.float32

    def rows(v):
        return np.broadcast_to(v.reshape(1, -1), (P, v.size))

    k, q = np.arange(P)[:, None], np.arange(P)[None, :]
    w1, w2 = g["L1_ffn_W1"], g["L1_ffn_W2"]
    part = {
        "ident": (k == q).astype(f), "tri": (k <= q).astype(f),
        "r8": rows((np.arange(P) % E != 0).astype(f)), "r16": rows((np.arange(P) % T != 0).astype(f)),
        "e256": rows((np.arange(P) // T * CAP).astype(f)), "jt": rows((np.arange(P) % T * P).astype(f)),
        "ti": rows((np.arange(NT * E) // E).astype(f)),
        "f0_wr": g["L0_ffn_Wr"], "f0_br": rows(g["L0_ffn_br"]), "f0_b1": g["L0_ffn_b1"].T,
        "f1_wr": g["L1_ffn_Wr"],
        "a0_bg": np.repeat(g["L0_attn_bg"], DH)[:, None],
        "a1_bq": g["L1_attn_bq"][:, None], "a1_bk": g["L1_attn_bk"][:, None],
        "f0_w1": g["L0_ffn_W1"].transpose(1, 0, 2).reshape(P, E * P),
        "f0_w2": g["L0_ffn_W2"].transpose(1, 0, 2).reshape(P, E * P),
        "f0_b2": rows(g["L0_ffn_b2"]),
        "a0_wq": g["L0_attn_Wq"].T, "a0_wk": g["L0_attn_Wk"].T,
        "a0_wg": np.repeat(g["L0_attn_Wg"].T, DH, axis=1),
        "a0_wv": np.repeat(g["L0_attn_Wv"].T.reshape(P, H, DH).transpose(0, 2, 1)[..., None], DH, axis=3).reshape(P, DH * P),
        "a0_wo": np.repeat(g["L0_attn_Wo"].T.reshape(H, 1, DH * P), DH, axis=1).reshape(P, DH * P),
        "a1_wq": g["L1_attn_Wq"].T, "a1_wk": g["L1_attn_Wk"].T, "a1_wv": g["L1_attn_Wv"].T,
        "a1_bv": rows(g["L1_attn_bv"]), "a1_gamma": rows(g["L1_attn_gamma"]), "a1_beta": rows(g["L1_attn_beta"]),
    }
    for name, (_, width) in COLS.items():
        assert part[name].shape == (P, width), (name, part[name].shape)
    params = np.ascontiguousarray(np.concatenate([part[name] for name in COLS], axis=1))
    pack = np.ascontiguousarray(np.concatenate([
        w1, w2.reshape(E, FB, P, P).transpose(0, 2, 1, 3).reshape(E, P, FB * P),
        g["L1_ffn_b1"].reshape(E, FB, P).transpose(0, 2, 1)], axis=2))
    b2 = np.ascontiguousarray(g["L1_ffn_b2"])

    nc = _bacc.Bacc("TRN2", target_bir_lowering=False, num_devices=1)
    arrays = {"x_dram": x, "params_dram": params, "pack_dram": pack, "b2_dram": b2}
    args = [nc.dram_tensor(n, a.shape, F32, kind="ExternalInput").ap() for n, a in arrays.items()]
    args.append(nc.dram_tensor("out_dram", (N, P), F32, kind="ExternalOutput").ap())
    macaron_kernel(nc, *args)
    r = _run(nc, [arrays], core_ids=[0])
    return r.results[0]["out_dram"].reshape(B, S, P)
```

```python
from contextlib import ExitStack

import concourse.bass as bass
from concourse import mybir

ALU = mybir.AluOpType
ACT = mybir.ActivationFunctionType
AX = mybir.AxisListType
F32 = mybir.dt.float32
BF16 = mybir.dt.bfloat16
U32 = mybir.dt.uint32
I32 = mybir.dt.int32

P = 128
B, S = 2, 1024
N = B * S
T = N // P
TB = S // P
E = 8
CAP = N // E
F1 = 512
FB = F1 // P
NT = T + E - 1
H, DH = 16, 8
EPS = 1e-5
QSCALE = DH ** -0.5
BIG = 65536.0
WB = F1 + FB * P + FB

NG = H // 4
GR = B * NG
PAIRS = 9
KQ = PAIRS * DH
MR = KQ
Q3R = 3
HQ = TB // 2
NPT = 12
MI = 3
LEAD = 1
VD = 1
VG = 2
NBB = 3
STEPS = [(0, j) for j in range(TB)] + [(1, j) for j in range(TB) ]
NS = len(STEPS)
Z0 = 3
ZGAP = 2
ZSTEPS = [GR // 2 * NS + Z0 + ZGAP * n for n in range(8)]

COLS = {}


def _columns():
    at = 0
    for name, width in (
        ("ident", P), ("tri", P), ("r8", P), ("r16", P), ("e256", P), ("jt", P), ("ti", NT * E),
        ("f0_wr", E), ("f0_br", E), ("f0_b1", E), ("f1_wr", E), ("a0_bg", 1), ("a1_bq", 1), ("a1_bk", 1),
        ("f0_w1", E * P), ("f0_w2", E * P), ("f0_b2", E * P),
        ("a0_wq", P), ("a0_wk", P), ("a0_wg", P), ("a0_wv", DH * P), ("a0_wo", DH * P),
        ("a1_wq", P), ("a1_wk", P), ("a1_wv", P), ("a1_bv", P), ("a1_gamma", P), ("a1_beta", P),
    ):
        COLS[name] = (at, width)
        at += width
    return at


NCOL = _columns()
EARLY = COLS["f0_w1"][0]
FFN0 = COLS["a0_wq"][0]


def head_of(group, g):
    u, ab = (group % NG) // 2, group % 2
    return 8 * u + 2 * g + ab


def units_of(group):
    return [(4 * group + g, h) for h in range(2) for g in range(4)]


def tiles_of_unit(h):
    return range(HQ * h, HQ * (h + 1))


def attention_turns():
    turns, last = [], None
    for hh, h in [x for G in range(GR) for x in units_of(G)]:
        for n, i in enumerate(tiles_of_unit(h)):
            turns.append(("A", hh, i))
            if n == 1 and last:
                turns.append(("S", *last))
            if n == MI and last:
                turns.append(("M", *last))
        last = (hh, h)
    return turns + [("S", *last), ("M", *last)]


def attention_plan():
    turns = attention_turns()
    plan, at = [], 0
    ahead = turns.index(("M", 3, 0)) + 1 + LEAD
    rest = len(turns) - ahead
    while at < ahead:
        plan.append(turns[at])
        at += 1
    steps = GR * NS
    for m in range(steps):
        G, s = divmod(m, NS)
        for g in range(4):
            want = ahead + -(-rest * (4 * m + g + 1) // (4 * (steps - TB)))
            if g == 0 and s in (0, TB):
                want = max(want, turns.index(("M", 4 * G + 3, s // TB)) + 1 + LEAD)
            while at < min(want, len(turns)):
                plan.append(turns[at])
                at += 1
            plan.append(("B", m, g))
            if m >= VD and g == VG:
                plan.append(("V", m - VD, 0))
                if (m - VD + 1) % (2 * NS) == 0:
                    plan += [("T", (m - VD) // (2 * NS), 0), ("T", (m - VD) // (2 * NS), 1)]
        if m in ZSTEPS:
            plan.append(("Z", ZSTEPS.index(m), 0))
    assert at == len(turns)
    for m in range(steps - VD, steps):
        plan.append(("V", m, 0))
    plan += [("T", GR // 2 - 1, 0), ("T", GR // 2 - 1, 1)]
    return plan


def macaron_kernel(nc, x_in, params, f1_pack, f1_b2, out):
    with ExitStack() as ctx:
        def sb(name, shape, dt=F32):
            return ctx.enter_context(nc.sbuf_tensor(name, shape, dt))

        def sem(name):
            return ctx.enter_context(nc.semaphore(name))

        X = sb("X", [P, T, P])
        XN = sb("XN", [P, T, P])
        XNT = sb("XNT", [P, N])
        C = sb("C", [P, NCOL])
        TRI = sb("TRI", [P, P], BF16)
        ONES = sb("ONES", [P, P], BF16)
        IDB = sb("IDB", [P, P], BF16)
        STATS = sb("STATS", [P, T, 6])
        MV = sb("MV", [P, T, 2])
        RSTD = sb("RSTD", [P, T])
        ZERO = sb("ZERO", [P, P])
        MT = sb("MT", [P, 4, P], BF16)
        B2 = sb("B2", [P, E * P])
        LG = sb("LG", [P, T, E])
        LMAX = sb("LMAX", [P, T])
        EX = sb("EX", [P, T, E])
        SUM = sb("SUM", [P, T])
        GATE = sb("GATE", [P, T])
        HIT = sb("HIT", [P, T * E])
        NTH = sb("NTH", [P, T * E])
        MASK = sb("MASK", [P, E, T])
        MASKB = sb("MASKB", [P, E * T], BF16)
        INCL = sb("INCL", [P, E * T])
        POS = sb("POS", [P, E * T])
        PRD = sb("PRD", [P, E, T])
        SLOT = sb("SLOT", [P, T])
        PLACE = sb("PLACE", [P, T])
        KEPT = sb("KEPT", [P, T])
        SCAT = sb("SCAT", [P, T])
        GATH = sb("GATH", [P, T])
        EFF = sb("EFF", [P, T])
        CMP = sb("CMP", [P, E, T])
        TILES = sb("TILES", [P, E])
        ENDS = sb("ENDS", [P, E])
        BASE = sb("BASE", [P, E])
        CMP2 = sb("CMP2", [P, NT, E])
        OWNER = sb("OWNER", [P, NT])
        OWNERI = sb("OWNERI", [P, NT], I32)
        SCATI = sb("SCATI", [P, T], U32)
        GATHI = sb("GATHI", [P, T], U32)

        ARENA = sb("ARENA", [P, 32768])

        class Carve:
            def __init__(self):
                self.at = 0

            def __call__(self, *shape):
                size = 1
                for s in shape:
                    size *= s
                a = ARENA[:, self.at:self.at + size]
                self.at += size
                assert self.at <= 32768
                return a

            def bf(self, size):
                a = ARENA[:, self.at:self.at + size // 2].bitcast(BF16)
                self.at += size // 2
                assert self.at <= 32768
                return a

        WEIGHTS = 32768 - E * WB
        WT = ARENA[:, WEIGHTS:WEIGHTS + E * WB]

        m = Carve()
        XG = m(T * P).rearrange("p (t d) -> p t d", t=T)
        YG = m(T * P).rearrange("p (t d) -> p t d", t=T)
        XS = m(NT * P).rearrange("p (t d) -> p t d", t=NT)
        XST = m(NT * P)
        EO = m(NT * P).rearrange("p (t d) -> p t d", t=NT)
        HB = m(2 * F1).rearrange("p (r f) -> p r f", r=2)
        HG = m(2 * F1).rearrange("p (r f) -> p r f", r=2)
        W1 = m(2 * F1).rearrange("p (r f) -> p r f", r=2)
        assert m.at <= WEIGHTS

        m = Carve()
        KT = m(N)
        QT = m(N)
        GT = m(N)
        RL = m(2 * 512).rearrange("p (r n) -> p r n", r=2)
        MN = m(2 * 512).rearrange("p (r n) -> p r n", r=2)
        EXQ = m(2 * 512).rearrange("p (r n) -> p r n", r=2)
        KV = m(2 * S).rearrange("p (r n) -> p r n", r=2)
        ST = m(2 * S).rearrange("p (r n) -> p r n", r=2)
        QS = m(2 * S).rearrange("p (r n) -> p r n", r=2)

        m = Carve()
        Q3 = m.bf(Q3R * 4 * S).rearrange("p (r g n) -> p r g n", r=Q3R, g=4)
        K3 = m.bf(Q3R * 4 * S).rearrange("p (r g n) -> p r g n", r=Q3R, g=4)
        SPLIT = m.at
        PT = m(NPT * 512).rearrange("p (r n) -> p r n", r=NPT)
        MD = m(NPT * P).rearrange("p (r n) -> p r n", r=NPT)
        ZT = m(2 * S).rearrange("p (r n) -> p r n", r=2)
        m.at = max(m.at, SPLIT + 2 * 1024 + 2 * 3 * N // 2)
        V9 = m(T * H * 9).rearrange("p (t h j) -> p t h j", t=T, h=H)
        BQS = m(1)
        ONE8 = m(32)
        NM = m(4 * TB).rearrange("p (r i) -> p r i", r=4)
        NMR = m(4 * TB).rearrange("p (r i) -> p r i", r=4)
        M3 = m.bf(4 * 3 * TB).rearrange("p (r c) -> p r c", r=4)
        RD = m(32).rearrange("p (c g) -> p c g", g=4)
        assert m.at <= WEIGHTS
        sp0 = ARENA[:, SPLIT:SPLIT + 2 * 1024 + 2 * 3 * N // 2]
        QF = sp0[:, 0:1024].rearrange("p (r n) -> p r n", r=2)
        RF = sp0[:, 1024:2048].rearrange("p (r n) -> p r n", r=2)
        PART = sp0[:, 2048:].bitcast(BF16).rearrange("p (w a n) -> p w a n", w=2, a=3)
        Z = XNT[:, :].rearrange("p (t d) -> p t d", t=T)

        PS = ctx.enter_context(nc.psum_tensor("PS", [P, 8, 512], F32))

        sx = nc.dram_tensor("slots_x", [NT * P, P], F32, kind="Internal").ap()
        sy = nc.dram_tensor("slots_y", [NT * P, P], F32, kind="Internal").ap()
        qd = nc.dram_tensor("q_parts", [H, 3, DH, N], BF16, kind="Internal").ap()
        kd = nc.dram_tensor("k_parts", [H, 3, DH, N], BF16, kind="Internal").ap()

        def col(name, k=None, n=None):
            at, width = COLS[name]
            if k is None:
                return C[:, at:at + width]
            return C[:, at + k:at + k + n]

        x_loaded = [sem(f"x_loaded{c}") for c in range(4)]
        early_loaded = sem("early_loaded")
        ffn0_loaded = sem("ffn0_loaded")
        rest_loaded = sem("rest_loaded")
        consts_made = sem("consts_made")
        zero_made = sem("zero_made")
        zeroed = sem("zeroed")
        dve_step = sem("dve_step")
        pool_step = sem("pool_step")
        act_step = sem("act_step")
        var_ready = sem("var_ready")
        std_ready = sem("std_ready")
        xn_ready = sem("xn_ready")
        xt_turned = sem("xt_turned")
        xt_copied = sem("xt_copied")
        logits_done = sem("logits_done")
        lg_ready = sem("lg_ready")
        ex_ready = sem("ex_ready")
        mask_ready = sem("mask_ready")
        counts_done = sem("counts_done")
        index_ready = sem("index_ready")
        owner_ready = sem("owner_ready")
        xg_ready = sem("xg_ready")
        scattered = sem("scattered")
        xs_loaded = [sem(f"xs_loaded{k}") for k in range(6)]
        xs_turned = sem("xs_turned")
        xs_copied = sem("xs_copied")
        hid_done = sem("hid_done")
        hid_biased = sem("hid_biased")
        hid_active = sem("hid_active")
        eo_done = sem("eo_done")
        eo_copied = sem("eo_copied")
        eo_stored = sem("eo_stored")
        w_loaded = sem("w_loaded")
        w1_copied = sem("w1_copied")
        gathered = [sem(f"gathered{k}") for k in range(T)]
        x_updated = sem("x_updated")
        g_done = sem("g_done")
        g_ready = sem("g_ready")
        qk_done = sem("qk_done")
        relu_done = sem("relu_done")
        min_done = sem("min_done")
        exq_done = sem("exq_done")
        qk_ready = sem("qk_ready")
        v_done = sem("v_done")
        kv_done = sem("kv_done")
        state_done = sem("state_done")
        qs_done = sem("qs_done")
        lin_used = sem("lin_used")
        lin_done = sem("lin_done")
        proj_done = sem("proj_done")
        qf_done = sem("qf_done")
        part0_done = sem("part0_done")
        parts_done = sem("parts_done")
        parts_stored = [sem(f"parts_stored{b}") for b in range(B)]
        vproj_done = sem("vproj_done")
        v9_ones = sem("v9_ones")
        v9_ready = sem("v9_ready")
        ones_loaded = sem("ones_loaded")
        one8_made = sem("one8_made")
        ring_loaded = [sem(f"ring_loaded{k}") for k in range(Q3R)]
        a_scores = sem("a_scores")
        a_max = sem("a_max")
        m_split = sem("m_split")
        m_turned = sem("m_turned")
        m_copied = sem("m_copied")
        m_rows = [sem(f"m_rows{k}") for k in range(4)]
        b_scores = sem("b_scores")
        b_exp = sem("b_exp")
        b_masked = sem("b_masked")
        pv_done = sem("pv_done")
        z_copied = sem("z_copied")
        z_turned = sem("z_turned")
        z_scaled = sem("z_scaled")
        out_stored = sem("out_stored")

        x_rows = x_in.rearrange("(t p) d -> p t d", p=P)
        out_rows = out.rearrange("(t p) d -> p t d", p=P)
        sx_rows = sx.rearrange("(t p) d -> p t d", p=P)
        sy_rows = sy.rearrange("(t p) d -> p t d", p=P)

        STAGES = (("ffn0", 0, 0), ("lin", 1, None), ("ffn0", 2, 1), ("ffn1", 3, 2), ("soft", 4, None), ("ffn1", 5, 3))

        def tiles_of(kind):
            return T if kind == "ffn0" else NT

        def chunks_of(kind):
            n = tiles_of(kind)
            return [(a, min(a + 4, n)) for a in range(0, n, 4)]

        def before(k, per0, per1):
            return min(k, 2) * per0 + max(k - 2, 0) * per1

        plan = attention_plan()
        turns = [x for x in plan if x[0] in "AT"]
        ring = [x for x in plan if x[0] in "BM"]
        ring_number = {x: n for n, x in enumerate(ring)}
        scores = [x for x in turns if x[0] == "A"]
        score_number = {x: n for n, x in enumerate(scores)}
        maxima = [x[1:] for x in plan if x[0] == "M"]
        maxima_number = {x: n for n, x in enumerate(maxima)}
        last_scores = {}
        for hh, h in maxima:
            last_scores[hh, h] = score_number["A", hh, tiles_of_unit(h)[-1]]

        def last_unit(hh):
            return max(n for n, x in enumerate(maxima) if x[0] == hh)

        def rows_stored(hh, h):
            return 16 * sum(x[0] % 4 == hh % 4 for x in maxima[:maxima_number[hh, h] + 1])
        turn_number = {x: n for n, x in enumerate(turns)}

        def columns(m):
            half, j = STEPS[m % NS]
            if half == 0:
                return 4 * P, (P * j if j < HQ else None)
            return 4 * P, (P * (j - HQ) if j >= HQ else None)

        def unit_columns(h):
            return 3 * HQ * h, 3 * HQ

        def masked_before(m):
            return 4 * (2 * HQ * (m // NS) + sum(columns(k)[1] is not None for k in range(m % NS)))

        def head_number(hh):
            G, g = divmod(hh, 4)
            return G // NG, head_of(G, g)

        block = ctx.enter_context(nc.Block())

        @block.sync
        def _(sp):
            for a in range(0, T, 4):
                sp.dma_start(X[:, a:a + 4, :], x_rows[:, a:a + 4, :]).then_inc(x_loaded[a // 4], 16)
            sp.dma_start(C[:, 0:EARLY], params[:, 0:EARLY]).then_inc(early_loaded, 16)
            sp.dma_start(C[:, EARLY:FFN0], params[:, EARLY:FFN0]).then_inc(ffn0_loaded, 16)
            sp.dma_start(C[:, FFN0:NCOL], params[:, FFN0:NCOL]).then_inc(rest_loaded, 16)
            sp.wait_ge(zero_made, 1)
            for t in range(NT):
                sp.dma_start(sx_rows[:, t, :], ZERO[:, :]).then_inc(zeroed, 16)
            for e in range(E):
                sp.dma_start(WT[:, e * WB:(e + 1) * WB], f1_pack[e]).then_inc(w_loaded, 16)
            sp.dma_start(B2[:, :], f1_b2[:, :]).then_inc(w_loaded, 16)

            def moe(kind, k):
                sp.wait_ge(scattered, 16 * T * (k + 1))
                for c, (a, b) in enumerate(chunks_of(kind)):
                    sp.dma_start(XS[:, a:b, :], sx_rows[:, a:b, :]).then_inc(xs_loaded[c], 16)
                for i in range(E if kind == "ffn0" else NT):
                    store(kind, k, i)

            def store(kind, k, i):
                sp.wait_ge(eo_copied, before(k, E, NT) + i + 1)
                a, b = (2 * i, 2 * i + 2) if kind == "ffn0" else (i, i + 1)
                sp.dma_start(sy_rows[:, a:b, :], EO[:, a:b, :]).then_inc(eo_stored, 16)

            def soft():
                def store_parts(b, w):
                    sp.wait_ge(parts_done, 2 * (2 * b + w + 1))
                    half = slice(b * S, (b + 1) * S)
                    for a in range(3):
                        sp.dma_start((qd, kd)[w][:, a, :, half], PART[:, w, a, half]).then_inc(parts_stored[b], 16)

                def load_group(G):
                    sp.wait_ge(parts_stored[G // NG], 6 * 16)
                    b, ring = G // NG, G % Q3R
                    u, ab = (G % NG) // 2, G % 2
                    heads = slice(8 * u + ab, 8 * u + ab + 7, 2)
                    for c in range(3):
                        row = 3 * DH * c
                        q = qd[heads, :, :, b * S:(b + 1) * S].rearrange("g a d n -> (a d) g n")
                        sp.dma_start(Q3[row:row + 3 * DH, ring, :, :], q).then_inc(ring_loaded[ring], 16)
                        k = kd[heads, c, :, b * S:(b + 1) * S].rearrange("g d n -> d g n")
                        for a in range(3):
                            sp.dma_start(K3[row + DH * a:row + DH * (a + 1), ring, :, :], k
                                         ).then_inc(ring_loaded[ring], 16)

                store_parts(0, 0)
                store_parts(0, 1)
                load_group(0)
                for r in range(3):
                    sp.dma_start(K3[MR + r:MR + r + 1, :, :, :].rearrange("o r g n -> o (r g n)"),
                                 ONES[0:Q3R * 4 * S // P, :]).then_inc(ones_loaded, 16)
                store_parts(1, 0)
                store_parts(1, 1)
                for G in range(1, Q3R):
                    load_group(G)
                for x in plan:
                    if x[0] == "M":
                        _, hh, h = x
                        G, g = divmod(hh, 4)
                        tiles = tiles_of_unit(h)
                        sp.wait_ge(m_copied, maxima_number[hh, h] + 1)
                        sp.dma_start(Q3[MR:MR + 3, G % Q3R, g, tiles[0] * P:(tiles[-1] + 1) * P],
                                     MT[0:3 * len(tiles), hh % 4, :]).then_inc(m_rows[hh % 4], 16)
                    if x[0] == "V" and x[1] % NS == NS - 1:
                        G = x[1] // NS
                        if G + Q3R < GR:
                            sp.wait_ge(pv_done, NS * (G + 1))
                            load_group(G + Q3R)

            for kind, ln, k in STAGES:
                if kind in ("ffn0", "ffn1"):
                    moe(kind, k)
                elif kind == "soft":
                    soft()
            for t in range(T):
                sp.wait_ge(x_updated, T * 3 + t + 1)
                sp.dma_start(out_rows[:, t, :], X[:, t, :]).then_inc(out_stored, 16)
            sp.wait_ge(out_stored, 16 * T)

        @block.tensor
        def _(pe):
            ident = col("ident")

            def norm_turned(ln, kind):
                wr = col("f0_wr" if kind == "ffn0" else "f1_wr")

                def logits(c):
                    pe.wait_ge(xt_copied, 4 * ln + c + 1)
                    for t in range(4 * c, 4 * c + 4):
                        i = nc.tensor.matmul(PS[:, 2, t * E:(t + 1) * E], XNT[:, t * P:(t + 1) * P], wr,
                                             start=True, stop=True)
                    return i

                if ln == 5:
                    pe.wait_ge(z_scaled, GR)
                for c in range(T // 4):
                    pe.wait_ge(xn_ready, T * ln + 4 * c + 4)
                    if 4 * ln + c >= 2:
                        pe.wait_ge(xt_copied, 4 * ln + c - 1)
                    for t in range(4 * c, 4 * c + 4):
                        i = nc.tensor.transpose(PS[:, c % 2, (t % 4) * P:(t % 4 + 1) * P], XN[:, t, :], ident)
                    i.then_inc(xt_turned, 1)
                    if kind in ("ffn0", "ffn1") and c >= 1:
                        logits(c - 1)
                if kind in ("ffn0", "ffn1"):
                    logits(T // 4 - 1).then_inc(logits_done, 1)

            def moe(kind, ln, k):
                pe.wait_ge(mask_ready, k + 1)
                nc.tensor.matmul(PS[:, 3, 0:P], TRI[:, :], MASKB[:, :], start=True, stop=True)
                nc.tensor.matmul(PS[:, 3, P:2 * P], ONES[:, :], MASKB[:, :], start=True,
                                 stop=True).then_inc(counts_done, 1)

                chunks = chunks_of(kind)
                nb = before(k, len(chunks_of("ffn0")), len(chunks_of("ffn1")))

                def turn(c):
                    a, b = chunks[c]
                    pe.wait_ge(xs_loaded[c], 16 * (k + 1 if c < 4 else k - 1))
                    if c >= 2:
                        pe.wait_ge(xs_copied, nb + c - 1)
                    for t in range(a, b):
                        i = nc.tensor.transpose(PS[:, c % 2, (t - a) * P:(t - a + 1) * P], XS[:, t, :], ident)
                    i.then_inc(xs_turned, 1)

                base = before(k, E, NT)
                if kind == "ffn0":
                    w1, w2 = col("f0_w1"), col("f0_w2")

                    def up(e):
                        pe.wait_ge(xs_copied, nb + e // 2 + 1)
                        if e >= 2:
                            pe.wait_ge(hid_active, base + e - 1)
                        nc.tensor.matmul(PS[:, 4 + e % 2, 0:CAP], w1[:, e * P:(e + 1) * P],
                                         XST[:, e * CAP:(e + 1) * CAP], start=True, stop=True).then_inc(hid_done, 1)

                    def down(e):
                        pe.wait_ge(hid_active, base + e + 1)
                        if e >= 2:
                            pe.wait_ge(eo_copied, base + e - 1)
                        for s in range(2):
                            i = nc.tensor.matmul(PS[:, 6 + e % 2, s * P:(s + 1) * P],
                                                 HG[:, e % 2, s * P:(s + 1) * P],
                                                 w2[:, e * P:(e + 1) * P], start=True, stop=True)
                        i.then_inc(eo_done, 1)

                    turn(0)
                    turn(1)
                    for e in range(E):
                        if e % 2 == 0 and e // 2 + 2 < len(chunks):
                            turn(e // 2 + 2)
                        up(e)
                        if e >= 1:
                            down(e - 1)
                    down(E - 1)
                    return

                pe.wait_ge(w_loaded, 16 * (E + 1))
                pe.wait_ge(owner_ready, k - 1)
                owner = {}

                def up1(i):
                    n = (k - 2) * NT + i
                    owner[i] = pe.value_load(OWNERI[0:1, i:i + 1], min_val=0, max_val=E - 1)
                    pe.wait_ge(xs_copied, nb + i // 4 + 1)
                    pe.wait_ge(w1_copied, n + 1)
                    if i >= 2:
                        pe.wait_ge(hid_biased, n - 1)
                    for f in range(FB):
                        ins = nc.tensor.matmul(PS[:, 4 + i % 2, f * P:(f + 1) * P],
                                               W1[:, i % 2, f * P:(f + 1) * P],
                                               XST[:, i * P:(i + 1) * P], start=True, stop=True)
                    ins.then_inc(hid_done, 1)

                def down1(i):
                    pe.wait_ge(hid_active, base + i + 1)
                    if i >= 2:
                        pe.wait_ge(eo_copied, base + i - 1)
                    o = PS[:, 6 + i % 2, 0:P]
                    for f in range(FB):
                        ins = nc.tensor.matmul(o, HG[:, i % 2, f * P:(f + 1) * P],
                                               WT[:, bass.ds(owner[i] * WB + F1 + f * P, P)], start=(f == 0),
                                               stop=(f == FB - 1))
                    ins.then_inc(eo_done, 1)

                turn(0)
                turn(1)
                for i in range(NT):
                    if i % 4 == 0 and i // 4 + 2 < len(chunks):
                        turn(i // 4 + 2)
                    up1(i)
                    if i >= 1:
                        down1(i - 1)
                down1(NT - 1)

            def linear(ln):
                pe.wait_ge(xt_copied, 4 * ln + 4)
                pe.wait_ge(rest_loaded, 16)
                for c in range(4):
                    i = nc.tensor.matmul(PS[:, c, :], col("a0_wg"), XNT[:, c * 512:(c + 1) * 512],
                                         start=True, stop=True)
                    i.then_inc(g_done, 1)
                for n in range(8):
                    w, c = n % 2, n // 2
                    if n >= 4:
                        pe.wait_ge(qk_ready, n - 3)
                    nc.tensor.matmul(PS[:, 4 + n % 4, :], col(("a0_wk", "a0_wq")[w]),
                                     XNT[:, c * 512:(c + 1) * 512], start=True, stop=True).then_inc(qk_done, 1)
                pe.wait_ge(g_ready, 4)
                pe.wait_ge(qk_ready, 8)

                def values(n):
                    b, j = divmod(n, DH)
                    if n >= 2:
                        pe.wait_ge(kv_done, n - 1)
                    for c in range(2):
                        i = nc.tensor.matmul(PS[:, 2 * (n % 2) + c, :], col("a0_wv", j * P, P),
                                             XNT[:, b * S + c * 512:b * S + (c + 1) * 512], start=True, stop=True)
                    i.then_inc(v_done, 1)

                def project(n):
                    b, j = divmod(n, DH)
                    pe.wait_ge(qs_done, n + 1)
                    for t in range(TB):
                        i = nc.tensor.matmul(PS[:, 4 + 2 * b + t // 4, (t % 4) * P:(t % 4 + 1) * P],
                                             QS[:, n % 2, t * P:(t + 1) * P], col("a0_wo", j * P, P),
                                             start=(j == 0 and t % 4 == 0), stop=(j == DH - 1),
                                             skip_group_check=True)
                    i.then_inc(lin_used, 1)

                values(0)
                values(1)
                for n in range(B * DH):
                    project(n)
                    if n + 2 < B * DH:
                        values(n + 2)

            def soft(ln):
                pe.wait_ge(xt_copied, 4 * ln + 4)
                for n in range(8):
                    c, w = 2 * (n // 4) + n % 2, n // 2 % 2
                    if n >= 4:
                        pe.wait_ge(qf_done, n - 3)
                    nc.tensor.matmul(PS[:, n % 4, :], col(("a1_wq", "a1_wk")[w]),
                                     XNT[:, c * 512:(c + 1) * 512], start=True, stop=True).then_inc(proj_done, 1)
                for c in range(4):
                    for t in range(4 * c, 4 * c + 4):
                        i = nc.tensor.matmul(PS[:, 4 + c, (t % 4) * P:(t % 4 + 1) * P],
                                             XNT[:, t * P:(t + 1) * P], col("a1_wv"), start=True, stop=True)
                    i.then_inc(vproj_done, 1)
                pe.wait_ge(qf_done, 8)
                pe.wait_ge(one8_made, 1)

                def wait_slot(n):
                    if n < 2:
                        return
                    kind, k, i = turns[n - 2]
                    if kind == "A":
                        pe.wait_ge(a_max, score_number["A", k, i] + 1)
                    else:
                        pe.wait_ge(z_scaled, 2 * k + i + 1)

                def wait_ring(x):
                    n = ring_number[x]
                    if n < NBB:
                        return
                    kind, k, i = ring[n - NBB]
                    if kind == "M":
                        pe.wait_ge(m_copied, maxima_number[k, i] + 1)
                    else:
                        pe.wait_ge(b_exp, 4 * k + i + 1)

                begun = set()
                pe.wait_ge(v9_ready, 4)
                for x in plan:
                    kind, k, i = x
                    if kind in "AT":
                        n = turn_number[x]
                        slot = 2 * (n % 2)
                        wait_slot(n)
                    elif kind in "BM":
                        bank = 4 + ring_number[x] % NBB
                        wait_ring(x)
                    if kind == "A":
                        G, g = divmod(k, 4)
                        if G not in begun:
                            begun.add(G)
                            pe.wait_ge(ring_loaded[G % Q3R], 16 * 12 * (G // Q3R + 1))
                        for c in range(2):
                            ins = nc.tensor.matmul(PS[:, slot + c, :], Q3[0:KQ, G % Q3R, g, i * P:(i + 1) * P],
                                                   K3[0:KQ, G % Q3R, g, c * 512:(c + 1) * 512],
                                                   start=True, stop=True)
                        ins.then_inc(a_scores, 1)
                    elif kind == "M":
                        pe.wait_ge(m_split, maxima_number[k, i] + 1)
                        at, width = unit_columns(i)
                        o = PS[0:width, bank, 0:P // 2].bitcast(BF16)
                        nc.tensor.transpose(o, M3[:, k % 4, at:at + width], IDB[:, :]).then_inc(m_turned, 1)
                    elif kind == "T":
                        pe.wait_ge(z_copied, 4 * (k + 1))
                        for c in range(8 * i, 8 * i + 8):
                            src = ZT[:, :, :].rearrange("p a (r c) -> p c a r", c=16)[:, c]
                            ins = nc.tensor.transpose(PS[:, slot + (c % 8) // 4, (c % 4) * P:(c % 4 + 1) * P],
                                                      src, ident)
                        ins.then_inc(z_turned, 1)
                    elif kind == "B":
                        G, st = divmod(k, NS)
                        half, j = STEPS[st]
                        if st in (0, TB):
                            pe.wait_ge(m_rows[i], rows_stored(4 * G + i, half))
                        if k == 0:
                            pe.wait_ge(ones_loaded, 48)
                        w = columns(k)[0]
                        nc.tensor.matmul(PS[:, bank, 0:w], K3[0:MR + 3, G % Q3R, i, j * P:(j + 1) * P],
                                         Q3[0:MR + 3, G % Q3R, i, half * 512:half * 512 + w], start=True, stop=True
                                         ).then_inc(b_scores, 1)
                    elif kind == "V":
                        G, st = divmod(k, NS)
                        half, j = STEPS[st]
                        w, diag = columns(k)
                        if st in (0, TB) and 2 * G + half >= 1:
                            pe.wait_ge(z_copied, 2 * G + half)
                        pe.wait_ge(b_exp, 4 * (k + 1))
                        parts = []
                        if diag is None:
                            parts.append((0, w, "both" if half == 0 else "denominator"))
                        else:
                            parts.append((diag, w, "denominator"))
                            if diag > 0:
                                parts.append((0, diag, "both"))
                            parts.append((diag, diag + P, "masked"))
                        for lo, hi, what in parts:
                            if what == "masked":
                                pe.wait_ge(b_masked, masked_before(k + 1))
                            for g in range(4):
                                b, h = head_number(4 * G + g)
                                r = (4 * k + g) % NPT
                                v, width = V9[:, b * TB + j, h, :], 9
                                probs = PT[:, r, lo:hi]
                                if what == "denominator":
                                    v, width = ONE8, 32
                                elif what == "masked":
                                    v, width, probs = v[:, 0:DH], DH, MD[:, r, :]
                                ins = nc.tensor.matmul(PS[32 * g:32 * g + width, 7, lo:hi], v, probs,
                                                       start=(what == "denominator" and st in (0, TB)),
                                                       stop=(j == TB - 1), skip_group_check=True)
                        ins.then_inc(pv_done, 1)

            pe.wait_ge(early_loaded, 16)
            pe.wait_ge(consts_made, 3)
            for kind, ln, k in STAGES:
                norm_turned(ln, kind)
                if kind == "ffn0":
                    pe.wait_ge(ffn0_loaded, 16)
                if kind in ("ffn0", "ffn1"):
                    moe(kind, ln, k)
                elif kind == "lin":
                    linear(ln)
                else:
                    soft(ln)

        @block.scalar
        def _(act):
            stds = 0

            def std(c):
                nonlocal stds
                stds += 1
                act.wait_ge(var_ready, stds)
                r = RSTD[:, 4 * c:4 * c + 4]
                nc.scalar.activation(r, r, ACT.Sqrt).then_inc(std_ready, 1)

            def norm_turned(ln, after_soft):
                for c in range(T // 4):
                    if after_soft and c >= T // 8:
                        std(c)
                    if not after_soft or c >= T // 8:
                        std(c)
                    act.wait_ge(xt_turned, 4 * ln + c + 1)
                    nc.scalar.copy(XNT[:, c * 512:(c + 1) * 512], PS[:, c % 2, :]).then_inc(xt_copied, 1)

            def moe(kind, k):
                act.wait_ge(lg_ready, k + 1)
                nc.scalar.activation(EX[:, :, :], LG[:, :, :], ACT.Exp).then_inc(ex_ready, 1)
                chunks = chunks_of(kind)
                nb = before(k, len(chunks_of("ffn0")), len(chunks_of("ffn1")))

                def copy_turned(c):
                    a, b = chunks[c]
                    act.wait_ge(xs_turned, nb + c + 1)
                    nc.scalar.copy(XST[:, a * P:b * P], PS[:, c % 2, 0:(b - a) * P]).then_inc(xs_copied, 1)

                copy_turned(0)
                copy_turned(1)
                base = before(k, E, NT)
                if kind == "ffn0":
                    for e in range(E):
                        if e % 2 == 0 and e // 2 + 2 < len(chunks):
                            copy_turned(e // 2 + 2)
                        act.wait_ge(hid_done, base + e + 1)
                        if e >= 2:
                            act.wait_ge(eo_done, base + e - 1)
                        nc.scalar.activation(HG[:, e % 2, 0:CAP], PS[:, 4 + e % 2, 0:CAP], ACT.Relu,
                                             bias=col("f0_b1", e, 1)).then_inc(hid_active, 1)
                    return
                act.wait_ge(w_loaded, 16 * (E + 1))
                act.wait_ge(owner_ready, k - 1)

                def copy_w1(i):
                    owner = act.value_load(OWNERI[0:1, i:i + 1], min_val=0, max_val=E - 1)
                    if i >= 2:
                        act.wait_ge(hid_done, base + i - 1)
                    nc.scalar.copy(W1[:, i % 2, :], WT[:, bass.ds(owner * WB, F1)]).then_inc(w1_copied, 1)

                copy_w1(0)
                for i in range(NT):
                    if i + 1 < NT:
                        copy_w1(i + 1)
                    if i % 4 == 0 and i // 4 + 2 < len(chunks):
                        copy_turned(i // 4 + 2)
                    act.wait_ge(hid_biased, (k - 2) * NT + i + 1)
                    if i >= 2:
                        act.wait_ge(eo_done, base + i - 1)
                    nc.scalar.activation(HG[:, i % 2, :], HB[:, i % 2, :], ACT.Gelu).then_inc(hid_active, 1)

            def linear():
                for c in range(4):
                    act.wait_ge(g_done, c + 1)
                    nc.scalar.activation(GT[:, c * 512:(c + 1) * 512], PS[:, c, :], ACT.Sigmoid,
                                         bias=col("a0_bg")).then_inc(g_ready, 1)
                for n in range(8):
                    w = n % 2
                    scale = (1.0, QSCALE)[w]
                    act.wait_ge(qk_done, n + 1)
                    if n >= 2:
                        act.wait_ge(qk_ready, n - 1)
                    nc.scalar.activation(RL[:, n % 2, :], PS[:, 4 + n % 4, :], ACT.Relu,
                                         scale=scale).then_inc(relu_done, 1)
                    act.wait_ge(min_done, n + 1)
                    nc.scalar.activation(EXQ[:, n % 2, :], MN[:, n % 2, :], ACT.Exp,
                                         scale=scale).then_inc(exq_done, 1)

            def soft():
                act.wait_ge(v9_ones, 1)
                nc.scalar.activation(BQS[:, :], col("a1_bq"), ACT.Copy, scale=S ** -0.5).then_inc(act_step, 1)
                act.wait_ge(act_step, 1)
                for n in range(8):
                    c, w = 2 * (n // 4) + n % 2, n // 2 % 2
                    four = slice(c * 512, (c + 1) * 512)
                    act.wait_ge(proj_done, n + 1)
                    if n >= 2:
                        act.wait_ge(parts_done, n - 1)
                    nc.scalar.activation(QF[:, n % 2, :], PS[:, n % 4, :], ACT.Identity,
                                         bias=(BQS[:, :], col("a1_bk"))[w], scale=(S ** -0.5, 1.0)[w]).then_inc(qf_done, 1)
                    act.wait_ge(qf_done, n + 1)
                    nc.scalar.copy(PART[:, w, 0, four], QF[:, n % 2, :]).then_inc(part0_done, 1)
                for x in plan:
                    kind, k, i = x
                    if kind == "M":
                        act.wait_ge(m_turned, maxima_number[k, i] + 1)
                        before = rows_stored(k, i) - 16
                        if before:
                            act.wait_ge(m_rows[k % 4], before)
                        width = unit_columns(i)[1]
                        nc.scalar.copy(MT[0:width, k % 4, :],
                                       PS[0:width, 4 + ring_number[x] % NBB, 0:P // 2].bitcast(BF16)
                                       ).then_inc(m_copied, 1)
                    elif kind == "Z" and k in (2, 5):
                        std(0)
                        std(1)
                    elif kind == "B":
                        n = 4 * k + i
                        act.wait_ge(b_scores, n + 1)
                        if n == 0:
                            for b in range(B):
                                act.wait_ge(parts_stored[b], 6 * 16)
                        if k >= NPT // 4:
                            act.wait_ge(pv_done, k - NPT // 4 + 1)
                        w = columns(k)[0]
                        nc.scalar.activation(PT[:, n % NPT, 0:w], PS[:, 4 + ring_number[x] % NBB, 0:w], ACT.Exp).then_inc(b_exp, 1)
                    elif kind == "V" and k % NS in (TB - 1, NS - 1):
                        G, half = k // NS, int(k % NS == NS - 1)
                        act.wait_ge(pv_done, k + 1)
                        if G >= 2:
                            act.wait_ge(z_turned, 2 * (G // 2))
                        nc.scalar.copy(ZT[:, G % 2, half * 512:(half + 1) * 512], PS[:, 7, :]).then_inc(z_copied, 1)

            for kind, ln, k in STAGES:
                norm_turned(ln, ln == 5)
                if kind in ("ffn0", "ffn1"):
                    moe(kind, k)
                elif kind == "lin":
                    linear()
                else:
                    soft()

        @block.vector
        def _(dve):
            steps = [0]

            def link(ins):
                steps[0] += 1
                ins.then_inc(dve_step, 1)
                dve.wait_ge(dve_step, steps[0])

            stds = 0

            def stats(src, t):
                return nc.vector.bn_stats(STATS[:, t, :], src[:, t, :])

            def variances(c, last_stats):
                nonlocal stds
                link(last_stats)
                for t in range(4 * c, 4 * c + 4):
                    last = nc.vector.bn_aggr(MV[:, t, :], STATS[:, t, :])
                link(last)
                nc.vector.tensor_scalar(RSTD[:, 4 * c:4 * c + 4], MV[:, 4 * c:4 * c + 4, 1], EPS, None, ALU.add
                                        ).then_inc(var_ready, 1)
                stds += 1
                return stds

            def inverse(c, number):
                dve.wait_ge(std_ready, number)
                r = RSTD[:, 4 * c:4 * c + 4]
                link(nc.vector.reciprocal(r, r))

            def norm(c, last_stats):
                inverse(c, variances(c, last_stats))

            def write_xn(c):
                for t in range(4 * c, 4 * c + 4):
                    nc.vector.tensor_scalar(XN[:, t, :], X[:, t, :], MV[:, t, 0:1], RSTD[:, t:t + 1],
                                            ALU.subtract, ALU.mult).then_inc(xn_ready, 1)

            def normed(before_norm):
                for c in range(T // 8 if before_norm == after_soft else 0, T // 4):
                    norm(c, before_norm(c))
                    write_xn(c)

            def after_load(c):
                dve.wait_ge(x_loaded[c], 16)
                for t in range(4 * c, 4 * c + 4):
                    last = stats(X, t)
                return last

            def add_expert(k, t):
                dve.wait_ge(gathered[t], 16 * (k + 1))
                nc.vector.scalar_tensor_tensor(out=X[:, t, :], in0=YG[:, t, :], scalar=EFF[:, t:t + 1],
                                               in1=X[:, t, :], op0=ALU.mult, op1=ALU.add).then_inc(x_updated, 1)

            def after_moe(k, c):
                for t in range(4 * c, 4 * c + 4):
                    add_expert(k, t)
                    if t > 4 * c:
                        dve.wait_ge(x_updated, T * k + t)
                        stats(X, t - 1)
                dve.wait_ge(x_updated, T * k + t + 1)
                return stats(X, t)

            def after_linear(c):
                dve.wait_ge(lin_used, DH * (c // 2 + 1))
                xt = X[:, 4 * c:4 * c + 4, :]
                link(nc.vector.tensor_tensor(xt, xt, PS[:, 4 + c, :].rearrange("p (t d) -> p t d", t=4), ALU.add))
                for t in range(4 * c, 4 * c + 4):
                    last = stats(X, t)
                return last

            def attention_stats(c):
                four = slice(4 * c, 4 * c + 4)
                link(nc.vector.tensor_tensor(Z[:, four, :], Z[:, four, :], XN[:, four, :], ALU.add))
                for t in range(4 * c, 4 * c + 4):
                    last = stats(Z, t)
                return last

            def add_attention(c):
                four = slice(4 * c, 4 * c + 4)
                for t in range(4 * c, 4 * c + 4):
                    last = nc.vector.scalar_tensor_tensor(out=Z[:, t, :], in0=Z[:, t, :], scalar=MV[:, t, 0:1],
                                                          in1=col("a1_gamma"), op0=ALU.subtract, op1=ALU.mult)
                link(last)
                for t in range(4 * c, 4 * c + 4):
                    last = nc.vector.scalar_tensor_tensor(out=Z[:, t, :], in0=Z[:, t, :], scalar=RSTD[:, t:t + 1],
                                                          in1=col("a1_beta"), op0=ALU.mult, op1=ALU.add)
                link(last)
                link(nc.vector.tensor_tensor(X[:, four, :], X[:, four, :], Z[:, four, :], ALU.add))
                for t in range(4 * c, 4 * c + 4):
                    last = stats(X, t)
                return last

            def after_soft(c):
                dve.wait_ge(z_scaled, GR)
                norm(c, attention_stats(c))
                return add_attention(c)

            numbers = {}

            def first_batch(piece):
                if piece in (0, 1):
                    dve.wait_ge(z_scaled, GR // 2)
                    numbers[0, piece] = variances(piece, attention_stats(piece))
                elif piece in (3, 4):
                    inverse(piece - 3, numbers[0, piece - 3])
                    numbers[1, piece - 3] = variances(piece - 3, add_attention(piece - 3))
                elif piece in (6, 7):
                    inverse(piece - 6, numbers[1, piece - 6])
                    write_xn(piece - 6)

            def over_e(a):
                return a.rearrange("p (t e) -> p e t", e=E)

            def moe(kind, k):
                dve.wait_ge(logits_done, k + 1)
                logits = PS[:, 2, 0:T * E].rearrange("p (t e) -> p t e", e=E)
                if kind == "ffn0":
                    br = col("f0_br").unsqueeze(1).to_broadcast([P, T, E])
                    link(nc.vector.tensor_tensor(LG[:, :, :], logits, br, ALU.add))
                else:
                    link(nc.vector.tensor_copy(LG[:, :, :], logits))
                link(nc.vector.tensor_reduce(LMAX[:, :], LG[:, :, :], AX.X, ALU.max))
                nc.vector.tensor_tensor(LG[:, :, :], LG[:, :, :], LMAX[:, :].unsqueeze(2).to_broadcast([P, T, E]),
                                        ALU.subtract).then_inc(lg_ready, 1)
                dve.wait_ge(lg_ready, k + 1)
                link(nc.vector.tensor_scalar(HIT[:, :], LG[:, :, :].rearrange("p t e -> p (t e)"), -(2.0 ** -25), None,
                                             ALU.is_ge))
                link(nc.vector.tensor_tensor_scan(NTH[:, :], col("r8"), HIT[:, :], 0.0, ALU.mult, ALU.add))
                link(nc.vector.scalar_tensor_tensor(out=MASK[:, :, :], in0=over_e(NTH[:, :]), scalar=1.0,
                                                    in1=over_e(HIT[:, :]), op0=ALU.is_equal, op1=ALU.mult))
                nc.vector.tensor_copy(MASKB[:, :], MASK[:, :, :].rearrange("p e t -> p (e t)")
                                      ).then_inc(mask_ready, 1)
                dve.wait_ge(ex_ready, k + 1)
                link(nc.vector.tensor_reduce(SUM[:, :], EX[:, :, :], AX.X, ALU.add))
                link(nc.vector.reciprocal(GATE[:, :], SUM[:, :]))
                dve.wait_ge(counts_done, k + 1)
                within, total = PS[:, 3, 0:P], PS[:, 3, P:2 * P]
                link(nc.vector.tensor_tensor_scan(INCL[:, :], col("r16"), total, 0.0, ALU.mult, ALU.add))
                link(nc.vector.tensor_tensor(POS[:, :], INCL[:, :], total, ALU.subtract))
                link(nc.vector.tensor_tensor(POS[:, :], POS[:, :], within, ALU.add))
                pos = POS[:, :].rearrange("p (e t) -> p e t", e=E)
                by_t = PRD[:, :, :].rearrange("p e t -> p t e")
                if kind == "ffn0":
                    link(nc.vector.tensor_tensor(PRD[:, :, :], pos, MASK[:, :, :], ALU.mult))
                    link(nc.vector.tensor_reduce(PLACE[:, :], by_t, AX.X, ALU.add))
                    link(nc.vector.tensor_scalar(KEPT[:, :], PLACE[:, :], float(CAP), None, ALU.is_lt))
                    link(nc.vector.tensor_tensor(PRD[:, :, :], col("e256").rearrange("p (e t) -> p e t", e=E),
                                                 MASK[:, :, :], ALU.mult))
                    link(nc.vector.tensor_reduce(SLOT[:, :], by_t, AX.X, ALU.add))
                    link(nc.vector.tensor_tensor(SLOT[:, :], SLOT[:, :], PLACE[:, :], ALU.add))
                    link(nc.vector.tensor_scalar(SCAT[:, :], KEPT[:, :], -BIG, BIG, ALU.mult, ALU.add))
                    link(nc.vector.tensor_tensor(SCAT[:, :], SCAT[:, :], SLOT[:, :], ALU.add))
                    link(nc.vector.tensor_tensor(GATH[:, :], SLOT[:, :], KEPT[:, :], ALU.mult))
                    link(nc.vector.tensor_copy(GATHI[:, :], GATH[:, :]))
                    nc.vector.tensor_copy(SCATI[:, :], SCAT[:, :]).then_inc(index_ready, 1)
                    for t in range(T):
                        nc.vector.tensor_scalar(XG[:, t, :], XN[:, t, :], GATE[:, t:t + 1], None,
                                                ALU.mult).then_inc(xg_ready, 1)
                    link(nc.vector.scalar_tensor_tensor(out=EFF[:, :], in0=GATE[:, :], scalar=0.5, in1=KEPT[:, :],
                                                        op0=ALU.mult, op1=ALU.mult))
                else:
                    ends = INCL[:, :].rearrange("p (e t) -> p e t", e=E)[:, :, T - 1:T].to_broadcast([P, E, T])
                    link(nc.vector.tensor_tensor(CMP[:, :, :], ends, col("jt").rearrange("p (e t) -> p e t", e=E),
                                                 ALU.is_gt))
                    link(nc.vector.tensor_reduce(TILES[:, :], CMP[:, :, :], AX.X, ALU.add))
                    link(nc.vector.tensor_tensor_scan(ENDS[:, :], col("r16", 1, E), TILES[:, :], 0.0,
                                                      ALU.mult, ALU.add))
                    link(nc.vector.tensor_tensor(BASE[:, :], ENDS[:, :], TILES[:, :], ALU.subtract))
                    link(nc.vector.tensor_scalar(BASE[:, :], BASE[:, :], float(P), -1.0, ALU.mult, ALU.add))
                    link(nc.vector.tensor_tensor(PRD[:, :, :], pos, BASE[:, :].unsqueeze(2).to_broadcast([P, E, T]),
                                                 ALU.add))
                    link(nc.vector.tensor_tensor(PRD[:, :, :], PRD[:, :, :], MASK[:, :, :], ALU.mult))
                    link(nc.vector.tensor_reduce(SLOT[:, :], by_t, AX.X, ALU.add))
                    link(nc.vector.tensor_copy(GATHI[:, :], SLOT[:, :]))
                    nc.vector.tensor_copy(SCATI[:, :], SLOT[:, :]).then_inc(index_ready, 1)
                    link(nc.vector.tensor_tensor(CMP2[:, :, :], col("ti").rearrange("p (i e) -> p i e", e=E),
                                                 ENDS[:, :].unsqueeze(1).to_broadcast([P, NT, E]), ALU.is_ge))
                    link(nc.vector.tensor_reduce(OWNER[:, :], CMP2[:, :, :], AX.X, ALU.add))
                    nc.vector.tensor_scalar(OWNERI[:, :], OWNER[:, :], float(E - 1), None, ALU.min
                                            ).then_inc(owner_ready, 1)
                    link(nc.vector.tensor_scalar(EFF[:, :], GATE[:, :], 0.5, None, ALU.mult))

                base = before(k, E, NT)
                if kind == "ffn0":
                    for e in range(E):
                        dve.wait_ge(eo_done, base + e + 1)
                        nc.vector.tensor_tensor(
                            EO[:, 2 * e:2 * e + 2, :],
                            PS[:, 6 + e % 2, 0:2 * P].rearrange("p (s d) -> p s d", s=2),
                            col("f0_b2", e * P, P).unsqueeze(1).to_broadcast([P, 2, P]), ALU.add
                        ).then_inc(eo_copied, 1)
                else:
                    dve.wait_ge(w_loaded, 16 * (E + 1))
                    dve.wait_ge(owner_ready, k - 1)
                    owner = {}

                    def biased(i):
                        owner[i] = dve.value_load(OWNERI[0:1, i:i + 1], min_val=0, max_val=E - 1)
                        dve.wait_ge(hid_done, base + i + 1)
                        if i >= 2:
                            dve.wait_ge(hid_active, base + i - 1)
                        b1 = WT[:, bass.ds(owner[i] * WB + F1 + FB * P, FB)].unsqueeze(2).to_broadcast([P, FB, P])
                        nc.vector.tensor_tensor(HB[:, i % 2, :].rearrange("p (f n) -> p f n", f=FB),
                                                PS[:, 4 + i % 2, :].rearrange("p (f n) -> p f n", f=FB), b1,
                                                ALU.add).then_inc(hid_biased, 1)

                    biased(0)
                    for i in range(NT):
                        if i + 1 < NT:
                            biased(i + 1)
                        dve.wait_ge(eo_done, base + i + 1)
                        nc.vector.tensor_tensor(EO[:, i, :], PS[:, 6 + i % 2, 0:P], B2[:, bass.ds(owner[i] * P, P)],
                                                ALU.add).then_inc(eo_copied, 1)
            def linear():
                for n in range(8):
                    w, c = n % 2, n // 2
                    dve.wait_ge(qk_done, n + 1)
                    if n >= 2:
                        dve.wait_ge(exq_done, n - 1)
                    dve.wait_ge(relu_done, n + 1)
                    nc.vector.tensor_scalar(MN[:, n % 2, :], PS[:, 4 + n % 4, :], 0.0, None,
                                            ALU.min).then_inc(min_done, 1)
                    dve.wait_ge(exq_done, n + 1)
                    nc.vector.tensor_tensor((KT, QT)[w][:, c * 512:(c + 1) * 512], RL[:, n % 2, :], EXQ[:, n % 2, :],
                                            ALU.add).then_inc(qk_ready, 1)
                dve.wait_ge(qk_ready, 8)
                dve.wait_ge(g_ready, 4)
                for n in range(B * DH):
                    b, j = divmod(n, DH)
                    dve.wait_ge(v_done, n + 1)
                    if n >= 2:
                        dve.wait_ge(state_done, n - 1)
                    ps = PS[:, 2 * (n % 2):2 * (n % 2) + 2, :].rearrange("p c n -> p (c n)")
                    nc.vector.tensor_tensor(KV[:, n % 2, :], KT[:, b * S:(b + 1) * S], ps, ALU.mult
                                            ).then_inc(kv_done, 1)
                    dve.wait_ge(kv_done, n + 1)
                    if n >= 2:
                        dve.wait_ge(qs_done, n - 1)
                    nc.vector.tensor_tensor_scan(ST[:, n % 2, :], GT[:, b * S:(b + 1) * S], KV[:, n % 2, :], 0.0,
                                                 ALU.mult, ALU.add).then_inc(state_done, 1)

            def soft():
                for n in range(8):
                    c, w = 2 * (n // 4) + n % 2, n // 2 % 2
                    four = slice(c * 512, (c + 1) * 512)
                    dve.wait_ge(part0_done, n + 1)
                    link(nc.vector.tensor_tensor(RF[:, n % 2, :], QF[:, n % 2, :], PART[:, w, 0, four], ALU.subtract))
                    link(nc.vector.tensor_copy(PART[:, w, 1, four], RF[:, n % 2, :]))
                    nc.vector.tensor_tensor(PART[:, w, 2, four], RF[:, n % 2, :], PART[:, w, 1, four], ALU.subtract
                                            ).then_inc(parts_done, 1)
                dve.wait_ge(v9_ones, 1)
                for c in range(4):
                    dve.wait_ge(vproj_done, c + 1)
                    nc.vector.tensor_tensor(
                        V9[:, 4 * c:4 * c + 4, :, 0:DH],
                        PS[:, 4 + c, :].rearrange("p (t h j) -> p t h j", t=4, h=H),
                        col("a1_bv").rearrange("p (h j) -> p h j", h=H).unsqueeze(1).to_broadcast([P, 4, H, DH]),
                        ALU.add).then_inc(v9_ready, 1)
                z_steps = 0
                for x in plan:
                    kind, k, i = x
                    if kind == "A":
                        slot = 2 * (turn_number[x] % 2)
                        dve.wait_ge(a_scores, score_number[x] + 1)
                        if k >= 4 and i == 0:
                            dve.wait_ge(m_split, last_unit(k - 4) + 1)
                        nc.vector.tensor_reduce(NM[:, k % 4, i:i + 1],
                                                PS[:, slot:slot + 2, :].rearrange("p b n -> p (b n)"),
                                                AX.X, ALU.max, negate=True).then_inc(a_max, 1)
                    elif kind == "Z":
                        first_batch(k)
                    elif kind == "T":
                        slot = 2 * (turn_number[x] % 2)
                        dve.wait_ge(z_turned, 2 * k + i + 1)
                        tile0 = 4 * k
                        zz = Z[:, tile0:tile0 + 4, 64 * i:64 * i + 64].rearrange("p g (c j) -> p c g j", j=DH)
                        ps = PS[:, slot:slot + 2, :].rearrange("p b (c g w) -> p (b c) g w", g=4, w=32)
                        if 2 * k + i >= 1:
                            dve.wait_ge(z_scaled, 2 * k + i)
                        link(nc.vector.reciprocal(RD[:, :, :], ps[:, :, :, 8]))
                        nc.vector.tensor_tensor(zz, ps[:, :, :, 0:DH],
                                                RD[:, :, :].unsqueeze(3).to_broadcast([P, 8, 4, DH]),
                                                ALU.mult).then_inc(z_scaled, 1)

            dve.wait_ge(early_loaded, 16)
            nc.vector.tensor_copy(TRI[:, :], col("tri")).then_inc(consts_made, 1)
            nc.vector.tensor_copy(IDB[:, :], col("ident")).then_inc(consts_made, 1)
            nc.vector.memset(ONES[:, :], 1.0).then_inc(consts_made, 1)
            before_norm = after_load
            for kind, ln, k in STAGES:
                normed(before_norm)
                if ln == 0:
                    dve.wait_ge(ffn0_loaded, 16)
                if kind in ("ffn0", "ffn1"):
                    moe(kind, k)

                    def before_norm(c, k=k):
                        return after_moe(k, c)
                elif kind == "lin":
                    linear()
                    before_norm = after_linear
                else:
                    soft()
                    before_norm = after_soft
            for t in range(T):
                add_expert(3, t)

        @block.gpsimd
        def _(pool):
            def moe(kind, k):
                pool.wait_ge(index_ready, k + 1)
                src = XG if kind == "ffn0" else XN
                slots = tiles_of(kind) * P
                for t in range(T):
                    if kind == "ffn0":
                        pool.wait_ge(xg_ready, T * k + t + 1)
                    pool.indirect_dma_start(sx[0:slots, :], bass.IndirectOffsetOnAxis(ap=SCATI[:, t:t + 1], axis=0),
                                            src[:, t, :], None, bounds_check=slots - 1, oob_is_err=False
                                            ).then_inc(scattered, 16)
                pool.wait_ge(eo_stored, 16 * before(k + 1, E, NT))
                for t in range(T):
                    pool.indirect_dma_start(YG[:, t, :], None, sy[0:slots, :],
                                            bass.IndirectOffsetOnAxis(ap=GATHI[:, t:t + 1], axis=0),
                                            bounds_check=slots - 1, oob_is_err=False).then_inc(gathered[t], 16)

            def linear():
                pool.wait_ge(qk_ready, 8)
                for n in range(B * DH):
                    b = n // DH
                    pool.wait_ge(state_done, n + 1)
                    if n >= 2:
                        pool.wait_ge(lin_used, n - 1)
                    nc.gpsimd.tensor_tensor(QS[:, n % 2, :], QT[:, b * S:(b + 1) * S], ST[:, n % 2, :], ALU.mult
                                            ).then_inc(qs_done, 1)

            def soft():
                pool.wait_ge(x_updated, T * 3)
                nc.gpsimd.memset(V9[:, :, :, DH:DH + 1], 1.0).then_inc(v9_ones, 1)
                nc.gpsimd.memset(ONE8[:, :], 0.0).then_inc(pool_step, 1)
                pool.wait_ge(pool_step, 1)
                nc.gpsimd.memset(ONE8[:, DH:DH + 1], 1.0).then_inc(one8_made, 1)
                step = 1

                def then(ins):
                    nonlocal step
                    step += 1
                    ins.then_inc(pool_step, 1)
                    pool.wait_ge(pool_step, step)

                for x in plan:
                    kind, k, i = x
                    if kind == "S":
                        pool.wait_ge(a_max, last_scores[k, i] + 1)
                        if k >= 4:
                            pool.wait_ge(m_turned, last_unit(k - 4) + 1)
                        tiles, (at, width) = tiles_of_unit(i), unit_columns(i)
                        n = len(tiles)
                        nm, rest = NM[:, k % 4, tiles[0]:tiles[-1] + 1], NMR[:, k % 4, tiles[0]:tiles[-1] + 1]
                        m0, m1, m2 = (M3[:, k % 4, at + r * n:at + (r + 1) * n] for r in range(3))
                        then(nc.gpsimd.tensor_copy(m0, nm))
                        then(nc.gpsimd.tensor_tensor(rest, nm, m0, ALU.subtract))
                        then(nc.gpsimd.tensor_copy(m1, rest))
                        nc.gpsimd.tensor_tensor(m2, rest, m1, ALU.subtract).then_inc(m_split, 1)
                    if kind == "B":
                        _, diag = columns(k)
                        if diag is None:
                            continue
                        n = 4 * k + i
                        pool.wait_ge(b_exp, n + 1)
                        nc.gpsimd.affine_select(out=MD[:, n % NPT, :], in_=PT[:, n % NPT, diag:diag + P],
                                                compare_op=ALU.is_ge, fill=0.0, base=0, pattern=[[-1, P]],
                                                channel_multiplier=1).then_inc(b_masked, 1)

            nc.gpsimd.memset(ZERO[:, :], 0.0).then_inc(zero_made, 1)
            pool.wait_ge(zeroed, 16 * NT)
            for kind, ln, k in STAGES:
                if kind in ("ffn0", "ffn1"):
                    moe(kind, k)
                elif kind == "lin":
                    linear()
                else:
                    soft()


def kernel(**inputs):
    import numpy as np
    import concourse.bacc as _bacc
    from concourse.bass_utils import run_bass_kernel_spmd as _run

    g = {k: np.asarray(v) for k, v in inputs.items()}
    x = np.ascontiguousarray(g["L0_attn_x"].reshape(N, P))
    f = np.float32

    def rows(v):
        return np.broadcast_to(v.reshape(1, -1), (P, v.size))

    k, q = np.arange(P)[:, None], np.arange(P)[None, :]
    w1, w2 = g["L1_ffn_W1"], g["L1_ffn_W2"]
    part = {
        "ident": (k == q).astype(f), "tri": (k <= q).astype(f),
        "r8": rows((np.arange(P) % E != 0).astype(f)), "r16": rows((np.arange(P) % T != 0).astype(f)),
        "e256": rows((np.arange(P) // T * CAP).astype(f)), "jt": rows((np.arange(P) % T * P).astype(f)),
        "ti": rows((np.arange(NT * E) // E).astype(f)),
        "f0_wr": g["L0_ffn_Wr"], "f0_br": rows(g["L0_ffn_br"]), "f0_b1": g["L0_ffn_b1"].T,
        "f1_wr": g["L1_ffn_Wr"],
        "a0_bg": np.repeat(g["L0_attn_bg"], DH)[:, None],
        "a1_bq": g["L1_attn_bq"][:, None], "a1_bk": g["L1_attn_bk"][:, None],
        "f0_w1": g["L0_ffn_W1"].transpose(1, 0, 2).reshape(P, E * P),
        "f0_w2": g["L0_ffn_W2"].transpose(1, 0, 2).reshape(P, E * P),
        "f0_b2": rows(g["L0_ffn_b2"]),
        "a0_wq": g["L0_attn_Wq"].T, "a0_wk": g["L0_attn_Wk"].T,
        "a0_wg": np.repeat(g["L0_attn_Wg"].T, DH, axis=1),
        "a0_wv": np.repeat(g["L0_attn_Wv"].T.reshape(P, H, DH).transpose(0, 2, 1)[..., None], DH, axis=3).reshape(P, DH * P),
        "a0_wo": np.repeat(g["L0_attn_Wo"].T.reshape(H, 1, DH * P), DH, axis=1).reshape(P, DH * P),
        "a1_wq": g["L1_attn_Wq"].T, "a1_wk": g["L1_attn_Wk"].T, "a1_wv": g["L1_attn_Wv"].T,
        "a1_bv": rows(g["L1_attn_bv"]), "a1_gamma": rows(g["L1_attn_gamma"]), "a1_beta": rows(g["L1_attn_beta"]),
    }
    for name, (_, width) in COLS.items():
        assert part[name].shape == (P, width), (name, part[name].shape)
    params = np.ascontiguousarray(np.concatenate([part[name] for name in COLS], axis=1))
    pack = np.ascontiguousarray(np.concatenate([
        w1, w2.reshape(E, FB, P, P).transpose(0, 2, 1, 3).reshape(E, P, FB * P),
        g["L1_ffn_b1"].reshape(E, FB, P).transpose(0, 2, 1)], axis=2))
    b2 = np.ascontiguousarray(rows(g["L1_ffn_b2"]))

    nc = _bacc.Bacc("TRN2", target_bir_lowering=False, num_devices=1)
    arrays = {"x_dram": x, "params_dram": params, "pack_dram": pack, "b2_dram": b2}
    args = [nc.dram_tensor(n, a.shape, F32, kind="ExternalInput").ap() for n, a in arrays.items()]
    args.append(nc.dram_tensor("out_dram", (N, P), F32, kind="ExternalOutput").ap())
    macaron_kernel(nc, *args)
    r = _run(nc, [arrays], core_ids=[0])
    return r.results[0]["out_dram"].reshape(B, S, P)
```

```python
from contextlib import ExitStack

import concourse.bass as bass
from concourse import mybir

ALU = mybir.AluOpType
ACT = mybir.ActivationFunctionType
AX = mybir.AxisListType
F32 = mybir.dt.float32
BF16 = mybir.dt.bfloat16
U32 = mybir.dt.uint32
I32 = mybir.dt.int32

P = 128
B, S = 2, 1024
N = B * S
T = N // P
TB = S // P
E = 8
CAP = N // E
F1 = 512
FB = F1 // P
NT = T + E - 1
H, DH = 16, 8
EPS = 1e-5
QSCALE = DH ** -0.5
BIG = 65536.0
WB = F1 + FB * P + FB

SL = 8

NG = H // 4
GR = B * NG
PAIRS = 9
KQ = PAIRS * DH
MR = KQ
Q3R = 3
HQ = TB // 2
NPT = 12
SI = 1
MI = 3
LEAD = 0
VD = 1
VG = 2
NBB = 3
STEPS = [(0, j) for j in range(TB)] + [(1, j) for j in range(TB)]
NS = len(STEPS)
Z0 = 3
ZSTEPS = [GR // 2 * NS + Z0 + n for n in range(16)]

COLS = {}


def _columns():
    at = 0
    for name, width in (
        ("ident", P), ("tri", P), ("r8", P), ("r16", P), ("e256", P), ("jt", P), ("ti", NT * E), ("ids", T + 1),
        ("f0_wr", E), ("f0_br", E), ("f0_b1", E), ("f1_wr", E), ("a0_bg", 1), ("a1_bq", 1), ("a1_bk", 1),
        ("f0_w1", E * P), ("f0_w2", E * P), ("f0_b2", E * P),
        ("a0_wq", P), ("a0_wk", P), ("a0_wg", P), ("a0_wv", DH * P), ("a0_wo", P), ("hsum", 2 * 32),
        ("a1_wq", P), ("a1_wk", P), ("a1_wv", P), ("a1_bv", P), ("a1_gamma", P), ("a1_beta", P),
    ):
        COLS[name] = (at, width)
        at += width
    return at


NCOL = _columns()
EARLY = COLS["f0_w1"][0]
FFN0 = COLS["a0_wq"][0]


def head_of(group, g):
    u, ab = (group % NG) // 2, group % 2
    return 8 * u + 2 * g + ab


def units_of(group):
    return [(4 * group + g, h) for h in range(2) for g in range(4)]


def tiles_of_unit(h):
    return range(HQ * h, HQ * (h + 1))


def attention_turns():
    turns, last = [], None
    for hh, h in [x for G in range(GR) for x in units_of(G)]:
        for n, i in enumerate(tiles_of_unit(h)):
            turns.append(("A", hh, i))
            if n == SI and last:
                turns.append(("S", *last))
            if n == MI and last:
                turns.append(("M", *last))
        last = (hh, h)
    return turns + [("S", *last), ("M", *last)]


def attention_plan():
    turns = attention_turns()
    plan, at = [], 0
    ahead = turns.index(("M", 3, 0)) + 1 + LEAD
    rest = len(turns) - ahead
    while at < ahead:
        plan.append(turns[at])
        at += 1
    steps = GR * NS
    for m in range(steps):
        G, s = divmod(m, NS)
        for g in range(4):
            want = ahead + -(-rest * (4 * m + g + 1) // (4 * (steps - TB)))
            if g == 0 and s in (0, TB):
                want = max(want, turns.index(("M", 4 * G + 3, s // TB)) + 1 + LEAD)
            while at < min(want, len(turns)):
                plan.append(turns[at])
                at += 1
            plan.append(("B", m, g))
            if m >= VD and g == VG:
                plan.append(("V", m - VD, 0))
                if (m - VD + 1) % (2 * NS) == 0:
                    plan += [("T", (m - VD) // (2 * NS), 0), ("T", (m - VD) // (2 * NS), 1)]
        plan += [("Z", piece, 0) for piece in range(len(ZSTEPS)) if ZSTEPS[piece] == m]
    assert at == len(turns)
    for m in range(steps - VD, steps):
        plan.append(("V", m, 0))
    plan += [("T", GR // 2 - 1, 0), ("T", GR // 2 - 1, 1)]
    return plan


def macaron_kernel(nc, x_in, params, f1_pack, f1_b2, out):
    with ExitStack() as ctx:
        def sb(name, shape, dt=F32):
            return ctx.enter_context(nc.sbuf_tensor(name, shape, dt))

        def sem(name):
            return ctx.enter_context(nc.semaphore(name))

        X = sb("X", [P, T, P])
        XN = sb("XN", [P, T, P + 1])
        XNT = sb("XNT", [P, N])
        C = sb("C", [P, NCOL])
        TRI = sb("TRI", [P, P], BF16)
        ONES = sb("ONES", [P, P], BF16)
        IDB = sb("IDB", [P, P], BF16)
        STATS = sb("STATS", [P, T, 6])
        MV = sb("MV", [P, T, 2])
        RSTD = sb("RSTD", [P, T])
        EPS1 = sb("EPS1", [P, 1])
        FILL = sb("FILL", [P, P + 1])
        MT = sb("MT", [P, 4, P], BF16)
        B2 = sb("B2", [P, E * P])
        LG = sb("LG", [P, T, E])
        LMAX = sb("LMAX", [P, T])
        EX = sb("EX", [P, T, E])
        SUM = sb("SUM", [P, T])
        GATE = sb("GATE", [P, T])
        HIT = sb("HIT", [P, T * E])
        NTH = sb("NTH", [P, T * E])
        MASK = sb("MASK", [P, E, T])
        MASKB = sb("MASKB", [P, E * T], BF16)
        INCL = sb("INCL", [P, E * T])
        POS = sb("POS", [P, E * T])
        PRD = sb("PRD", [P, E, T])
        SLOT = sb("SLOT", [P, T])
        PLACE = sb("PLACE", [P, T])
        KEPT = sb("KEPT", [P, T])
        SCAT = sb("SCAT", [P, T])
        GATH = sb("GATH", [P, T])
        EFF = sb("EFF", [P, T])
        CMP = sb("CMP", [P, E, T])
        TILES = sb("TILES", [P, E])
        ENDS = sb("ENDS", [P, E])
        BASE = sb("BASE", [P, E])
        CMP2 = sb("CMP2", [P, NT, E])
        OWNER = sb("OWNER", [P, NT])
        OWNERI = sb("OWNERI", [P, NT], I32)
        SCATI = sb("SCATI", [P, T], U32)
        GATHI = sb("GATHI", [P, T], U32)

        ARENA = sb("ARENA", [P, 32768])

        class Carve:
            def __init__(self):
                self.at = 0

            def __call__(self, *shape):
                size = 1
                for s in shape:
                    size *= s
                a = ARENA[:, self.at:self.at + size]
                self.at += size
                assert self.at <= 32768
                return a

            def bf(self, size):
                a = ARENA[:, self.at:self.at + size // 2].bitcast(BF16)
                self.at += size // 2
                assert self.at <= 32768
                return a

        WEIGHTS = 32768 - E * WB
        WT = ARENA[:, WEIGHTS:WEIGHTS + E * WB]

        m = Carve()
        XG = m(T * P).rearrange("p (t d) -> p t d", t=T)
        YG = m(T * P).rearrange("p (t d) -> p t d", t=T)
        XS = m(NT * (P + 1)).rearrange("p (t d) -> p t d", t=NT)
        XST = m(NT * P)
        EO = m(NT * P).rearrange("p (t d) -> p t d", t=NT)
        HB = m(2 * F1).rearrange("p (r f) -> p r f", r=2)
        HG = m(2 * F1).rearrange("p (r f) -> p r f", r=2)
        W1 = m(2 * F1).rearrange("p (r f) -> p r f", r=2)
        assert m.at <= WEIGHTS

        m = Carve()
        KT = m(N)
        QT = m(N)
        GT = m(N)
        RL = m(2 * 512).rearrange("p (r n) -> p r n", r=2)
        EXQ = m(2 * 512).rearrange("p (r n) -> p r n", r=2)
        KV = m(2 * S).rearrange("p (r n) -> p r n", r=2)
        ST = m(2 * S).rearrange("p (r n) -> p r n", r=2)
        QS = m(8 * S).rearrange("p (r n) -> p r n", r=8)
        Y = m(2 * S).rearrange("p (b n) -> p b n", b=2)

        m = Carve()
        Q3 = m.bf(Q3R * 4 * S).rearrange("p (r g n) -> p r g n", r=Q3R, g=4)
        K3 = m.bf(Q3R * 4 * S).rearrange("p (r g n) -> p r g n", r=Q3R, g=4)
        SPLIT = m.at
        PT = m(NPT * 512).rearrange("p (r n) -> p r n", r=NPT)
        MD = m(NPT * P).rearrange("p (r n) -> p r n", r=NPT)
        ZT = m(2 * S).rearrange("p (r n) -> p r n", r=2)
        m.at = max(m.at, SPLIT + 2 * 1024 + 2 * 3 * N // 2)
        V9 = m(T * H * 9).rearrange("p (t h j) -> p t h j", t=T, h=H)
        BQS = m(1)
        ONE8 = m(32)
        NM = m(4 * TB).rearrange("p (r i) -> p r i", r=4)
        NMR = m(4 * TB).rearrange("p (r i) -> p r i", r=4)
        M3 = m.bf(4 * 3 * TB).rearrange("p (r c) -> p r c", r=4)
        RD = m(32).rearrange("p (c g) -> p c g", g=4)
        assert m.at <= WEIGHTS
        sp0 = ARENA[:, SPLIT:SPLIT + 2 * 1024 + 2 * 3 * N // 2]
        QF = sp0[:, 0:1024].rearrange("p (r n) -> p r n", r=2)
        RF = sp0[:, 1024:2048].rearrange("p (r n) -> p r n", r=2)
        PART = sp0[:, 2048:].bitcast(BF16).rearrange("p (w a n) -> p w a n", w=2, a=3)
        Z = XNT[:, :].rearrange("p (t d) -> p t d", t=T)

        PS = ctx.enter_context(nc.psum_tensor("PS", [P, 8, 512], F32))

        sx = [nc.dram_tensor("slots_x", [T * P, P], F32, kind="Internal").ap()] * 2
        sx += [nc.dram_tensor(f"slots_x{k}", [NT * P, P + 1], F32, kind="Internal").ap() for k in (2, 3)]
        sy = nc.dram_tensor("slots_y", [T * P, P], F32, kind="Internal").ap()
        ty = nc.dram_tensor("tokens_y", [N, P], F32, kind="Internal").ap()
        qd = nc.dram_tensor("q_parts", [H, 3, DH, N], BF16, kind="Internal").ap()
        kd = nc.dram_tensor("k_parts", [H, 3, DH, N], BF16, kind="Internal").ap()

        def col(name, k=None, n=None):
            at, width = COLS[name]
            if k is None:
                return C[:, at:at + width]
            return C[:, at + k:at + k + n]

        x_loaded = [sem(f"x_loaded{c}") for c in range(4)]
        early_loaded = sem("early_loaded")
        ffn0_loaded = sem("ffn0_loaded")
        rest_loaded = sem("rest_loaded")
        consts_made = sem("consts_made")
        fill_made = sem("fill_made")
        eps_made = sem("eps_made")
        ids_made = sem("ids_made")
        slots_filled = [sem(f"slots_filled{k}") for k in range(4)]
        y_loaded = [sem(f"y_loaded{c}") for c in range(4)]
        y_scattered = sem("y_scattered")
        dve_step = sem("dve_step")
        pool_step = sem("pool_step")
        act_step = sem("act_step")
        var_ready = sem("var_ready")
        std_ready = sem("std_ready")
        xn_ready = sem("xn_ready")
        xt_turned = sem("xt_turned")
        xt_copied = sem("xt_copied")
        logits_done = sem("logits_done")
        lg_ready = sem("lg_ready")
        ex_ready = sem("ex_ready")
        mask_ready = sem("mask_ready")
        counts_done = sem("counts_done")
        index_ready = sem("index_ready")
        gath_ready = sem("gath_ready")
        owner_ready = sem("owner_ready")
        xg_ready = sem("xg_ready")
        scattered = sem("scattered")
        xs_loaded = [sem(f"xs_loaded{k}") for k in range(6)]
        xs_turned = sem("xs_turned")
        xs_copied = sem("xs_copied")
        hid_done = sem("hid_done")
        hid_biased = sem("hid_biased")
        hid_active = sem("hid_active")
        eo_done = sem("eo_done")
        eo_copied = sem("eo_copied")
        eo_stored = sem("eo_stored")
        w_loaded = sem("w_loaded")
        w1_copied = sem("w1_copied")
        gathered = [sem(f"gathered{k}") for k in range(T)]
        x_updated = sem("x_updated")
        g_done = sem("g_done")
        g_ready = sem("g_ready")
        qk_done = sem("qk_done")
        exq_done = sem("exq_done")
        qk_ready = sem("qk_ready")
        v_done = sem("v_done")
        kv_done = sem("kv_done")
        state_done = sem("state_done")
        qs_done = sem("qs_done")
        sums_done = sem("sums_done")
        y_copied = sem("y_copied")
        lin_done = sem("lin_done")
        proj_done = sem("proj_done")
        qf_done = sem("qf_done")
        part0_done = sem("part0_done")
        parts_done = sem("parts_done")
        parts_stored = [sem(f"parts_stored{b}") for b in range(B)]
        vproj_done = sem("vproj_done")
        v9_ones = sem("v9_ones")
        v9_ready = sem("v9_ready")
        ones_loaded = sem("ones_loaded")
        one8_made = sem("one8_made")
        ring_loaded = [sem(f"ring_loaded{k}") for k in range(Q3R)]
        a_scores = sem("a_scores")
        a_max = sem("a_max")
        m_split = sem("m_split")
        m_turned = sem("m_turned")
        m_copied = sem("m_copied")
        m_rows = [sem(f"m_rows{k}") for k in range(4)]
        b_scores = sem("b_scores")
        b_exp = sem("b_exp")
        b_masked = sem("b_masked")
        pv_done = sem("pv_done")
        z_copied = sem("z_copied")
        z_turned = sem("z_turned")
        z_scaled = sem("z_scaled")
        out_stored = sem("out_stored")

        x_rows = x_in.rearrange("(t p) d -> p t d", p=P)
        out_rows = out.rearrange("(t p) d -> p t d", p=P)
        sx_rows = [a.rearrange("(t p) d -> p t d", p=P) for a in sx]
        ty_rows = ty.rearrange("(t p) d -> p t d", p=P)
        sy_rows = sy.rearrange("(t p) d -> p t d", p=P)

        STAGES = (("ffn0", 0, 0), ("lin", 1, None), ("ffn0", 2, 1), ("ffn1", 3, 2), ("soft", 4, None), ("ffn1", 5, 3))

        def tiles_of(kind):
            return T if kind == "ffn0" else NT

        def chunks_of(kind):
            n = tiles_of(kind)
            return [(a, min(a + 4, n)) for a in range(0, n, 4)]

        def before(k, per0, per1):
            return min(k, 2) * per0 + max(k - 2, 0) * per1

        plan = attention_plan()
        turns = [x for x in plan if x[0] in "AT"]
        ring = [x for x in plan if x[0] in "BM"]
        ring_number = {x: n for n, x in enumerate(ring)}
        scores = [x for x in turns if x[0] == "A"]
        score_number = {x: n for n, x in enumerate(scores)}
        maxima = [x[1:] for x in plan if x[0] == "M"]
        maxima_number = {x: n for n, x in enumerate(maxima)}
        last_scores = {}
        for hh, h in maxima:
            last_scores[hh, h] = score_number["A", hh, tiles_of_unit(h)[-1]]

        def last_unit(hh):
            return max(n for n, x in enumerate(maxima) if x[0] == hh)

        def rows_stored(hh, h):
            return 16 * sum(x[0] % 4 == hh % 4 for x in maxima[:maxima_number[hh, h] + 1])
        turn_number = {x: n for n, x in enumerate(turns)}

        def columns(m):
            half, j = STEPS[m % NS]
            if half == 0:
                return 4 * P, (P * j if j < HQ else None)
            return 4 * P, (P * (j - HQ) if j >= HQ else None)

        def unit_columns(h):
            return 3 * HQ * h, 3 * HQ

        def masked_before(m):
            return 4 * (2 * HQ * (m // NS) + sum(columns(k)[1] is not None for k in range(m % NS)))

        def head_number(hh):
            G, g = divmod(hh, 4)
            return G // NG, head_of(G, g)

        block = ctx.enter_context(nc.Block())

        @block.sync
        def _(sp):
            for a in range(0, T, 4):
                sp.dma_start(X[:, a:a + 4, :], x_rows[:, a:a + 4, :]).then_inc(x_loaded[a // 4], 16)
            sp.wait_ge(x_loaded[3], 16)
            sp.dma_start(C[:, EARLY:FFN0], params[:, EARLY:FFN0]).then_inc(ffn0_loaded, 16)
            sp.wait_ge(fill_made, 2)
            for k, n, width in ((0, T, P), (2, NT, P + 1), (3, NT, P + 1)):
                sp.dma_start(sx_rows[k], FILL[:, 0:width].unsqueeze(1).to_broadcast([P, n, width])
                             ).then_inc(slots_filled[k], 16)
            sp.dma_start(C[:, FFN0:NCOL], params[:, FFN0:NCOL]).then_inc(rest_loaded, 16)
            for e in range(E):
                sp.dma_start(WT[:, e * WB:(e + 1) * WB], f1_pack[e]).then_inc(w_loaded, 16)
            sp.dma_start(B2[:, :], f1_b2[:, :]).then_inc(w_loaded, 16)

            def moe(kind, k):
                sp.wait_ge(scattered, 16 * T * (k + 1))
                for c, (a, b) in enumerate(chunks_of(kind)):
                    width = P if kind == "ffn0" else P + 1
                    sp.dma_start(XS[:, a:b, 0:width], sx_rows[k][:, a:b, :]).then_inc(xs_loaded[c], 16)
                if kind == "ffn0":
                    for e in range(E):
                        sp.wait_ge(eo_copied, before(k, E, NT) + e + 1)
                        sp.dma_start(sy_rows[:, 2 * e:2 * e + 2, :], EO[:, 2 * e:2 * e + 2, :]).then_inc(eo_stored, 16)
                    return
                sp.wait_ge(y_scattered, 16 * NT * (k - 1))
                for c in range(T // 4):
                    sp.dma_start(YG[:, 4 * c:4 * c + 4, :], ty_rows[:, 4 * c:4 * c + 4, :]).then_inc(y_loaded[c], 16)

            def soft():
                def store_parts(b, w):
                    sp.wait_ge(parts_done, 2 * (2 * b + w + 1))
                    half = slice(b * S, (b + 1) * S)
                    for a in range(3):
                        sp.dma_start((qd, kd)[w][:, a, :, half], PART[:, w, a, half]).then_inc(parts_stored[b], 16)

                def load_group(G):
                    sp.wait_ge(parts_stored[G // NG], 6 * 16)
                    b, ring = G // NG, G % Q3R
                    u, ab = (G % NG) // 2, G % 2
                    heads = slice(8 * u + ab, 8 * u + ab + 7, 2)
                    for c in range(3):
                        row = 3 * DH * c
                        q = qd[heads, :, :, b * S:(b + 1) * S].rearrange("g a d n -> (a d) g n")
                        sp.dma_start(Q3[row:row + 3 * DH, ring, :, :], q).then_inc(ring_loaded[ring], 16)
                        k = kd[heads, c, :, b * S:(b + 1) * S].rearrange("g d n -> d g n")
                        for a in range(3):
                            sp.dma_start(K3[row + DH * a:row + DH * (a + 1), ring, :, :], k
                                         ).then_inc(ring_loaded[ring], 16)

                store_parts(0, 0)
                store_parts(0, 1)
                load_group(0)
                for r in range(3):
                    sp.dma_start(K3[MR + r:MR + r + 1, :, :, :].rearrange("o r g n -> o (r g n)"),
                                 ONES[0:Q3R * 4 * S // P, :]).then_inc(ones_loaded, 16)
                store_parts(1, 0)
                store_parts(1, 1)
                for G in range(1, Q3R):
                    load_group(G)
                for x in plan:
                    if x[0] == "M":
                        _, hh, h = x
                        G, g = divmod(hh, 4)
                        tiles = tiles_of_unit(h)
                        sp.wait_ge(m_copied, maxima_number[hh, h] + 1)
                        sp.dma_start(Q3[MR:MR + 3, G % Q3R, g, tiles[0] * P:(tiles[-1] + 1) * P],
                                     MT[0:3 * len(tiles), hh % 4, :]).then_inc(m_rows[hh % 4], 16)
                    if x[0] == "V" and x[1] % NS == NS - 1:
                        G = x[1] // NS
                        if G + Q3R < GR:
                            sp.wait_ge(pv_done, NS * (G + 1))
                            load_group(G + Q3R)

            for kind, ln, k in STAGES:
                if kind in ("ffn0", "ffn1"):
                    moe(kind, k)
                elif kind == "soft":
                    soft()
            for t in range(0, T, 4):
                sp.wait_ge(x_updated, T * 3 + t + 4)
                sp.dma_start(out_rows[:, t:t + 4, :], X[:, t:t + 4, :]).then_inc(out_stored, 16)
            sp.wait_ge(out_stored, 16 * T // 4)

        @block.tensor
        def _(pe):
            ident = col("ident")

            def norm_turned(ln, kind):
                wr = col("f0_wr" if kind == "ffn0" else "f1_wr")

                def logits(c):
                    pe.wait_ge(xt_copied, 4 * ln + c + 1)
                    for t in range(4 * c, 4 * c + 4):
                        i = nc.tensor.matmul(PS[:, 2, t * E:(t + 1) * E], XNT[:, t * P:(t + 1) * P], wr,
                                             start=True, stop=True)
                    return i

                def gates(c):
                    pe.wait_ge(rest_loaded, 16)
                    pe.wait_ge(xt_copied, 4 * ln + c + 1)
                    nc.tensor.matmul(PS[:, 4 + c, :], col("a0_wg"), XNT[:, c * 512:(c + 1) * 512],
                                     start=True, stop=True).then_inc(g_done, 1)

                if ln == 5:
                    pe.wait_ge(z_scaled, GR)
                for c in range(T // 4):
                    pe.wait_ge(xn_ready, T * ln + 4 * c + 4)
                    if 4 * ln + c >= 2:
                        pe.wait_ge(xt_copied, 4 * ln + c - 1)
                    for t in range(4 * c, 4 * c + 4):
                        i = nc.tensor.transpose(PS[:, c % 2, (t % 4) * P:(t % 4 + 1) * P], XN[:, t, 0:P], ident)
                    i.then_inc(xt_turned, 1)
                    if kind in ("ffn0", "ffn1") and c >= 1:
                        logits(c - 1)
                    if kind == "lin" and c >= 1:
                        gates(c - 1)
                if kind == "lin":
                    gates(T // 4 - 1)
                if kind in ("ffn0", "ffn1"):
                    logits(T // 4 - 1).then_inc(logits_done, 1)

            def moe(kind, ln, k):
                pe.wait_ge(mask_ready, k + 1)
                nc.tensor.matmul(PS[:, 3, 0:P], TRI[:, :], MASKB[:, :], start=True, stop=True)
                nc.tensor.matmul(PS[:, 3, P:2 * P], ONES[:, :], MASKB[:, :], start=True,
                                 stop=True).then_inc(counts_done, 1)

                chunks = chunks_of(kind)
                nb = before(k, len(chunks_of("ffn0")), len(chunks_of("ffn1")))

                def turn(c):
                    a, b = chunks[c]
                    pe.wait_ge(xs_loaded[c], 16 * (k + 1 if c < 4 else k - 1))
                    if c >= 2:
                        pe.wait_ge(xs_copied, nb + c - 1)
                    for t in range(a, b):
                        i = nc.tensor.transpose(PS[:, c % 2, (t - a) * P:(t - a + 1) * P], XS[:, t, 0:P], ident)
                    i.then_inc(xs_turned, 1)

                base = before(k, E, NT)
                if kind == "ffn0":
                    pe.wait_ge(ffn0_loaded, 16)
                    w1, w2 = col("f0_w1"), col("f0_w2")

                    def up(e):
                        pe.wait_ge(xs_copied, nb + e // 2 + 1)
                        if e >= 2:
                            pe.wait_ge(hid_active, base + e - 1)
                        nc.tensor.matmul(PS[:, 4 + e % 2, 0:CAP], w1[:, e * P:(e + 1) * P],
                                         XST[:, e * CAP:(e + 1) * CAP], start=True, stop=True).then_inc(hid_done, 1)

                    def down(e):
                        pe.wait_ge(hid_active, base + e + 1)
                        if e >= 2:
                            pe.wait_ge(eo_copied, base + e - 1)
                        for s in range(2):
                            i = nc.tensor.matmul(PS[:, 6 + e % 2, s * P:(s + 1) * P],
                                                 HG[:, e % 2, s * P:(s + 1) * P],
                                                 w2[:, e * P:(e + 1) * P], start=True, stop=True)
                        i.then_inc(eo_done, 1)

                    turn(0)
                    turn(1)
                    for e in range(E):
                        if e % 2 == 0 and e // 2 + 2 < len(chunks):
                            turn(e // 2 + 2)
                        up(e)
                        if e >= 1:
                            down(e - 1)
                    down(E - 1)
                    return

                pe.wait_ge(w_loaded, 16 * (E + 1))
                pe.wait_ge(owner_ready, k - 1)
                owner = {}

                def up1(i):
                    n = (k - 2) * NT + i
                    owner[i] = pe.value_load(OWNERI[0:1, i:i + 1], min_val=0, max_val=E - 1)
                    pe.wait_ge(xs_copied, nb + i // 4 + 1)
                    pe.wait_ge(w1_copied, n + 1)
                    if i >= 2:
                        pe.wait_ge(hid_biased, n - 1)
                    for f in range(FB):
                        ins = nc.tensor.matmul(PS[:, 4 + i % 2, f * P:(f + 1) * P],
                                               W1[:, i % 2, f * P:(f + 1) * P],
                                               XST[:, i * P:(i + 1) * P], start=True, stop=True)
                    ins.then_inc(hid_done, 1)

                def down1(i):
                    pe.wait_ge(hid_active, base + i + 1)
                    if i >= 2:
                        pe.wait_ge(eo_copied, base + i - 1)
                    o = PS[:, 6 + i % 2, 0:P]
                    for f in range(FB):
                        ins = nc.tensor.matmul(o, HG[:, i % 2, f * P:(f + 1) * P],
                                               WT[:, bass.ds(owner[i] * WB + F1 + f * P, P)], start=(f == 0),
                                               stop=(f == FB - 1))
                    ins.then_inc(eo_done, 1)

                turn(0)
                turn(1)
                for i in range(NT):
                    if i % 4 == 0 and i // 4 + 2 < len(chunks):
                        turn(i // 4 + 2)
                    up1(i)
                    if i >= 1:
                        down1(i - 1)
                down1(NT - 1)

            def linear(ln):
                pe.wait_ge(xt_copied, 4 * ln + 4)
                pe.wait_ge(rest_loaded, 16)

                def features(n):
                    w, c = n % 2, n // 2
                    if n >= 4:
                        pe.wait_ge(g_ready, n - 3)
                    bank = (2, 3, 0, 1, 4, 5, 6, 7)[n]
                    nc.tensor.matmul(PS[:, bank, :], col(("a0_wk", "a0_wq")[w]),
                                     XNT[:, c * 512:(c + 1) * 512], start=True, stop=True).then_inc(qk_done, 1)

                def values(n):
                    b, j = divmod(n, DH)
                    if n >= 2:
                        pe.wait_ge(kv_done, n - 1)
                    else:
                        pe.wait_ge(exq_done, 4)
                    for c in range(2):
                        i = nc.tensor.matmul(PS[:, 2 * (n % 2) + c, :], col("a0_wv", j * P, P),
                                             XNT[:, b * S + c * 512:b * S + (c + 1) * 512], start=True, stop=True)
                    i.then_inc(v_done, 1)

                def sums(n):
                    b, r = divmod(n, 2)
                    pe.wait_ge(exq_done, 8)
                    pe.wait_ge(qs_done, 4 * (n + 1))
                    for c in range(2):
                        for q in range(4):
                            i = nc.tensor.matmul(PS[32 * q:32 * q + 32, 4 + 2 * b + c, :], col("hsum", 32 * r, 32),
                                                 QS[:, (4 * n + q) % 8, c * 512:(c + 1) * 512],
                                                 start=(r == 0), stop=(r == 1), skip_group_check=True)
                    i.then_inc(sums_done, 1)

                def project(b):
                    pe.wait_ge(y_copied, 2 * (b + 1))
                    for c in range(2):
                        for t in range(4 * c, 4 * c + 4):
                            i = nc.tensor.matmul(PS[:, 4 + 2 * b + c, (t % 4) * P:(t % 4 + 1) * P],
                                                 Y[:, b, t * P:(t + 1) * P], col("a0_wo"), start=True, stop=True)
                        i.then_inc(lin_done, 1)

                for n in range(8):
                    features(n)
                for n in range(B * DH):
                    values(n)
                    if n >= SL and (n - SL) % 4 == 0:
                        sums((n - SL) // 4)
                        if n - SL == 4:
                            project(0)
                for n in range((B * DH - 1 - SL) // 4 + 1, B * DH // 4):
                    sums(n)
                project(1)

            def soft(ln):
                pe.wait_ge(xt_copied, 4 * ln + 4)
                for n in range(8):
                    c, w = 2 * (n // 4) + n % 2, n // 2 % 2
                    if n >= 4:
                        pe.wait_ge(qf_done, n - 3)
                    nc.tensor.matmul(PS[:, n % 4, :], col(("a1_wq", "a1_wk")[w]),
                                     XNT[:, c * 512:(c + 1) * 512], start=True, stop=True).then_inc(proj_done, 1)
                for c in range(4):
                    for t in range(4 * c, 4 * c + 4):
                        i = nc.tensor.matmul(PS[:, 4 + c, (t % 4) * P:(t % 4 + 1) * P],
                                             XNT[:, t * P:(t + 1) * P], col("a1_wv"), start=True, stop=True)
                    i.then_inc(vproj_done, 1)
                pe.wait_ge(qf_done, 8)
                pe.wait_ge(one8_made, 1)

                def wait_slot(n):
                    if n < 2:
                        return
                    kind, k, i = turns[n - 2]
                    if kind == "A":
                        pe.wait_ge(a_max, score_number["A", k, i] + 1)
                    else:
                        pe.wait_ge(z_scaled, 2 * k + i + 1)

                def wait_ring(x):
                    n = ring_number[x]
                    if n < NBB:
                        return
                    kind, k, i = ring[n - NBB]
                    if kind == "M":
                        pe.wait_ge(m_copied, maxima_number[k, i] + 1)
                    else:
                        pe.wait_ge(b_exp, 4 * k + i + 1)

                begun = set()
                pe.wait_ge(v9_ready, 4)
                for x in plan:
                    kind, k, i = x
                    if kind in "AT":
                        n = turn_number[x]
                        slot = 2 * (n % 2)
                        wait_slot(n)
                    elif kind in "BM":
                        bank = 4 + ring_number[x] % NBB
                        wait_ring(x)
                    if kind == "A":
                        G, g = divmod(k, 4)
                        if G not in begun:
                            begun.add(G)
                            pe.wait_ge(ring_loaded[G % Q3R], 16 * 12 * (G // Q3R + 1))
                        for c in range(2):
                            ins = nc.tensor.matmul(PS[:, slot + c, :], Q3[0:KQ, G % Q3R, g, i * P:(i + 1) * P],
                                                   K3[0:KQ, G % Q3R, g, c * 512:(c + 1) * 512],
                                                   start=True, stop=True)
                        ins.then_inc(a_scores, 1)
                    elif kind == "M":
                        pe.wait_ge(m_split, maxima_number[k, i] + 1)
                        at, width = unit_columns(i)
                        o = PS[0:width, bank, 0:P // 2].bitcast(BF16)
                        nc.tensor.transpose(o, M3[:, k % 4, at:at + width], IDB[:, :]).then_inc(m_turned, 1)
                    elif kind == "T":
                        pe.wait_ge(z_copied, 4 * (k + 1))
                        for c in range(8 * i, 8 * i + 8):
                            src = ZT[:, :, :].rearrange("p a (r c) -> p c a r", c=16)[:, c]
                            ins = nc.tensor.transpose(PS[:, slot + (c % 8) // 4, (c % 4) * P:(c % 4 + 1) * P],
                                                      src, ident)
                        ins.then_inc(z_turned, 1)
                    elif kind == "B":
                        G, st = divmod(k, NS)
                        half, j = STEPS[st]
                        if st in (0, TB):
                            pe.wait_ge(m_rows[i], rows_stored(4 * G + i, half))
                        if k == 0:
                            pe.wait_ge(ones_loaded, 48)
                        w = columns(k)[0]
                        nc.tensor.matmul(PS[:, bank, 0:w], K3[0:MR + 3, G % Q3R, i, j * P:(j + 1) * P],
                                         Q3[0:MR + 3, G % Q3R, i, half * 512:half * 512 + w], start=True, stop=True
                                         ).then_inc(b_scores, 1)
                    elif kind == "V":
                        G, st = divmod(k, NS)
                        half, j = STEPS[st]
                        w, diag = columns(k)
                        if st in (0, TB) and 2 * G + half >= 1:
                            pe.wait_ge(z_copied, 2 * G + half)
                        pe.wait_ge(b_exp, 4 * (k + 1))
                        parts = []
                        if diag is None:
                            parts.append((0, w, "both" if half == 0 else "denominator"))
                        else:
                            parts.append((diag, w, "denominator"))
                            if diag > 0:
                                parts.append((0, diag, "both"))
                            parts.append((diag, diag + P, "masked"))
                        for lo, hi, what in parts:
                            if what == "masked":
                                pe.wait_ge(b_masked, masked_before(k + 1))
                            for g in range(4):
                                b, h = head_number(4 * G + g)
                                r = (4 * k + g) % NPT
                                v, width = V9[:, b * TB + j, h, :], 9
                                probs = PT[:, r, lo:hi]
                                if what == "denominator":
                                    v, width = ONE8, 32
                                elif what == "masked":
                                    v, width, probs = v[:, 0:DH], DH, MD[:, r, :]
                                ins = nc.tensor.matmul(PS[32 * g:32 * g + width, 7, lo:hi], v, probs,
                                                       start=(what == "denominator" and st in (0, TB)),
                                                       stop=(j == TB - 1), skip_group_check=True)
                        ins.then_inc(pv_done, 1)

            pe.wait_ge(early_loaded, 16)
            pe.wait_ge(consts_made, 3)
            for kind, ln, k in STAGES:
                norm_turned(ln, kind)
                if kind in ("ffn0", "ffn1"):
                    moe(kind, ln, k)
                elif kind == "lin":
                    linear(ln)
                else:
                    soft(ln)

        @block.scalar
        def _(act):
            act.dma_start(C[:, 0:EARLY], params[:, 0:EARLY]).then_inc(early_loaded, 16)
            act.wait_ge(eps_made, 1)

            stds = 0

            def std(c):
                nonlocal stds
                stds += 1
                act.wait_ge(var_ready, stds)
                nc.scalar.activation(RSTD[:, 4 * c:4 * c + 4], MV[:, 4 * c:4 * c + 4, 1], ACT.Sqrt,
                                     bias=EPS1[:, :]).then_inc(std_ready, 1)

            def copy_y(b):
                act.wait_ge(sums_done, 2 * (b + 1))
                for c in range(2):
                    nc.scalar.copy(Y[:, b, c * 512:(c + 1) * 512], PS[:, 4 + 2 * b + c, :]).then_inc(y_copied, 1)

            def norm_turned(ln, after_soft):
                ahead = ln in (0, 2, 4)
                if ahead:
                    std(0)
                for c in range(T // 4):
                    if ahead and c + 1 < T // 4:
                        std(c + 1)
                    if ln == 2 and c == 0:
                        copy_y(1)
                    if after_soft and c >= T // 8:
                        std(c)
                    if not ahead and (not after_soft or c >= T // 8):
                        std(c)
                    act.wait_ge(xt_turned, 4 * ln + c + 1)
                    nc.scalar.copy(XNT[:, c * 512:(c + 1) * 512], PS[:, c % 2, :]).then_inc(xt_copied, 1)

            def moe(kind, k):
                act.wait_ge(lg_ready, k + 1)
                nc.scalar.activation(EX[:, :, :], LG[:, :, :], ACT.Exp).then_inc(ex_ready, 1)
                chunks = chunks_of(kind)
                nb = before(k, len(chunks_of("ffn0")), len(chunks_of("ffn1")))

                def copy_turned(c):
                    a, b = chunks[c]
                    act.wait_ge(xs_turned, nb + c + 1)
                    nc.scalar.copy(XST[:, a * P:b * P], PS[:, c % 2, 0:(b - a) * P]).then_inc(xs_copied, 1)

                copy_turned(0)
                copy_turned(1)
                base = before(k, E, NT)
                if kind == "ffn0":
                    for e in range(E):
                        if e % 2 == 0 and e // 2 + 2 < len(chunks):
                            copy_turned(e // 2 + 2)
                        act.wait_ge(hid_done, base + e + 1)
                        if e >= 2:
                            act.wait_ge(eo_done, base + e - 1)
                        nc.scalar.activation(HG[:, e % 2, 0:CAP], PS[:, 4 + e % 2, 0:CAP], ACT.Relu,
                                             bias=col("f0_b1", e, 1)).then_inc(hid_active, 1)
                    return
                act.wait_ge(w_loaded, 16 * (E + 1))
                act.wait_ge(owner_ready, k - 1)

                def copy_w1(i):
                    owner = act.value_load(OWNERI[0:1, i:i + 1], min_val=0, max_val=E - 1)
                    if i >= 2:
                        act.wait_ge(hid_done, base + i - 1)
                    nc.scalar.copy(W1[:, i % 2, :], WT[:, bass.ds(owner * WB, F1)]).then_inc(w1_copied, 1)

                copy_w1(0)
                for i in range(NT):
                    if i + 1 < NT:
                        copy_w1(i + 1)
                    if i % 4 == 0 and i // 4 + 2 < len(chunks):
                        copy_turned(i // 4 + 2)
                    act.wait_ge(hid_biased, (k - 2) * NT + i + 1)
                    if i >= 2:
                        act.wait_ge(eo_done, base + i - 1)
                    nc.scalar.activation(HG[:, i % 2, :], HB[:, i % 2, :], ACT.Gelu).then_inc(hid_active, 1)

            def linear():
                for c in range(4):
                    act.wait_ge(g_done, c + 1)
                    nc.scalar.activation(GT[:, c * 512:(c + 1) * 512], PS[:, 4 + c, :], ACT.Sigmoid,
                                         bias=col("a0_bg")).then_inc(g_ready, 1)
                for n in range(8):
                    w = n % 2
                    scale = (1.0, QSCALE)[w]
                    act.wait_ge(qk_done, n + 1)
                    if n >= 2:
                        act.wait_ge(qk_ready, n - 1)
                    bank = (2, 3, 0, 1, 4, 5, 6, 7)[n]
                    nc.scalar.activation(RL[:, n % 2, :], PS[:, bank, :], ACT.Relu, scale=scale)
                    nc.scalar.activation(EXQ[:, n % 2, :], PS[:, bank, :], ACT.Exp, scale=scale).then_inc(exq_done, 1)
                copy_y(0)

            def soft():
                act.wait_ge(v9_ones, 1)
                nc.scalar.activation(BQS[:, :], col("a1_bq"), ACT.Copy, scale=S ** -0.5).then_inc(act_step, 1)
                act.wait_ge(act_step, 1)
                for n in range(8):
                    c, w = 2 * (n // 4) + n % 2, n // 2 % 2
                    four = slice(c * 512, (c + 1) * 512)
                    act.wait_ge(proj_done, n + 1)
                    if n >= 2:
                        act.wait_ge(parts_done, n - 1)
                    nc.scalar.activation(QF[:, n % 2, :], PS[:, n % 4, :], ACT.Identity,
                                         bias=(BQS[:, :], col("a1_bk"))[w], scale=(S ** -0.5, 1.0)[w]).then_inc(qf_done, 1)
                    act.wait_ge(qf_done, n + 1)
                    nc.scalar.copy(PART[:, w, 0, four], QF[:, n % 2, :]).then_inc(part0_done, 1)
                for x in plan:
                    kind, k, i = x
                    if kind == "M":
                        act.wait_ge(m_turned, maxima_number[k, i] + 1)
                        before = rows_stored(k, i) - 16
                        if before:
                            act.wait_ge(m_rows[k % 4], before)
                        width = unit_columns(i)[1]
                        nc.scalar.copy(MT[0:width, k % 4, :],
                                       PS[0:width, 4 + ring_number[x] % NBB, 0:P // 2].bitcast(BF16)
                                       ).then_inc(m_copied, 1)
                    elif kind == "Z" and k in (4, 13):
                        std(0)
                        std(1)
                    elif kind == "B":
                        n = 4 * k + i
                        act.wait_ge(b_scores, n + 1)
                        if n == 0:
                            for b in range(B):
                                act.wait_ge(parts_stored[b], 6 * 16)
                        if k >= NPT // 4:
                            act.wait_ge(pv_done, k - NPT // 4 + 1)
                        w = columns(k)[0]
                        nc.scalar.activation(PT[:, n % NPT, 0:w], PS[:, 4 + ring_number[x] % NBB, 0:w], ACT.Exp
                                             ).then_inc(b_exp, 1)
                    elif kind == "V" and k % NS in (TB - 1, NS - 1):
                        G, half = k // NS, int(k % NS == NS - 1)
                        act.wait_ge(pv_done, k + 1)
                        if G >= 2:
                            act.wait_ge(z_turned, 2 * (G // 2))
                        nc.scalar.copy(ZT[:, G % 2, half * 512:(half + 1) * 512], PS[:, 7, :]).then_inc(z_copied, 1)

            for kind, ln, k in STAGES:
                norm_turned(ln, ln == 5)
                if kind in ("ffn0", "ffn1"):
                    moe(kind, k)
                elif kind == "lin":
                    linear()
                else:
                    soft()

        @block.vector
        def _(dve):
            steps = [0]

            def link(ins):
                steps[0] += 1
                ins.then_inc(dve_step, 1)
                dve.wait_ge(dve_step, steps[0])

            stds = 0

            def stats(src, t):
                return nc.vector.bn_stats(STATS[:, t, :], src[:, t, :])

            def variances(c, last_stats):
                nonlocal stds
                link(last_stats)
                for t in range(4 * c, 4 * c + 4):
                    last = nc.vector.bn_aggr(MV[:, t, :], STATS[:, t, :])
                last.then_inc(var_ready, 1)
                stds += 1
                return stds

            def inverse(c, number):
                dve.wait_ge(std_ready, number)
                r = RSTD[:, 4 * c:4 * c + 4]
                link(nc.vector.reciprocal(r, r))

            def norm(c, last_stats):
                inverse(c, variances(c, last_stats))

            def write_xn(c):
                for t in range(4 * c, 4 * c + 4):
                    nc.vector.tensor_scalar(XN[:, t, 0:P], X[:, t, :], MV[:, t, 0:1], RSTD[:, t:t + 1],
                                            ALU.subtract, ALU.mult).then_inc(xn_ready, 1)

            def normed(before_norm, ahead):
                first = T // 8 if before_norm == after_soft else 0
                if ahead:
                    number = variances(0, before_norm(0))
                    for c in range(T // 4):
                        this = number
                        if c + 1 < T // 4:
                            number = variances(c + 1, before_norm(c + 1))
                        inverse(c, this)
                        write_xn(c)
                    return
                for c in range(first, T // 4):
                    norm(c, before_norm(c))
                    write_xn(c)

            def constants():
                dve.wait_ge(early_loaded, 16)
                nc.vector.tensor_copy(TRI[:, :], col("tri")).then_inc(consts_made, 1)
                nc.vector.tensor_copy(IDB[:, :], col("ident")).then_inc(consts_made, 1)
                nc.vector.memset(ONES[:, :], 1.0).then_inc(consts_made, 1)
                ids = col("ids")
                nc.vector.tensor_copy(FILL[:, P:P + 1].bitcast(U32), ids[:, T:T + 1]).then_inc(fill_made, 1)
                nc.vector.tensor_copy(XN[:, :, P:P + 1].rearrange("p t o -> p (t o)").bitcast(U32), ids[:, 0:T]
                                      ).then_inc(ids_made, 1)

            def after_load(c):
                if c == 1:
                    constants()
                dve.wait_ge(x_loaded[c], 16)
                for t in range(4 * c, 4 * c + 4):
                    last = stats(X, t)
                return last

            def add_expert(k, t):
                if k < 2:
                    dve.wait_ge(gathered[t], 16 * (k + 1))
                else:
                    dve.wait_ge(y_loaded[t // 4], 16 * (k - 1))
                nc.vector.scalar_tensor_tensor(out=X[:, t, :], in0=YG[:, t, :], scalar=EFF[:, t:t + 1],
                                               in1=X[:, t, :], op0=ALU.mult, op1=ALU.add).then_inc(x_updated, 1)

            def after_moe(k, c):
                for t in range(4 * c, 4 * c + 4):
                    add_expert(k, t)
                    if t > 4 * c:
                        dve.wait_ge(x_updated, T * k + t)
                        stats(X, t - 1)
                dve.wait_ge(x_updated, T * k + t + 1)
                return stats(X, t)

            def after_linear(c):
                dve.wait_ge(lin_done, c + 1)
                xt = X[:, 4 * c:4 * c + 4, :]
                link(nc.vector.tensor_tensor(xt, xt, PS[:, 4 + c, :].rearrange("p (t d) -> p t d", t=4), ALU.add))
                for t in range(4 * c, 4 * c + 4):
                    last = stats(X, t)
                return last

            def input_added(c):
                four = slice(4 * c, 4 * c + 4)
                link(nc.vector.tensor_tensor(Z[:, four, :], Z[:, four, :], XN[:, four, 0:P], ALU.add))

            def stats_of(src, c):
                for t in range(4 * c, 4 * c + 4):
                    last = stats(src, t)
                return last

            def scaled(c):
                for t in range(4 * c, 4 * c + 4):
                    last = nc.vector.scalar_tensor_tensor(out=Z[:, t, :], in0=Z[:, t, :], scalar=MV[:, t, 0:1],
                                                          in1=col("a1_gamma"), op0=ALU.subtract, op1=ALU.mult)
                link(last)

            def shifted(c):
                for t in range(4 * c, 4 * c + 4):
                    last = nc.vector.scalar_tensor_tensor(out=Z[:, t, :], in0=Z[:, t, :], scalar=RSTD[:, t:t + 1],
                                                          in1=col("a1_beta"), op0=ALU.mult, op1=ALU.add)
                link(last)

            def attention_added(c):
                four = slice(4 * c, 4 * c + 4)
                link(nc.vector.tensor_tensor(X[:, four, :], X[:, four, :], Z[:, four, :], ALU.add))

            def after_soft(c):
                dve.wait_ge(z_scaled, GR)
                input_added(c)
                norm(c, stats_of(Z, c))
                scaled(c)
                shifted(c)
                attention_added(c)
                return stats_of(X, c)

            numbers = {}

            def first_batch(piece):
                if piece == 0:
                    dve.wait_ge(z_scaled, GR // 2)
                if piece < 4:
                    c = piece // 2
                    if piece % 2 == 0:
                        input_added(c)
                    else:
                        numbers[0, c] = variances(c, stats_of(Z, c))
                elif 5 <= piece < 13:
                    c, part = divmod(piece - 5, 4)
                    if part == 0:
                        inverse(c, numbers[0, c])
                        scaled(c)
                    elif part == 1:
                        shifted(c)
                    elif part == 2:
                        attention_added(c)
                    else:
                        numbers[1, c] = variances(c, stats_of(X, c))
                elif piece >= 14:
                    inverse(piece - 14, numbers[1, piece - 14])
                    write_xn(piece - 14)

            def over_e(a):
                return a.rearrange("p (t e) -> p e t", e=E)

            def moe(kind, k):
                dve.wait_ge(logits_done, k + 1)
                logits = PS[:, 2, 0:T * E].rearrange("p (t e) -> p t e", e=E)
                if kind == "ffn0":
                    br = col("f0_br").unsqueeze(1).to_broadcast([P, T, E])
                    link(nc.vector.tensor_tensor(LG[:, :, :], logits, br, ALU.add))
                else:
                    link(nc.vector.tensor_copy(LG[:, :, :], logits))
                link(nc.vector.tensor_reduce(LMAX[:, :], LG[:, :, :], AX.X, ALU.max))
                nc.vector.tensor_tensor(LG[:, :, :], LG[:, :, :], LMAX[:, :].unsqueeze(2).to_broadcast([P, T, E]),
                                        ALU.subtract).then_inc(lg_ready, 1)
                dve.wait_ge(lg_ready, k + 1)
                link(nc.vector.tensor_scalar(HIT[:, :], LG[:, :, :].rearrange("p t e -> p (t e)"), -(2.0 ** -25), None,
                                             ALU.is_ge))
                link(nc.vector.tensor_tensor_scan(NTH[:, :], col("r8"), HIT[:, :], 0.0, ALU.mult, ALU.add))
                link(nc.vector.scalar_tensor_tensor(out=MASK[:, :, :], in0=over_e(NTH[:, :]), scalar=1.0,
                                                    in1=over_e(HIT[:, :]), op0=ALU.is_equal, op1=ALU.mult))
                nc.vector.tensor_copy(MASKB[:, :], MASK[:, :, :].rearrange("p e t -> p (e t)")
                                      ).then_inc(mask_ready, 1)
                dve.wait_ge(ex_ready, k + 1)
                link(nc.vector.tensor_reduce(SUM[:, :], EX[:, :, :], AX.X, ALU.add))
                link(nc.vector.reciprocal(GATE[:, :], SUM[:, :]))
                by_t = PRD[:, :, :].rearrange("p e t -> p t e")
                if kind == "ffn0":
                    link(nc.vector.tensor_tensor(PRD[:, :, :], col("e256").rearrange("p (e t) -> p e t", e=E),
                                                 MASK[:, :, :], ALU.mult))
                    link(nc.vector.tensor_reduce(SLOT[:, :], by_t, AX.X, ALU.add))
                dve.wait_ge(counts_done, k + 1)
                behind, total = PS[:, 3, 0:P], PS[:, 3, P:2 * P]
                link(nc.vector.tensor_tensor_scan(INCL[:, :], col("r16"), total, 0.0, ALU.mult, ALU.add))
                link(nc.vector.tensor_tensor(POS[:, :], INCL[:, :], behind, ALU.add))
                pos = POS[:, :].rearrange("p (e t) -> p e t", e=E)
                if kind == "ffn0":
                    link(nc.vector.tensor_tensor(PRD[:, :, :], pos, MASK[:, :, :], ALU.mult))
                    link(nc.vector.tensor_reduce(PLACE[:, :], by_t, AX.X, ALU.add))
                    link(nc.vector.tensor_scalar(KEPT[:, :], PLACE[:, :], float(CAP), None, ALU.is_lt))
                    link(nc.vector.tensor_tensor(SLOT[:, :], SLOT[:, :], PLACE[:, :], ALU.add))
                    link(nc.vector.scalar_tensor_tensor(out=SCAT[:, :], in0=KEPT[:, :], scalar=-BIG, in1=SLOT[:, :],
                                                        op0=ALU.mult, op1=ALU.add))
                    link(nc.vector.tensor_scalar(SCAT[:, :], SCAT[:, :], BIG, None, ALU.add))
                    nc.vector.tensor_copy(SCATI[:, :], SCAT[:, :]).then_inc(index_ready, 1)
                    for t in range(T):
                        nc.vector.tensor_scalar(XG[:, t, :], XN[:, t, 0:P], GATE[:, t:t + 1], None,
                                                ALU.mult).then_inc(xg_ready, 1)
                    link(nc.vector.tensor_tensor(GATH[:, :], SLOT[:, :], KEPT[:, :], ALU.mult))
                    nc.vector.tensor_copy(GATHI[:, :], GATH[:, :]).then_inc(gath_ready, 1)
                    link(nc.vector.scalar_tensor_tensor(out=EFF[:, :], in0=GATE[:, :], scalar=0.5, in1=KEPT[:, :],
                                                        op0=ALU.mult, op1=ALU.mult))
                else:
                    ends = INCL[:, :].rearrange("p (e t) -> p e t", e=E)[:, :, T - 1:T].to_broadcast([P, E, T])
                    link(nc.vector.tensor_tensor(CMP[:, :, :], ends, col("jt").rearrange("p (e t) -> p e t", e=E),
                                                 ALU.is_gt))
                    link(nc.vector.tensor_reduce(TILES[:, :], CMP[:, :, :], AX.X, ALU.add))
                    link(nc.vector.tensor_tensor_scan(ENDS[:, :], col("r16", 1, E), TILES[:, :], 0.0,
                                                      ALU.mult, ALU.add))
                    link(nc.vector.tensor_tensor(BASE[:, :], ENDS[:, :], TILES[:, :], ALU.subtract))
                    link(nc.vector.tensor_scalar(BASE[:, :], BASE[:, :], float(P), -1.0, ALU.mult, ALU.add))
                    link(nc.vector.tensor_tensor(PRD[:, :, :], pos, BASE[:, :].unsqueeze(2).to_broadcast([P, E, T]),
                                                 ALU.add))
                    link(nc.vector.tensor_tensor(PRD[:, :, :], PRD[:, :, :], MASK[:, :, :], ALU.mult))
                    link(nc.vector.tensor_reduce(SLOT[:, :], by_t, AX.X, ALU.add))
                    nc.vector.tensor_copy(SCATI[:, :], SLOT[:, :]).then_inc(index_ready, 1)
                    link(nc.vector.tensor_tensor(CMP2[:, :, :], col("ti").rearrange("p (i e) -> p i e", e=E),
                                                 ENDS[:, :].unsqueeze(1).to_broadcast([P, NT, E]), ALU.is_ge))
                    link(nc.vector.tensor_reduce(OWNER[:, :], CMP2[:, :, :], AX.X, ALU.add))
                    nc.vector.tensor_scalar(OWNERI[:, :], OWNER[:, :], float(E - 1), None, ALU.min
                                            ).then_inc(owner_ready, 1)
                    link(nc.vector.tensor_scalar(EFF[:, :], GATE[:, :], 0.5, None, ALU.mult))

                base = before(k, E, NT)
                if kind == "ffn0":
                    dve.wait_ge(ffn0_loaded, 16)
                    for e in range(E):
                        dve.wait_ge(eo_done, base + e + 1)
                        nc.vector.tensor_tensor(
                            EO[:, 2 * e:2 * e + 2, :],
                            PS[:, 6 + e % 2, 0:2 * P].rearrange("p (s d) -> p s d", s=2),
                            col("f0_b2", e * P, P).unsqueeze(1).to_broadcast([P, 2, P]), ALU.add
                        ).then_inc(eo_copied, 1)
                else:
                    dve.wait_ge(w_loaded, 16 * (E + 1))
                    dve.wait_ge(owner_ready, k - 1)
                    owner = {}

                    def biased(i):
                        owner[i] = dve.value_load(OWNERI[0:1, i:i + 1], min_val=0, max_val=E - 1)
                        dve.wait_ge(hid_done, base + i + 1)
                        if i >= 2:
                            dve.wait_ge(hid_active, base + i - 1)
                        b1 = WT[:, bass.ds(owner[i] * WB + F1 + FB * P, FB)].unsqueeze(2).to_broadcast([P, FB, P])
                        nc.vector.tensor_tensor(HB[:, i % 2, :].rearrange("p (f n) -> p f n", f=FB),
                                                PS[:, 4 + i % 2, :].rearrange("p (f n) -> p f n", f=FB), b1,
                                                ALU.add).then_inc(hid_biased, 1)

                    biased(0)
                    for i in range(NT):
                        if i + 1 < NT:
                            biased(i + 1)
                        dve.wait_ge(eo_done, base + i + 1)
                        nc.vector.tensor_tensor(EO[:, i, :], PS[:, 6 + i % 2, 0:P], B2[:, bass.ds(owner[i] * P, P)],
                                                ALU.add).then_inc(eo_copied, 1)
            def linear():
                def feature_map(n):
                    w, c = n % 2, n // 2
                    dve.wait_ge(exq_done, n + 1)
                    nc.vector.scalar_tensor_tensor(out=(KT, QT)[w][:, c * 512:(c + 1) * 512], in0=EXQ[:, n % 2, :],
                                                   scalar=1.0, in1=RL[:, n % 2, :], op0=ALU.min, op1=ALU.add
                                                   ).then_inc(qk_ready, 1)

                for n in range(4):
                    feature_map(n)
                dve.wait_ge(g_ready, 4)

                def products(n):
                    b = n // DH
                    dve.wait_ge(v_done, n + 1)
                    if n >= 2:
                        dve.wait_ge(state_done, n - 1)
                    dve.wait_ge(qk_ready, 4 * (b + 1))
                    ps = PS[:, 2 * (n % 2):2 * (n % 2) + 2, :].rearrange("p c n -> p (c n)")
                    nc.vector.tensor_tensor(KV[:, n % 2, :], KT[:, b * S:(b + 1) * S], ps, ALU.mult
                                            ).then_inc(kv_done, 1)

                products(0)
                for n in range(B * DH):
                    b = n // DH
                    if n < 4:
                        feature_map(4 + n)
                    if n + 1 < B * DH:
                        products(n + 1)
                    dve.wait_ge(kv_done, n + 1)
                    if n >= 2:
                        dve.wait_ge(qs_done, n - 1)
                    nc.vector.tensor_tensor_scan(ST[:, n % 2, :], GT[:, b * S:(b + 1) * S], KV[:, n % 2, :], 0.0,
                                                 ALU.mult, ALU.add).then_inc(state_done, 1)

            def soft():
                for n in range(8):
                    c, w = 2 * (n // 4) + n % 2, n // 2 % 2
                    four = slice(c * 512, (c + 1) * 512)
                    dve.wait_ge(part0_done, n + 1)
                    link(nc.vector.tensor_tensor(RF[:, n % 2, :], QF[:, n % 2, :], PART[:, w, 0, four], ALU.subtract))
                    link(nc.vector.tensor_copy(PART[:, w, 1, four], RF[:, n % 2, :]))
                    nc.vector.tensor_tensor(PART[:, w, 2, four], RF[:, n % 2, :], PART[:, w, 1, four], ALU.subtract
                                            ).then_inc(parts_done, 1)
                dve.wait_ge(v9_ones, 1)
                for c in range(4):
                    dve.wait_ge(vproj_done, c + 1)
                    nc.vector.tensor_tensor(
                        V9[:, 4 * c:4 * c + 4, :, 0:DH],
                        PS[:, 4 + c, :].rearrange("p (t h j) -> p t h j", t=4, h=H),
                        col("a1_bv").rearrange("p (h j) -> p h j", h=H).unsqueeze(1).to_broadcast([P, 4, H, DH]),
                        ALU.add).then_inc(v9_ready, 1)
                z_steps = 0
                for x in plan:
                    kind, k, i = x
                    if kind == "A":
                        slot = 2 * (turn_number[x] % 2)
                        dve.wait_ge(a_scores, score_number[x] + 1)
                        if k >= 4 and i == 0:
                            dve.wait_ge(m_split, last_unit(k - 4) + 1)
                        nc.vector.tensor_reduce(NM[:, k % 4, i:i + 1],
                                                PS[:, slot:slot + 2, :].rearrange("p b n -> p (b n)"),
                                                AX.X, ALU.max, negate=True).then_inc(a_max, 1)
                    elif kind == "Z":
                        first_batch(k)
                    elif kind == "T":
                        slot = 2 * (turn_number[x] % 2)
                        dve.wait_ge(z_turned, 2 * k + i + 1)
                        tile0 = 4 * k
                        zz = Z[:, tile0:tile0 + 4, 64 * i:64 * i + 64].rearrange("p g (c j) -> p c g j", j=DH)
                        ps = PS[:, slot:slot + 2, :].rearrange("p b (c g w) -> p (b c) g w", g=4, w=32)
                        if 2 * k + i >= 1:
                            dve.wait_ge(z_scaled, 2 * k + i)
                        link(nc.vector.reciprocal(RD[:, :, :], ps[:, :, :, 8]))
                        nc.vector.tensor_tensor(zz, ps[:, :, :, 0:DH],
                                                RD[:, :, :].unsqueeze(3).to_broadcast([P, 8, 4, DH]),
                                                ALU.mult).then_inc(z_scaled, 1)

            before_norm = after_load
            for kind, ln, k in STAGES:
                normed(before_norm, ln in (0, 2, 4))
                if kind in ("ffn0", "ffn1"):
                    moe(kind, k)

                    def before_norm(c, k=k):
                        return after_moe(k, c)
                elif kind == "lin":
                    linear()
                    before_norm = after_linear
                else:
                    soft()
                    before_norm = after_soft
            for t in range(T):
                add_expert(3, t)

        @block.gpsimd
        def _(pool):
            def moe(kind, k):
                pool.wait_ge(index_ready, k + 1)
                src = XG if kind == "ffn0" else XN
                slots = tiles_of(kind) * P
                pool.wait_ge(slots_filled[k if k > 1 else 0], 16)
                for t in range(T):
                    if kind == "ffn0":
                        pool.wait_ge(xg_ready, T * k + t + 1)
                    pool.indirect_dma_start(sx[k], bass.IndirectOffsetOnAxis(ap=SCATI[:, t:t + 1], axis=0),
                                            src[:, t, :], None, bounds_check=slots - 1, oob_is_err=False
                                            ).then_inc(scattered, 16)
                if kind == "ffn1":
                    for i in range(NT):
                        pool.wait_ge(eo_copied, before(k, E, NT) + i + 1)
                        pool.indirect_dma_start(ty, bass.IndirectOffsetOnAxis(ap=XS[:, i, P:P + 1].bitcast(U32), axis=0),
                                                EO[:, i, :], None, bounds_check=N - 1, oob_is_err=False
                                                ).then_inc(y_scattered, 16)
                    return
                pool.wait_ge(gath_ready, k + 1)
                pool.wait_ge(eo_stored, 16 * before(k + 1, E, NT))
                for t in range(T):
                    pool.indirect_dma_start(YG[:, t, :], None, sy[0:slots, :],
                                            bass.IndirectOffsetOnAxis(ap=GATHI[:, t:t + 1], axis=0),
                                            bounds_check=slots - 1, oob_is_err=False).then_inc(gathered[t], 16)

            def linear():
                for n in range(B * DH):
                    b = n // DH
                    pool.wait_ge(qk_ready, 4 * (b + 1))
                    pool.wait_ge(state_done, n + 1)
                    if n >= 8:
                        pool.wait_ge(sums_done, n // 4 - 1)
                    nc.gpsimd.tensor_tensor(QS[:, n % 8, :], QT[:, b * S:(b + 1) * S], ST[:, n % 2, :], ALU.mult
                                            ).then_inc(qs_done, 1)

            def soft():
                pool.wait_ge(x_updated, T * 3)
                nc.gpsimd.memset(V9[:, :, :, DH:DH + 1], 1.0).then_inc(v9_ones, 1)
                nc.gpsimd.memset(ONE8[:, :], 0.0).then_inc(pool_step, 1)
                pool.wait_ge(pool_step, 1)
                nc.gpsimd.memset(ONE8[:, DH:DH + 1], 1.0).then_inc(one8_made, 1)
                step = 1

                def then(ins):
                    nonlocal step
                    step += 1
                    ins.then_inc(pool_step, 1)
                    pool.wait_ge(pool_step, step)

                for x in plan:
                    kind, k, i = x
                    if kind == "S":
                        pool.wait_ge(a_max, last_scores[k, i] + 1)
                        if k >= 4:
                            pool.wait_ge(m_turned, last_unit(k - 4) + 1)
                        tiles, (at, width) = tiles_of_unit(i), unit_columns(i)
                        n = len(tiles)
                        nm, rest = NM[:, k % 4, tiles[0]:tiles[-1] + 1], NMR[:, k % 4, tiles[0]:tiles[-1] + 1]
                        m0, m1, m2 = (M3[:, k % 4, at + r * n:at + (r + 1) * n] for r in range(3))
                        then(nc.gpsimd.tensor_copy(m0, nm))
                        then(nc.gpsimd.tensor_tensor(rest, nm, m0, ALU.subtract))
                        then(nc.gpsimd.tensor_copy(m1, rest))
                        nc.gpsimd.tensor_tensor(m2, rest, m1, ALU.subtract).then_inc(m_split, 1)
                    if kind == "B":
                        _, diag = columns(k)
                        if diag is None:
                            continue
                        n = 4 * k + i
                        pool.wait_ge(b_exp, n + 1)
                        nc.gpsimd.affine_select(out=MD[:, n % NPT, :], in_=PT[:, n % NPT, diag:diag + P],
                                                compare_op=ALU.is_ge, fill=0.0, base=0, pattern=[[-1, P]],
                                                channel_multiplier=1).then_inc(b_masked, 1)

            nc.gpsimd.memset(EPS1[:, :], EPS).then_inc(eps_made, 1)
            nc.gpsimd.memset(FILL[:, 0:P], 0.0).then_inc(fill_made, 1)
            pool.wait_ge(ids_made, 1)
            for kind, ln, k in STAGES:
                if kind in ("ffn0", "ffn1"):
                    moe(kind, k)
                elif kind == "lin":
                    linear()
                else:
                    soft()


def kernel(**inputs):
    import numpy as np
    import concourse.bacc as _bacc
    from concourse.bass_utils import run_bass_kernel_spmd as _run

    g = {k: np.asarray(v) for k, v in inputs.items()}
    x = np.ascontiguousarray(g["L0_attn_x"].reshape(N, P))
    f = np.float32

    def rows(v):
        return np.broadcast_to(v.reshape(1, -1), (P, v.size))

    k, q = np.arange(P)[:, None], np.arange(P)[None, :]
    w1, w2 = g["L1_ffn_W1"], g["L1_ffn_W2"]
    part = {
        "ident": (k == q).astype(f), "tri": -(k > q).astype(f),
        "r8": rows((np.arange(P) % E != 0).astype(f)), "r16": rows((np.arange(P) % T != 0).astype(f)),
        "e256": rows((np.arange(P) // T * CAP).astype(f)), "jt": rows((np.arange(P) % T * P).astype(f)),
        "ids": np.concatenate([P * q[:, :T] + k, np.full((P, 1), BIG)], axis=1).astype(f),
        "ti": rows((np.arange(NT * E) // E).astype(f)),
        "f0_wr": g["L0_ffn_Wr"], "f0_br": rows(g["L0_ffn_br"]), "f0_b1": g["L0_ffn_b1"].T,
        "f1_wr": g["L1_ffn_Wr"],
        "a0_bg": np.repeat(g["L0_attn_bg"], DH)[:, None],
        "a1_bq": g["L1_attn_bq"][:, None], "a1_bk": g["L1_attn_bk"][:, None],
        "f0_w1": g["L0_ffn_W1"].transpose(1, 0, 2).reshape(P, E * P),
        "f0_w2": g["L0_ffn_W2"].transpose(1, 0, 2).reshape(P, E * P),
        "f0_b2": rows(g["L0_ffn_b2"]),
        "a0_wq": g["L0_attn_Wq"].T, "a0_wk": g["L0_attn_Wk"].T,
        "a0_wg": np.repeat(g["L0_attn_Wg"].T, DH, axis=1),
        "a0_wv": np.repeat(g["L0_attn_Wv"].T.reshape(P, H, DH).transpose(0, 2, 1)[..., None], DH, axis=3).reshape(P, DH * P),
        "a0_wo": g["L0_attn_Wo"].T.reshape(H, 2, 4, P).transpose(2, 1, 0, 3).reshape(P, P),
        "hsum": (np.arange(32)[None, None, :] == 16 * np.arange(2)[None, :, None] + np.arange(P)[:, None, None] // DH
                 ).astype(f).reshape(P, 64),
        "a1_wq": g["L1_attn_Wq"].T, "a1_wk": g["L1_attn_Wk"].T, "a1_wv": g["L1_attn_Wv"].T,
        "a1_bv": rows(g["L1_attn_bv"]), "a1_gamma": rows(g["L1_attn_gamma"]), "a1_beta": rows(g["L1_attn_beta"]),
    }
    for name, (_, width) in COLS.items():
        assert part[name].shape == (P, width), (name, part[name].shape)
    params = np.ascontiguousarray(np.concatenate([part[name] for name in COLS], axis=1))
    pack = np.ascontiguousarray(np.concatenate([
        w1, w2.reshape(E, FB, P, P).transpose(0, 2, 1, 3).reshape(E, P, FB * P),
        g["L1_ffn_b1"].reshape(E, FB, P).transpose(0, 2, 1)], axis=2))
    b2 = np.ascontiguousarray(rows(g["L1_ffn_b2"]))

    nc = _bacc.Bacc("TRN2", target_bir_lowering=False, num_devices=1)
    arrays = {"x_dram": x, "params_dram": params, "pack_dram": pack, "b2_dram": b2}
    args = [nc.dram_tensor(n, a.shape, F32, kind="ExternalInput").ap() for n, a in arrays.items()]
    args.append(nc.dram_tensor("out_dram", (N, P), F32, kind="ExternalOutput").ap())
    macaron_kernel(nc, *args)
    r = _run(nc, [arrays], core_ids=[0])
    return r.results[0]["out_dram"].reshape(B, S, P)
```
